# Optimizing a Trainium2 kernel written in Bass

```python
import numpy as np
import jax
import jax.numpy as jnp

def _softmax(x, axis=-1):
    return jax.nn.softmax(x, axis=axis)

def _gelu(x):
    return jax.nn.gelu(x, approximate=True)

def _silu(x):
    return jax.nn.silu(x)

def _sigmoid(x):
    return jax.nn.sigmoid(x)

def _layernorm(x, axis=-1, eps=1e-05):
    m = jnp.mean(x, axis=axis, keepdims=True)
    v = jnp.var(x, axis=axis, keepdims=True)
    return (x - m) / jnp.sqrt(v + eps)

def _scatter_add(tgt, idx, src, axis=0):
    return tgt.at[idx].add(src)

def _segment_sum(src, seg, n):
    return jax.ops.segment_sum(src, seg, n)
kernel_name = 'mk_gnn_preln_d4_gnn_r32_5e914e'

def setup_inputs(seed: int=0):
    np.random.seed(seed)
    _w = jnp.asarray

    def _rec_inputs():
        import jax
        import jax.numpy as jnp
        _gk = jax.random.key(seed)
        x = -0.0003713 + 1 * jax.random.normal(jax.random.fold_in(_gk, 1), (3125, 128), jnp.float32)
        _s = jax.random.randint(jax.random.fold_in(_gk, 2), (25000,), 0, 3125, jnp.int32)
        _d = jax.random.randint(jax.random.fold_in(_gk, 3), (25000,), 0, 3125, jnp.int32)
        _loop = jnp.arange(3125, dtype=jnp.int32)
        src = jnp.concatenate([_s, _d, _loop])
        dst = jnp.concatenate([_d, _s, _loop])
        _o = jnp.argsort(dst, stable=True)
        src = src[_o]
        dst = dst[_o]
        edge_attr_128 = 9.41057e-06 + 1 * jax.random.normal(jax.random.fold_in(_gk, 11), (53125, 128), jnp.float32)
        return (x, src, dst, edge_attr_128)
    x, src, dst, edge_attr_128 = _rec_inputs()

    def _L0_gnn_setup():
        import jax, jax.numpy as jnp
        import numpy as np
        N_NODES = 3125
        N_EDGES = 50000
        D = 128
        BN_EPS = 1e-05
        key = jax.random.key(seed)
        ks = jax.random.split(key, 6)
        x = jax.random.normal(ks[0], (N_NODES, D), dtype=jnp.float32)
        edge_index = jax.random.randint(ks[1], (2, N_EDGES), 0, N_NODES, dtype=jnp.int64)
        s = 1.0 / np.sqrt(D)
        W1 = jax.random.uniform(ks[2], (D, D), jnp.float32, -s, s)
        W2 = jax.random.uniform(ks[3], (D, D), jnp.float32, -s, s)
        b1 = jnp.zeros((D,), jnp.float32)
        b2 = jnp.zeros((D,), jnp.float32)
        gamma = jnp.ones((D,), jnp.float32)
        beta = jnp.zeros((D,), jnp.float32)
        return {'x': x, 'edge_index': edge_index, 'W1': W1, 'b1': b1, 'W2': W2, 'b2': b2, 'gamma': gamma, 'beta': beta}
    _L0_gnn_all = _L0_gnn_setup()
    _L0_gnn_in = {k: v for k, v in _L0_gnn_all.items() if k in ('W1', 'b1', 'W2', 'b2', 'gamma', 'beta')}
    del _L0_gnn_all

    def _L1_gnn_setup():
        import math
        import jax, jax.numpy as jnp
        import numpy as np
        N = 50000
        C = 128
        H = 8
        D = C // H
        E = 25000

        def _layernorm(x, g, b, eps=1e-05):
            mu = jnp.mean(x, axis=-1, keepdims=True)
            var = jnp.var(x, axis=-1, keepdims=True)
            return (x - mu) * jax.lax.rsqrt(var + eps) * g + b
        key = jax.random.key(seed)
        ks = jax.random.split(key, 12)
        s = 1.0 / math.sqrt(C)
        s4 = 1.0 / math.sqrt(4 * C)
        return {'x': jax.random.normal(ks[0], (N, C), dtype=jnp.float32), 'edge_index': jax.random.randint(ks[1], (2, E), 0, N, dtype=jnp.int64), 'Wq': jax.random.normal(ks[2], (C, C), dtype=jnp.float32) * s, 'Wk': jax.random.normal(ks[3], (C, C), dtype=jnp.float32) * s, 'Wv': jax.random.normal(ks[4], (C, C), dtype=jnp.float32) * s, 'Wo': jax.random.normal(ks[5], (C, C), dtype=jnp.float32) * s, 'bo': jnp.zeros((C,), dtype=jnp.float32), 'Wf1': jax.random.normal(ks[6], (C, 4 * C), dtype=jnp.float32) * s, 'bf1': jnp.zeros((4 * C,), dtype=jnp.float32), 'Wf2': jax.random.normal(ks[7], (4 * C, C), dtype=jnp.float32) * s4, 'bf2': jnp.zeros((C,), dtype=jnp.float32), 'g1': jnp.ones((C,), dtype=jnp.float32), 'b1': jnp.zeros((C,), dtype=jnp.float32), 'g2': jnp.ones((C,), dtype=jnp.float32), 'b2': jnp.zeros((C,), dtype=jnp.float32)}
    _L1_gnn_all = _L1_gnn_setup()
    _L1_gnn_in = {k: v for k, v in _L1_gnn_all.items() if k in ('Wq', 'Wk', 'Wv', 'Wo', 'bo', 'Wf1', 'bf1', 'Wf2', 'bf2', 'g1', 'b1', 'g2', 'b2')}
    del _L1_gnn_all

    def _L2_gnn_setup():
        import jax, jax.numpy as jnp
        import numpy as np
        N_NODES = 3125

        def _gcn_conv(x, edge_index, W, b):
            n = x.shape[0]
            src, dst = (edge_index[0], edge_index[1])
            loop = jnp.arange(n, dtype=edge_index.dtype)
            src = jnp.concatenate([src, loop])
            dst = jnp.concatenate([dst, loop])
            h = x @ W
            deg = jax.ops.segment_sum(jnp.ones(src.shape, x.dtype), dst, num_segments=n)
            dinv = jax.lax.rsqrt(jnp.maximum(deg, jnp.asarray(1.0, x.dtype)))
            norm = dinv[src] * dinv[dst]
            msg = h[src] * norm[:, None]
            agg = jax.ops.segment_sum(msg, dst, num_segments=n)
            return agg + b
        key = jax.random.key(seed)
        k1, k2, k3, k4 = jax.random.split(key, 4)
        in_dim = out_dim = 128
        n_edges = 50000
        x = jax.random.normal(k1, (N_NODES, in_dim), dtype=jnp.float32)
        edge_index = jax.random.randint(k2, (2, n_edges), 0, N_NODES, dtype=jnp.int64)
        s = 1.0 / np.sqrt(in_dim)
        W_gcn = jax.random.normal(k3, (in_dim, out_dim), dtype=jnp.float32) * s
        b_gcn = jnp.zeros((out_dim,), dtype=jnp.float32)
        W_lin = jax.random.normal(k4, (in_dim, out_dim), dtype=jnp.float32) * s
        b_lin = jnp.zeros((out_dim,), dtype=jnp.float32)
        return {'x': x, 'edge_index': edge_index, 'W_gcn': W_gcn, 'b_gcn': b_gcn, 'W_lin': W_lin, 'b_lin': b_lin}
    _L2_gnn_all = _L2_gnn_setup()
    _L2_gnn_in = {k: v for k, v in _L2_gnn_all.items() if k in ('W_gcn', 'b_gcn', 'W_lin', 'b_lin')}
    del _L2_gnn_all

    def _L3_gnn_setup():
        import jax, jax.numpy as jnp
        import numpy as np
        N, E, D = (3125, 50000, 128)
        BN_EPS = 1e-05
        key = jax.random.key(seed)
        ks = jax.random.split(key, 8)
        x = jax.random.normal(ks[0], (N, D), dtype=jnp.float32)
        edge_index = jax.random.randint(ks[1], (2, E), 0, N, dtype=jnp.int64)
        edge_attr = jax.random.normal(ks[2], (E, D), dtype=jnp.float32)
        W1 = jax.random.normal(ks[3], (D, D), dtype=jnp.float32) / np.sqrt(D)
        b1 = jnp.zeros((D,), dtype=jnp.float32)
        gamma = jnp.ones((D,), dtype=jnp.float32)
        beta = jnp.zeros((D,), dtype=jnp.float32)
        W2 = jax.random.normal(ks[4], (D, D), dtype=jnp.float32) / np.sqrt(D)
        b2 = jnp.zeros((D,), dtype=jnp.float32)
        return {'x': x, 'edge_index': edge_index, 'edge_attr': edge_attr, 'W1': W1, 'b1': b1, 'gamma': gamma, 'beta': beta, 'W2': W2, 'b2': b2}
    _L3_gnn_all = _L3_gnn_setup()
    _L3_gnn_in = {k: v for k, v in _L3_gnn_all.items() if k in ('W1', 'b1', 'gamma', 'beta', 'W2', 'b2')}
    del _L3_gnn_all
    return {'x': x, 'src': src, 'dst': dst, 'edge_attr_128': edge_attr_128, 'L0_gnn_W1': _L0_gnn_in['W1'], 'L0_gnn_b1': _L0_gnn_in['b1'], 'L0_gnn_W2': _L0_gnn_in['W2'], 'L0_gnn_b2': _L0_gnn_in['b2'], 'L0_gnn_gamma': _L0_gnn_in['gamma'], 'L0_gnn_beta': _L0_gnn_in['beta'], 'L1_gnn_Wq': _L1_gnn_in['Wq'], 'L1_gnn_Wk': _L1_gnn_in['Wk'], 'L1_gnn_Wv': _L1_gnn_in['Wv'], 'L1_gnn_Wo': _L1_gnn_in['Wo'], 'L1_gnn_bo': _L1_gnn_in['bo'], 'L1_gnn_Wf1': _L1_gnn_in['Wf1'], 'L1_gnn_bf1': _L1_gnn_in['bf1'], 'L1_gnn_Wf2': _L1_gnn_in['Wf2'], 'L1_gnn_bf2': _L1_gnn_in['bf2'], 'L1_gnn_g1': _L1_gnn_in['g1'], 'L1_gnn_b1': _L1_gnn_in['b1'], 'L1_gnn_g2': _L1_gnn_in['g2'], 'L1_gnn_b2': _L1_gnn_in['b2'], 'L2_gnn_W_gcn': _L2_gnn_in['W_gcn'], 'L2_gnn_b_gcn': _L2_gnn_in['b_gcn'], 'L2_gnn_W_lin': _L2_gnn_in['W_lin'], 'L2_gnn_b_lin': _L2_gnn_in['b_lin'], 'L3_gnn_W1': _L3_gnn_in['W1'], 'L3_gnn_b1': _L3_gnn_in['b1'], 'L3_gnn_gamma': _L3_gnn_in['gamma'], 'L3_gnn_beta': _L3_gnn_in['beta'], 'L3_gnn_W2': _L3_gnn_in['W2'], 'L3_gnn_b2': _L3_gnn_in['b2']}

def reference(x, src, dst, edge_attr_128, L0_gnn_W1, L0_gnn_b1, L0_gnn_W2, L0_gnn_b2, L0_gnn_gamma, L0_gnn_beta, L1_gnn_Wq, L1_gnn_Wk, L1_gnn_Wv, L1_gnn_Wo, L1_gnn_bo, L1_gnn_Wf1, L1_gnn_bf1, L1_gnn_Wf2, L1_gnn_bf2, L1_gnn_g1, L1_gnn_b1, L1_gnn_g2, L1_gnn_b2, L2_gnn_W_gcn, L2_gnn_b_gcn, L2_gnn_W_lin, L2_gnn_b_lin, L3_gnn_W1, L3_gnn_b1, L3_gnn_gamma, L3_gnn_beta, L3_gnn_W2, L3_gnn_b2):
    import jax
    import jax.numpy as jnp

    def _L0_gnn_ref(x, edge_index, W1, b1, W2, b2, gamma, beta):
        import jax, jax.numpy as jnp
        import numpy as np
        N_NODES = 3125
        N_EDGES = 50000
        D = 128
        BN_EPS = 1e-05
        src = edge_index[0]
        dst = edge_index[1]
        agg = jax.ops.segment_sum(x[src], dst, num_segments=x.shape[0])
        h = agg + x
        h = jax.nn.relu(h @ W1 + b1) @ W2 + b2
        mean = jnp.mean(h, axis=0)
        var = jnp.mean(jnp.square(h - mean), axis=0)
        h = (h - mean) * jax.lax.rsqrt(var + BN_EPS) * gamma + beta
        return h + x

    def _L1_gnn_ref(x, edge_index, Wq, Wk, Wv, Wo, bo, Wf1, bf1, Wf2, bf2, g1, b1, g2, b2):
        import math
        import jax, jax.numpy as jnp
        import numpy as np
        N = 50000
        C = 128
        H = 8
        D = C // H
        E = 25000

        def _layernorm(x, g, b, eps=1e-05):
            mu = jnp.mean(x, axis=-1, keepdims=True)
            var = jnp.var(x, axis=-1, keepdims=True)
            return (x - mu) * jax.lax.rsqrt(var + eps) * g + b
        n = x.shape[0]
        loops = jnp.arange(n, dtype=edge_index.dtype)
        row = jnp.concatenate([edge_index[0], loops])
        col = jnp.concatenate([edge_index[1], loops])
        q = (x @ Wq).reshape(n, H, D)
        k = (x @ Wk).reshape(n, H, D)
        v = (x @ Wv).reshape(n, H, D)
        scores = jnp.einsum('ehd,ehd->eh', q[row], k[col]) / math.sqrt(D)
        smax = jax.ops.segment_max(scores, col, num_segments=n)
        exp = jnp.exp(scores - smax[col])
        ssum = jax.ops.segment_sum(exp, col, num_segments=n)
        alpha = exp / (ssum[col] + 1e-08)
        out = jax.ops.segment_sum(v[row] * alpha[..., None], col, num_segments=n)
        attn = out.reshape(n, C) @ Wo + bo
        residual = x
        x1 = _layernorm(residual + attn, g1, b1)
        ffn = jax.nn.gelu(x1 @ Wf1 + bf1, approximate=False) @ Wf2 + bf2
        return _layernorm(x1 + ffn, g2, b2)

    def _L2_gnn_ref(x, edge_index, W_gcn, b_gcn, W_lin, b_lin):
        import jax, jax.numpy as jnp
        import numpy as np
        N_NODES = 3125

        def _gcn_conv(x, edge_index, W, b):
            n = x.shape[0]
            src, dst = (edge_index[0], edge_index[1])
            loop = jnp.arange(n, dtype=edge_index.dtype)
            src = jnp.concatenate([src, loop])
            dst = jnp.concatenate([dst, loop])
            h = x @ W
            deg = jax.ops.segment_sum(jnp.ones(src.shape, x.dtype), dst, num_segments=n)
            dinv = jax.lax.rsqrt(jnp.maximum(deg, jnp.asarray(1.0, x.dtype)))
            norm = dinv[src] * dinv[dst]
            msg = h[src] * norm[:, None]
            agg = jax.ops.segment_sum(msg, dst, num_segments=n)
            return agg + b
        conv = _gcn_conv(x, edge_index, W_gcn, b_gcn)
        lin = x @ W_lin + b_lin
        return jax.nn.relu(conv + lin)

    def _L3_gnn_ref(x, edge_index, edge_attr, W1, b1, gamma, beta, W2, b2):
        import jax, jax.numpy as jnp
        import numpy as np
        N, E, D = (3125, 50000, 128)
        BN_EPS = 1e-05
        src = edge_index[0]
        dst = edge_index[1]
        msg = jax.nn.relu(x[src] + edge_attr)
        aggr = jax.ops.segment_sum(msg, dst, num_segments=x.shape[0])
        h = x + aggr
        h = jax.nn.relu(h @ W1 + b1)
        mean = jnp.mean(h, axis=0)
        var = jnp.var(h, axis=0)
        h = (h - mean) * jax.lax.rsqrt(var + BN_EPS) * gamma + beta
        return h @ W2 + b2
    edge_index = jnp.stack([src, dst])
    h = jnp.maximum(_layernorm(x, axis=-1), 0.0)
    x = x + _L0_gnn_ref(h, edge_index, L0_gnn_W1, L0_gnn_b1, L0_gnn_W2, L0_gnn_b2, L0_gnn_gamma, L0_gnn_beta)
    h = jnp.maximum(_layernorm(x, axis=-1), 0.0)
    x = x + _L1_gnn_ref(h, edge_index, L1_gnn_Wq, L1_gnn_Wk, L1_gnn_Wv, L1_gnn_Wo, L1_gnn_bo, L1_gnn_Wf1, L1_gnn_bf1, L1_gnn_Wf2, L1_gnn_bf2, L1_gnn_g1, L1_gnn_b1, L1_gnn_g2, L1_gnn_b2)
    h = jnp.maximum(_layernorm(x, axis=-1), 0.0)
    x = x + _L2_gnn_ref(h, edge_index, L2_gnn_W_gcn, L2_gnn_b_gcn, L2_gnn_W_lin, L2_gnn_b_lin)
    h = jnp.maximum(_layernorm(x, axis=-1), 0.0)
    x = x + _L3_gnn_ref(h, edge_index, edge_attr_128, L3_gnn_W1, L3_gnn_b1, L3_gnn_gamma, L3_gnn_beta, L3_gnn_W2, L3_gnn_b2)
    return x

_drawn_inputs = setup_inputs


def setup_inputs(seed=0):
    import zlib

    import numpy as np

    out = dict(_drawn_inputs(seed))
    spreads = {'L0_gnn_b1': (0.0, 0.488),
     'L0_gnn_b2': (0.0, 2.0),
     'L0_gnn_gamma': (1.0, 0.2),
     'L0_gnn_beta': (0.0, 0.1),
     'L1_gnn_bo': (0.0, 0.1),
     'L1_gnn_bf1': (0.0, 0.337),
     'L1_gnn_bf2': (0.0, 0.1),
     'L1_gnn_g1': (1.0, 0.2),
     'L1_gnn_b1': (0.0, 0.1),
     'L1_gnn_g2': (1.0, 0.2),
     'L1_gnn_b2': (0.0, 0.1),
     'L2_gnn_b_gcn': (0.0, 0.29),
     'L2_gnn_b_lin': (0.0, 0.344),
     'L3_gnn_b1': (0.0, 0.533),
     'L3_gnn_gamma': (1.0, 0.2),
     'L3_gnn_beta': (0.0, 0.1),
     'L3_gnn_b2': (0.0, 0.1)}
    factors = {}
    for name, (base, spread) in spreads.items():
        noise = np.random.default_rng([zlib.crc32(name.encode()), seed]).standard_normal(out[name].shape)
        drawn = base * np.exp(spread * noise) if base else spread * noise
        out[name] = jnp.asarray(drawn.astype(out[name].dtype))
    for name, factor in factors.items():
        out[name] = (out[name] * factor).astype(out[name].dtype)
    return out
```

```python
from contextlib import ExitStack

import concourse.bass as bass
from concourse import mybir

F32 = mybir.dt.float32
I32 = mybir.dt.int32
ALU = mybir.AluOpType
ACT = mybir.ActivationFunctionType
AX = mybir.AxisListType

P = 128
N_NODES = 3125
N_EDGES = 53125
D = 128
HEADS = 8
HD = D // HEADS
NW = -(-N_NODES // P)
NPAD = NW * P
NT = -(-N_EDGES // P)
LAST_TILE = NT - 1
LAST_ROW = N_EDGES - P
OVERLAP = LAST_TILE * P - LAST_ROW
NS = NT + NW - 1
U = 4
RING = 5
UNROLL = 2 * RING
NG = NS // U
BODIES = NG // UNROLL
assert BODIES * UNROLL * U == NS
NCH = (NT - 1) // P + 1
LASTCH = (NT - 1) - (NCH - 1) * P
CHUNKS = [P] * (NCH - 1) + [LASTCH, 1]
HID = 4 * D
HC = HID // P
LN_EPS = 1e-5
BN_EPS = 1e-5
NONE = -1e30
BANK = 512
BANKS = [(b * BANK, min(BANK, NPAD - b * BANK)) for b in range(-(-NPAD // BANK))]
NB = len(BANKS)
DEN = NPAD
B7 = 7 * BANK
MC = HEADS + 2
SQRT_HD = HD ** 0.5
LAYERS_LN = 53


def gnn_kernel(nc, t, out):
    ctx = ExitStack()
    with ctx:
        def sb(name, shape, dt=F32):
            return ctx.enter_context(nc.sbuf_tensor(name, shape, dt))

        sems = {}

        def sem(name):
            if name not in sems:
                sems[name] = ctx.enter_context(nc.semaphore(name))
            return sems[name]

        h0_rows = nc.dram_tensor("h0_rows", [NPAD, D], F32, kind="Internal").ap()
        qv_rows = nc.dram_tensor("qv_rows", [NPAD, 2 * D], F32, kind="Internal").ap()
        g2_rows = nc.dram_tensor("g2_rows", [NPAD, D], F32, kind="Internal").ap()
        h3_rows = nc.dram_tensor("h3_rows", [NPAD, D], F32, kind="Internal").ap()
        v_park = nc.dram_tensor("v_park", [NG * P, U * D], F32, kind="Internal").ap()

        x = sb("x", [P, NW, D])
        h = sb("h", [P, NW, D])
        hT = sb("hT", [P, NPAD])
        scratch = sb("scratch", [P, 3 * NPAD])
        bufA, bufB, bufC = (scratch[:, i * NPAD:(i + 1) * NPAD] for i in range(3))
        qkv = sb("qkv", [P, NW * 3 * D])
        qkv3 = qkv[:, :].rearrange("p (w c) -> p w c", w=NW)
        score = sb("score", [P, NG * U * HEADS])
        gath = sb("gath", [P, RING * U, 2 * D])
        gath_lo = [gath[:, j * U:(j + 1) * U, 0:D] for j in range(RING)]
        ring = [gath[:, j * U:(j + 1) * U, D:2 * D] for j in range(RING)]
        onehot = sb("onehot", [P, RING, U * P])
        onehotT = hT[:, 0:2 * U * P].rearrange("p (s c) -> p s c", s=2)
        weighted = hT[:, 2 * U * P:4 * U * P].rearrange("p (s c) -> p s c", s=2)
        Wt = sb("Wt", [P, 18, D])
        W_GIN1, W_GIN2, W_Q, W_K, W_V, W_O, W_F1, W_F2, W_GCN, W_LIN, W_E1, W_E2 = \
            0, 1, 2, 3, 4, 5, 6, 10, 14, 15, 16, 17
        ROWS = ['L1_gnn_bo', 'L1_gnn_g1', 'L1_gnn_b1', 'L1_gnn_bf2', 'L1_gnn_g2', 'L1_gnn_b2',
                'L2_gnn_b_gcn', 'L2_gnn_b_lin', 'L3_gnn_b2']
        rows_in = scratch[0:1, 2 * NPAD:2 * NPAD + len(ROWS) * D]
        rows = sb("rows", [P, len(ROWS), D])
        COLS = ['L0_gnn_b1', 'L0_gnn_b2', 'L0_gnn_gamma', 'L0_gnn_beta', 'L3_gnn_b1',
                'L3_gnn_gamma', 'L3_gnn_beta']
        cols = sb("cols", [P, len(COLS) + HC])
        col = {n: cols[:, i:i + 1] for i, n in enumerate(COLS)}
        bf1 = [cols[:, len(COLS) + c:len(COLS) + c + 1] for c in range(HC)]
        ident = sb("ident", [P, P])
        ones = sb("ones", [P, P])
        zeros = sb("zeros", [1, BANK])
        iota_node = sb("iota_node", [P, P])
        dloc = sb("dloc", [P, (NG + 1) * U])
        srcS = sb("srcS", [P, NS], I32)
        startS = sb("startS", [P, NS])
        lastS = sb("lastS", [P, NS])
        step_window = sb("step_window", [1, NG, U], I32)
        step_row = sb("step_row", [1, NG, U], I32)
        last_step = sb("last_step", [1, NW], I32)
        win_reset = sb("win_reset", [P, NS])
        idx_stage = sb("idx_stage", [P, RING * U], I32)
        stat = sb("stat", [P, NW, 6])
        mv = sb("mv", [P, NW, 2])
        rstd = sb("rstd", [P, NW])
        shift = sb("shift", [P, NW])
        bn = sb("bn", [P, 8])
        score_loop = sb("score_loop", [P, NW, HEADS])
        node10 = sb("node10", [P, NW, MC])
        m_node = sb("m_node", [P, NW * HEADS])
        m_all = sb("m_all", [P, NW * HEADS])
        f_edge = sb("f_edge", [P, NW * HEADS])
        f_loop = sb("f_loop", [P, NW * HEADS])
        den = sb("den", [P, NW * HEADS])
        dinv = sb("dinv", [P, NW])
        seg_start = sb("seg_start", [U * HEADS, 2, P])
        seg_max = sb("seg_max", [U * HEADS, 2, P])
        score_now = sb("score_now", [P, 2, U * HEADS])
        start_now = sb("start_now", [P, 2, U * HEADS])
        seg_last = sb("seg_last", [P, 2, U * MC])
        d_exp = sb("d_exp", [P, 2, U * HEADS])
        p_exp = sb("p_exp", [P, 2, U * HEADS])
        step_max = scratch[:, 0:NG * U * MC].rearrange("p (s c) -> p s c", c=MC)

        tq = [0]

        def early(n, rows_=P):
            a = qkv[0:rows_, tq[0]:tq[0] + n]
            tq[0] += n
            return a

        NC5 = len(CHUNKS)
        dstI, srcI = early(NC5 * P).bitcast(I32), early(NC5 * P).bitcast(I32)
        tabs = [early(NC5 * P).rearrange("p (c j) -> p c j", c=NC5) for _ in range(4)]
        dstT, srcT, startT, lastT = tabs
        dstI = dstI.rearrange("p (c j) -> p c j", c=NC5)
        srcI = srcI.rearrange("p (c j) -> p c j", c=NC5)
        sel = early(NC5 * NS).rearrange("p (c s) -> p c s", c=NC5)
        iota_s, tileF, winF, thr, before, fromW = (early(n) for n in (NS, NS, NS, NW - 1, NC5 * (NW - 1), NS))
        before = before.rearrange("p (c w) -> p c w", c=NC5)
        iota_back = early(NS)
        tile_id = early(NC5)
        cntF = early(1)
        lastF, rowF = early(NW), early(NS)
        winF_1 = early(NW)

        ps = ctx.enter_context(nc.psum_tensor("ps", [P, 8 * BANK], F32))
        acc = ps[:, 0:NPAD]

        block = ctx.enter_context(nc.Block())

        def hold(eng, s, value, name):
            eng.wait_ge(s, value)
            eng.sem_inc(sem("held_" + name), 1)

        def tiles_of(b):
            return range(4 * b, min(4 * b + 4, NW))

        def w3(a):
            return a.rearrange("p (w f) -> p w f", f=D)

        def over_groups(eng, body):
            for j in range(UNROLL):
                body(0, j, True)
            with eng.Fori(1, BODIES) as k:
                for j in range(UNROLL):
                    body(k, j, False)

        def slot_uses(k, j):
            return k * (UNROLL // RING) + j // RING + 1

        def all_gathered(phase, k, j):
            return (slot_uses(k, j) + phase * (NG // RING)) * 16 * U

        @block.sync
        def _(sp):
            for name, dstt in (('dst', dstI), ('src', srcI)):
                full = (NCH - 1) * P
                sp.dma_start(dstt[:, 0:NCH - 1, :],
                             t[name][0:full * P].rearrange("(c p j) -> p c j", p=P, j=P)).then_inc(sem("indices_in"), 16)
                sp.dma_start(dstt[0:LASTCH, NCH - 1, :],
                             t[name][full * P:(full + LASTCH) * P].rearrange("(p j) -> p j", j=P)).then_inc(sem("indices_in"), 16)
                sp.dma_start(dstt[0:1, NCH, :],
                             t[name][LAST_ROW:N_EDGES].rearrange("(p j) -> p j", j=P)).then_inc(sem("indices_in"), 16)
            sp.wait_ge(sem("x_cleared"), 1)
            sp.dma_start(x[:, 0:NW - 1, :],
                         t['x'][0:(NW - 1) * P, :].rearrange("(w p) f -> p w f", p=P)).then_inc(sem("x_in"), 16)
            sp.dma_start(x[0:N_NODES - (NW - 1) * P, NW - 1, :],
                         t['x'][(NW - 1) * P:N_NODES, :]).then_inc(sem("x_in"), 16)
            n_w = 0
            for slot, name in ((W_GIN1, 'L0_gnn_W1'), (W_GIN2, 'L0_gnn_W2'), (W_Q, 'L1_gnn_Wq'), (W_K, 'L1_gnn_Wk'),
                               (W_V, 'L1_gnn_Wv'), (W_O, 'L1_gnn_Wo'), (W_GCN, 'L2_gnn_W_gcn'), (W_LIN, 'L2_gnn_W_lin'),
                               (W_E1, 'L3_gnn_W1'), (W_E2, 'L3_gnn_W2')):
                sp.dma_start(Wt[:, slot, :], t[name]).then_inc(sem("weights_in"), 16)
            sp.dma_start(Wt[:, W_F1:W_F1 + HC, :],
                         t['L1_gnn_Wf1'].rearrange("k (c f) -> k c f", c=HC)).then_inc(sem("weights_in"), 16)
            sp.dma_start(Wt[:, W_F2:W_F2 + HC, :],
                         t['L1_gnn_Wf2'].rearrange("(c k) f -> k c f", c=HC)).then_inc(sem("weights_in"), 16)
            for i, name in enumerate(ROWS):
                sp.dma_start(rows_in[0:1, i * D:(i + 1) * D], t[name].rearrange("(a f) -> a f", a=1)).then_inc(sem("weights_in"), 16)
            for name in COLS:
                sp.dma_start(col[name], t[name].rearrange("(f a) -> f a", a=1)).then_inc(sem("weights_in"), 16)
            for c in range(HC):
                sp.dma_start(bf1[c], t['L1_gnn_bf1'][c * P:(c + 1) * P].rearrange("(f a) -> f a", a=1)).then_inc(sem("weights_in"), 16)

            def store_rows(dram, src3, ready, base, width):
                for c in range(0, NW, 5):
                    sp.wait_ge(ready, base + c + 5)
                    sp.dma_start(dram[c * P:(c + 5) * P, :].rearrange("(w p) f -> p w f", p=P),
                                 src3[:, c:c + 5, 0:width]).then_inc(sem("table_stored"), 16)

            store_rows(h0_rows, h, sem("normed"), 0, D)
            store_rows(qv_rows, qkv3, sem("qkv_out"), 0, 2 * D)

            def park(k, j, first):
                sp.wait_ge(sem(f"gathered{j % RING}"), all_gathered(1, k, j))
                sp.dma_start(v_park[bass.DynSlice((k * UNROLL + j) * P, P), :].rearrange("p (u f) -> p u f", u=U),
                             ring[j % RING]).then_inc(sem("parked"), 16)
                sp.wait_ge(sem("parked"), (k * UNROLL + j + 1) * 16)
                sp.sem_inc(sem("park_free"), 1)
            over_groups(sp, park)

            def unpark(k, j, first):
                if not (first and j < RING):
                    hold(sp, sem("c_weighted"), k * UNROLL + j + 1 - RING, "sp")
                sp.dma_start(ring[j % RING], v_park[bass.DynSlice((k * UNROLL + j) * P, P), :].rearrange("p (u f) -> p u f", u=U)).then_inc(sem(f"ring_in{j % RING}"), 16)
            over_groups(sp, unpark)

            store_rows(g2_rows, w3(bufA), sem("g2_out"), 0, D)
            store_rows(h3_rows, h, sem("normed"), 5 * NW, D)

            regs = [sp.alloc_register(f"edge_row{i}") for i in range(U)]

            def load_edges(k, j, first):
                if first and j < RING:
                    hold(sp, sem("c_weighted"), NG, "sp")
                else:
                    hold(sp, sem("e_summed"), k * UNROLL + j + 1 - RING, "sp")
                sp.load(regs, step_row[0:1, bass.DynSlice(k * UNROLL + j, 1), :].rearrange("a g u -> a (g u)"))
                for u in range(U):
                    r = sp.snap(regs[u], min_val=0, max_val=LAST_ROW)
                    sp.dma_start(ring[j % RING][:, u, :], t['edge_attr_128'][bass.DynSlice(r, P), :]).then_inc(sem(f"ring_in{j % RING}"), 16)
            over_groups(sp, load_edges)

            for b in range(NB):
                w0, w1 = tiles_of(b)[0], tiles_of(b)[-1] + 1
                sp.wait_ge(sem("final"), b + 1)
                if w1 * P <= N_NODES:
                    sp.dma_start(out[w0 * P:w1 * P, :].rearrange("(w p) f -> p w f", p=P), h[:, w0:w1, :]).then_inc(sem("stored"), 16)
                else:
                    sp.dma_start(out[w0 * P:N_NODES, :], h[0:N_NODES - w0 * P, w0, :]).then_inc(sem("stored"), 16)
            sp.wait_ge(sem("stored"), 16 * NB)

        @block.gpsimd
        def _(pool):
            pool.memset(x[:, NW - 1, :], 0.0).then_inc(sem("x_cleared"), 1)
            pool.memset(ident[:, :], 0.0).then_inc(sem("pool_zero"), 1)
            pool.memset(ones[:, :], 1.0).then_inc(sem("consts"), 1)
            pool.memset(zeros[:, :], 0.0).then_inc(sem("consts"), 1)
            pool.wait_ge(sem("pool_zero"), 1)
            pool.affine_select(out=ident[:, :], in_=ident[:, :], compare_op=ALU.not_equal, fill=1.0, base=0,
                               pattern=[[-1, P]], channel_multiplier=1).then_inc(sem("consts"), 1)
            imp = dict(allow_small_or_imprecise_dtypes=True)
            pool.iota(iota_node[:, :], [[1, P]], base=0, channel_multiplier=0, **imp).then_inc(sem("consts"), 1)
            pool.iota(iota_s, [[1, NS]], base=0, channel_multiplier=0, **imp).then_inc(sem("consts"), 1)
            pool.iota(iota_back[0:NW - 1, :], [[1, NS]], base=-1, channel_multiplier=-1, **imp).then_inc(sem("consts"), 1)
            pool.iota(thr, [[P, NW - 1]], base=P, channel_multiplier=0, **imp).then_inc(sem("consts"), 1)
            pool.iota(tile_id, [[P, NC5]], base=0, channel_multiplier=1, **imp).then_inc(sem("consts"), 1)
            pool.iota(winF_1[0:1, :], [[1, NW]], base=0, channel_multiplier=0, **imp).then_inc(sem("consts"), 1)

            def gather(phase, table, width, free_sems):
                def body(k, j, first):
                    g = k * UNROLL + j
                    if not (first and j < RING):
                        for s in free_sems:
                            hold(pool, s, g + 1 - RING, "pool")
                    done = (phase * NG + g) + 1
                    c0 = j % RING * U
                    pool.tensor_copy(idx_stage[:, c0:c0 + U], srcS[:, bass.DynSlice(g * U, U)]).then_inc(sem("idx_staged"), 1)
                    hold(pool, sem("idx_staged"), done, "pool")
                    for u in range(U):
                        pool.indirect_dma_start(gath[:, c0 + u, 0:width], None, table[:, :],
                                                bass.IndirectOffsetOnAxis(ap=idx_stage[:, c0 + u:c0 + u + 1], axis=0)
                                                ).then_inc(sem(f"gathered{j % RING}"), 16)
                over_groups(pool, body)

            pool.wait_ge(sem("step_tables"), 5)
            pool.wait_ge(sem("table_stored"), 5 * 16)
            gather(0, h0_rows, D, [sem("s0_summed")])
            pool.wait_ge(sem("table_stored"), 10 * 16)
            gather(1, qv_rows, 2 * D, [sem("a_prod"), sem("park_free")])
            pool.wait_ge(sem("f_ready"), 1)
            pool.tensor_tensor(qkv3[:, :, D:2 * D].rearrange("p w (e d) -> p w e d", d=HD),
                               qkv3[:, :, D:2 * D].rearrange("p w (e d) -> p w e d", d=HD),
                               f_loop[:, :].rearrange("p (w e) -> p w e", e=HEADS).unsqueeze(3).to_broadcast([P, NW, HEADS, HD]),
                               ALU.mult).then_inc(sem("loop_share"), 1)
            pool.wait_ge(sem("table_stored"), 15 * 16)
            gather(2, g2_rows, D, [sem("s2_summed")])
            pool.wait_ge(sem("table_stored"), 20 * 16)
            gather(3, h3_rows, D, [sem("e_added")])

        @block.vector
        def _(v):
            def ln_stats(i, src3):
                s = sem("ln_v")
                b = i * LAYERS_LN
                for w in range(NW):
                    v.bn_stats(stat[:, w, :], src3[:, w, :]).then_inc(s, 1)
                v.wait_ge(s, b + NW)
                for w in range(NW):
                    v.bn_aggr(mv[:, w, :], stat[:, w, :]).then_inc(s, 1)
                v.wait_ge(s, b + 2 * NW)
                v.tensor_scalar(rstd[:, :], mv[:, :, 1], LN_EPS, None, ALU.add).then_inc(s, 1)
                v.wait_ge(sem("ln_sqrt"), i + 1)
                v.reciprocal(rstd[:, :], rstd[:, :]).then_inc(s, 1)
                v.wait_ge(s, b + 2 * NW + 2)
                v.scalar_tensor_tensor(shift[:, :], mv[:, :, 0], -1.0, rstd[:, :], ALU.mult, ALU.mult).then_inc(s, 1)

            def evacuate(dst, ready, base, done, src=None):
                for b, (c0, n) in enumerate(BANKS):
                    v.wait_ge(ready, base + b + 1)
                    v.tensor_copy(dst[:, c0:c0 + n], ps[:, c0:c0 + n]).then_inc(done, 1)

            def make_onehot(dst, g_expr, done):
                for u in range(U):
                    i = v.tensor_scalar(dst[:, u * P:(u + 1) * P], iota_node[:, :],
                                        dloc[:, bass.DynSlice(g_expr * U + u, 1)], None, ALU.is_equal)
                i.then_inc(done, 1)

            def bn_coeffs(z, gamma, beta, s, z_done, z_value):
                v.wait_ge(z_done, z_value)
                for b, (c0, n) in enumerate(BANKS):
                    n = min(n, N_NODES - c0)
                    v.bn_stats(stat[:, b, :], z[:, c0:c0 + n]).then_inc(s, 1)
                v.wait_ge(s, NB)
                v.bn_aggr(bn[:, 0:2], stat[:, 0:NB, :].rearrange("p b c -> p (b c)")).then_inc(s, 1)
                v.wait_ge(s, NB + 1)
                v.tensor_scalar(bn[:, 4:5], bn[:, 1:2], BN_EPS, None, ALU.add).then_inc(s, 1)
                v.wait_ge(sem("bn_sqrt"), 1 if z_done is sem("gin_z2") else 2)
                v.reciprocal(bn[:, 5:6], bn[:, 4:5]).then_inc(s, 1)
                v.wait_ge(s, NB + 3)
                v.tensor_tensor(bn[:, 2:3], bn[:, 5:6], gamma, ALU.mult).then_inc(s, 1)
                v.wait_ge(s, NB + 4)
                v.tensor_tensor(bn[:, 6:7], bn[:, 0:1], bn[:, 2:3], ALU.mult).then_inc(s, 1)
                v.wait_ge(s, NB + 5)
                v.tensor_tensor(bn[:, 3:4], beta, bn[:, 6:7], ALU.subtract).then_inc(s, 1)

            q = sem("pro_v")
            n = [0]

            def step(i):
                n[0] += 1
                i.then_inc(q, 1)

            def settle():
                v.wait_ge(q, n[0])

            v.memset(dloc[:, NS:NS + U], -1.0).then_inc(sem("pad_set"), 1)
            v.wait_ge(sem("consts"), 9)
            v.wait_ge(sem("indices_in"), 6 * 16)
            for c, k in enumerate(CHUNKS):
                step(v.tensor_copy(dstT[0:k, c, :], dstI[0:k, c, :]))
                step(v.tensor_copy(srcT[0:k, c, :], srcI[0:k, c, :]))
            settle()
            step(v.memset(dstT[0:1, NCH, 0:OVERLAP], -1e6))
            for c, k in enumerate(CHUNKS[:NCH]):
                step(v.tensor_scalar(before[0:k, c, :], thr[0:k, :], dstT[0:k, c, P - 1:P], None, ALU.is_gt))
            settle()
            v.sem_inc(sem("before_ready"), 1)
            for c, k in enumerate(CHUNKS):
                step(v.memset(startT[0:k, c, 0:1], 0.0))
                step(v.memset(lastT[0:k, c, P - 1:P], 1.0))
                step(v.tensor_tensor(lastT[0:k, c, 0:P - 1], dstT[0:k, c, 1:P], dstT[0:k, c, 0:P - 1], ALU.not_equal))
            settle()
            for c, k in enumerate(CHUNKS):
                step(v.tensor_scalar(startT[0:k, c, 1:P], lastT[0:k, c, 0:P - 1], NONE, None, ALU.mult))
            v.wait_ge(sem("counts_ready"), 1)
            step(v.tensor_copy(cntF[0:NW - 1, :], ps[0:NW - 1, 0:1]))
            step(v.tensor_copy(lastF[0:1, 0:NW - 1], ps[0:1, BANK:BANK + NW - 1]))
            step(v.memset(lastF[0:1, NW - 1:NW], float(NT - 1)))
            settle()
            step(v.tensor_tensor(last_step[:, :], lastF[0:1, :], winF_1[0:1, :], ALU.add))
            step(v.tensor_scalar(fromW[0:NW - 1, :], iota_back[0:NW - 1, :], cntF[0:NW - 1, :], None, ALU.is_ge))
            settle()
            v.sem_inc(sem("reached_ready"), 1)
            v.wait_ge(sem("window_ready"), 1)
            step(v.tensor_copy(winF, ps[:, 2 * BANK:2 * BANK + NS]))
            settle()
            step(v.tensor_tensor(tileF, iota_s, winF, ALU.subtract))
            step(v.memset(win_reset[:, 0:1], NONE))
            step(v.tensor_tensor(win_reset[:, 1:NS], winF[:, 1:NS], winF[:, 0:NS - 1], ALU.not_equal))
            settle()
            for c in range(NCH):
                step(v.tensor_scalar(sel[:, c, :], tileF, tile_id[:, c:c + 1], None, ALU.is_equal))
            step(v.tensor_scalar(sel[0:1, NCH, :], tileF[0:1, :], float(LAST_TILE), None, ALU.is_equal))
            step(v.tensor_scalar(win_reset[:, 1:NS], win_reset[:, 1:NS], NONE, None, ALU.mult))
            settle()
            v.sem_inc(sem("select_ready"), 1)
            step(v.tensor_copy(step_window[:, :, :], winF[0:1, :].rearrange("p (g u) -> p g u", u=U)))
            step(v.tensor_scalar(rowF[0:1, :], tileF[0:1, :], float(P), float(LAST_ROW), ALU.mult, ALU.min))
            settle()
            step(v.tensor_copy(step_row[:, :, :], rowF[0:1, :].rearrange("p (g u) -> p g u", u=U)))
            v.wait_ge(sem("selected"), 1)
            v.scalar_tensor_tensor(dloc[:, 0:NS], winF, -float(P), ps[:, 3 * BANK:3 * BANK + NS], ALU.mult, ALU.add).then_inc(sem("step_tables"), 1)
            v.wait_ge(sem("selected"), 2)
            v.tensor_copy(srcS[:, :], ps[:, 4 * BANK:4 * BANK + NS]).then_inc(sem("step_tables"), 1)
            v.wait_ge(sem("selected"), 3)
            v.tensor_copy(startS[:, :], ps[:, 5 * BANK:5 * BANK + NS]).then_inc(sem("step_tables"), 1)
            v.wait_ge(sem("selected"), 4)
            v.tensor_copy(lastS[:, :], ps[:, 6 * BANK:6 * BANK + NS]).then_inc(sem("step_tables"), 1)
            settle()
            v.sem_inc(sem("step_tables"), 1)
            v.wait_ge(sem("weights_in"), 16 * (12 + len(ROWS) + len(COLS) + HC))
            v.tensor_scalar(Wt[:, W_Q, :], Wt[:, W_Q, :], 1.0 / SQRT_HD, None, ALU.mult).then_inc(sem("wq_scaled"), 1)
            v.wait_ge(sem("rows_spread"), 1)
            for i in range(3):
                v.tensor_copy(rows[:, 3 * i:3 * i + 3, :].rearrange("p r f -> p (r f)"), ps[:, i * BANK:i * BANK + 3 * D]).then_inc(sem("rows_ready"), 1)

            v.wait_ge(sem("x_in"), 32)
            ln_stats(0, x)
            evacuate(hT, sem("hT_mm"), 0, sem("hT_out"))

            def onehots_for(summed, made):
                def body(k, j, first):
                    if not (first and j < RING):
                        hold(v, summed, k * UNROLL + j + 1 - RING, "v")
                    make_onehot(onehot[:, j % RING, :], k * UNROLL + j, made)
                over_groups(v, body)

            onehots_for(sem("s0_summed"), sem("s0_onehot"))
            v.wait_ge(sem("s0_summed"), NG)
            for b, (c0, w) in enumerate(BANKS):
                v.tensor_tensor(bufA[:, c0:c0 + w], ps[:, c0:c0 + w], hT[:, c0:c0 + w], ALU.add).then_inc(sem("gin_sum"), 1)
            bn_coeffs(bufC, col['L0_gnn_gamma'], col['L0_gnn_beta'], sem("bn0"), sem("gin_z2"), NB)
            for b, (c0, w) in enumerate(BANKS):
                v.wait_ge(sem("gin_bn"), b + 1)
                v.tensor_tensor(bufA[:, c0:c0 + w], bufB[:, c0:c0 + w], hT[:, c0:c0 + w], ALU.add).then_inc(sem("gin_y"), 1)
            for b, (c0, w) in enumerate(BANKS):
                v.wait_ge(sem("gin_yT"), b + 1)
                xs = x[:, tiles_of(b)[0]:tiles_of(b)[-1] + 1, :].rearrange("p w f -> p (w f)")
                v.tensor_tensor(xs, xs, ps[:, c0:c0 + w], ALU.add).then_inc(sem("x_new"), 1)

            v.wait_ge(sem("x_new"), NB)
            ln_stats(1, x)
            evacuate(hT, sem("hT_mm"), NB, sem("hT_out"))
            for w in range(1, NW, 2):
                v.wait_ge(sem("qkv_mm"), w + 1)
                v.wait_ge(sem("qkv_out"), w)
                v.tensor_copy(qkv3[:, w, :], ps[:, (w % 7) * BANK:(w % 7) * BANK + 3 * D]).then_inc(sem("qkv_out"), 1)
            v.wait_ge(sem("qkv_out"), NW)
            v.tensor_tensor(w3(bufC), qkv3[:, :, 0:D], qkv3[:, :, 2 * D:3 * D], ALU.mult).then_inc(sem("loop_v"), 1)
            v.wait_ge(sem("loop_v"), 1)
            v.tensor_reduce(score_loop[:, :, :].rearrange("p w e -> p (w e)"), bufC.rearrange("p (g d) -> p g d", d=HD), AX.X, ALU.add).then_inc(sem("loop_v"), 1)

            def seg_scan(g, sl):
                v.wait_ge(sem("a_flags"), g + 1)
                v.tensor_tensor_scan(seg_max[:, sl, :], seg_start[:, sl, :], ps[0:U * HEADS, 4 * BANK:4 * BANK + P],
                                     NONE, ALU.add, ALU.max).then_inc(sem("a_scan"), 1)

            def seg_keep(g, sl):
                hold(v, sem("a_back"), g + 1, "v")
                last = lastS[:, bass.DynSlice(g * U, U)]
                sl3 = seg_last[:, sl, :].rearrange("p (u c) -> p u c", c=MC)
                v.tensor_tensor(sl3[:, :, 0:HEADS], ps[:, 6 * BANK:6 * BANK + U * HEADS].rearrange("p (u e) -> p u e", e=HEADS),
                                last.unsqueeze(2).to_broadcast([P, U, HEADS]), ALU.mult)
                v.tensor_copy(sl3[:, :, HEADS], last).then_inc(sem("a_last"), 1)

            v.memset(seg_last[:, :, :].rearrange("p s (u c) -> p (s u) c", c=MC)[:, :, MC - 1:MC], 1.0)
            make_onehot(onehot[:, 0, :], 0, sem("a_onehot"))

            def attend(k, j, first):
                g = k * UNROLL + j
                if not (first and j < RING - 1):
                    hold(v, sem("a_max_mm"), g + 2 - RING, "v")
                make_onehot(onehot[:, (j + 1) % RING, :], g + 1, sem("a_onehot"))
                if not (first and j == 0):
                    seg_scan(g - 1, (j - 1) % 2)
                v.wait_ge(sem(f"gathered{j % RING}"), all_gathered(1, k, j))
                v.wait_ge(sem("a_k"), g + 1)
                v.tensor_tensor(weighted[:, 0, :].rearrange("p (u f) -> p u f", u=U), ps[:, 2 * BANK:2 * BANK + U * D].rearrange("p (u f) -> p u f", u=U),
                                gath_lo[j % RING], ALU.mult).then_inc(sem("a_prod"), 1)
                hold(v, sem("a_prod"), g + 1, "v")
                v.tensor_reduce(score_now[:, j % 2, :], weighted[:, 0, :].rearrange("p (g d) -> p g d", d=HD),
                                AX.X, ALU.add).then_inc(sem("a_score"), 1)
                if not (first and j == 0):
                    seg_keep(g - 1, (j - 1) % 2)
            over_groups(v, attend)
            seg_scan(NG - 1, (NG - 1) % 2)
            seg_keep(NG - 1, (NG - 1) % 2)

            v.wait_ge(sem("a_max_out"), NG)
            c = sem("max_v")
            pen = bufC[:, 0:NS]
            v.tensor_scalar(pen, step_max[:, :, HEADS], -NONE, NONE, ALU.mult, ALU.add).then_inc(c, 1)
            v.wait_ge(c, 1)
            v.tensor_tensor(step_max[:, :, 0:HEADS], step_max[:, :, 0:HEADS], pen.unsqueeze(2).to_broadcast([P, NS, HEADS]), ALU.add).then_inc(c, 1)
            v.wait_ge(c, 2)
            for e in range(HEADS):
                v.tensor_tensor_scan(bufC[:, (e % 2) * NS + NS:(e % 2) * NS + 2 * NS], win_reset[:, :], step_max[:, :, e], NONE, ALU.add, ALU.max).then_inc(c, 1)
                v.wait_ge(c, 3 + 2 * e)
                v.tensor_copy(step_max[:, :, e], bufC[:, (e % 2) * NS + NS:(e % 2) * NS + 2 * NS]).then_inc(c, 1)
            v.tensor_tensor_scan(bufC[:, 3 * NS:4 * NS], step_max[:, :, MC - 1], step_max[:, :, MC - 1], 0.0, ALU.add, ALU.bypass).then_inc(c, 1)
            v.wait_ge(c, 3 + 2 * HEADS)
            v.tensor_copy(step_max[:, :, MC - 1], bufC[:, 3 * NS:4 * NS]).then_inc(c, 1)
            v.wait_ge(c, 4 + 2 * HEADS)
            r1 = v.alloc_register("last_step_reg")
            with v.Fori(0, NW) as w:
                v.load([r1], last_step[0:1, bass.DynSlice(w, 1)])
                s_last = v.snap(r1, min_val=0, max_val=NS - 1)
                v.tensor_copy(node10[:, bass.DynSlice(w, 1), :], step_max[:, bass.DynSlice(s_last, 1), :]).then_inc(sem("node_max"), 1)
            v.wait_ge(sem("node_max"), NW)
            f = sem("fac_v")
            v.tensor_copy(m_node[:, :].rearrange("p (w e) -> p w e", e=HEADS), node10[:, :, 0:HEADS]).then_inc(sem("m_ready"), 1)
            v.tensor_scalar(dinv[:, 0:1], node10[:, 0:1, MC - 1], 1.0, None, ALU.add).then_inc(f, 1)
            v.tensor_tensor(dinv[:, 1:NW], node10[:, 1:NW, MC - 1], node10[:, 0:NW - 1, MC - 1], ALU.subtract).then_inc(f, 1)
            v.wait_ge(f, 2)
            v.tensor_scalar(dinv[:, 1:NW], dinv[:, 1:NW], 1.0, None, ALU.add).then_inc(f, 1)
            v.wait_ge(f, 3)
            v.tensor_scalar(dinv[:, :], dinv[:, :], 1.0, None, ALU.max).then_inc(f, 1)
            v.wait_ge(sem("deg_sqrt"), 1)
            v.reciprocal(dinv[:, :], dinv[:, :]).then_inc(f, 1)
            v.wait_ge(sem("m_ready"), 1)
            sl = score_loop[:, :, :].rearrange("p w e -> p (w e)")
            v.wait_ge(sem("loop_v"), 2)
            v.tensor_tensor(m_all[:, :], m_node[:, :], sl, ALU.max).then_inc(f, 1)
            v.wait_ge(f, 6)
            v.tensor_tensor(f_edge[:, :], m_node[:, :], m_all[:, :], ALU.subtract).then_inc(f, 1)
            v.tensor_tensor(f_loop[:, :], sl, m_all[:, :], ALU.subtract).then_inc(f, 1)

            make_onehot(onehot[:, 0, :], 0, sem("c_onehot"))

            def soften(k, j, first):
                g = k * UNROLL + j
                par = j % 2
                v.wait_ge(sem("c_m"), g + 1)
                v.tensor_tensor(d_exp[:, par, :], score[:, bass.DynSlice(g * U * HEADS, U * HEADS)], ps[:, B7:B7 + U * HEADS],
                                ALU.subtract).then_inc(sem("c_d"), 1)
                if not (first and j < RING - 1):
                    hold(v, sem("c_summed"), g + 2 - RING, "v")
                make_onehot(onehot[:, (j + 1) % RING, :], g + 1, sem("c_onehot"))
                v.wait_ge(sem(f"ring_in{j % RING}"), slot_uses(k, j) * 16)
                v.wait_ge(sem("c_exp"), g + 1)
                v.tensor_tensor(weighted[:, par, :].rearrange("p (u e d) -> p u e d", u=U, d=HD),
                                ring[j % RING].rearrange("p u (e d) -> p u e d", d=HD),
                                p_exp[:, par, :].rearrange("p (u e) -> p u e", u=U).unsqueeze(3).to_broadcast([P, U, HEADS, HD]),
                                ALU.mult).then_inc(sem("c_weighted"), 1)
            over_groups(v, soften)

            v.wait_ge(sem("c_summed"), NG)
            v.wait_ge(sem("f_exp"), 2)
            v.tensor_tensor(den[:, :], ps[:, DEN:DEN + NW * HEADS], f_edge[:, :], ALU.mult).then_inc(f, 1)
            v.wait_ge(f, 9)
            v.tensor_tensor(den[:, :], den[:, :], f_loop[:, :], ALU.add).then_inc(f, 1)
            v.wait_ge(f, 10)
            v.tensor_scalar(den[:, :], den[:, :], 1e-8, None, ALU.add).then_inc(f, 1)
            v.wait_ge(f, 11)
            v.reciprocal(den[:, :], den[:, :]).then_inc(f, 1)
            v.wait_ge(f, 12)
            v.tensor_tensor(f_loop[:, :], f_loop[:, :], den[:, :], ALU.mult).then_inc(sem("f_ready"), 1)
            v.tensor_tensor(f_edge[:, :], f_edge[:, :], den[:, :], ALU.mult).then_inc(f, 1)
            v.wait_ge(f, 13)
            for b, (c0, n_) in enumerate(BANKS):
                w0, nw = tiles_of(b)[0], len(tiles_of(b))
                v.tensor_tensor(bufA[:, c0:c0 + n_].rearrange("p (g d) -> p g d", d=HD), ps[:, c0:c0 + n_].rearrange("p (g d) -> p g d", d=HD),
                                f_edge[:, w0 * HEADS:(w0 + nw) * HEADS].unsqueeze(2).to_broadcast([P, nw * HEADS, HD]), ALU.mult).then_inc(sem("o_edge"), 1)
            v.wait_ge(sem("rows_ready"), 3)
            v.tensor_tensor(h[:, :, :], h[:, :, :], rows[:, 0:1, :].to_broadcast([P, NW, D]), ALU.add).then_inc(sem("h_bo"), 1)
            v.wait_ge(sem("loop_share"), 1)
            for b, (c0, n_) in enumerate(BANKS):
                w0, w1 = tiles_of(b)[0], tiles_of(b)[-1] + 1
                v.wait_ge(sem("o_edge"), b + 1)
                v.tensor_tensor(w3(bufA)[:, w0:w1, :], w3(bufA)[:, w0:w1, :], qkv3[:, w0:w1, D:2 * D], ALU.add).then_inc(sem("o_all"), 1)
            evacuate(bufB, sem("oT_mm"), 0, sem("oT_out"))
            v.wait_ge(sem("h_bo"), 1)
            for b, (c0, n_) in enumerate(BANKS):
                w0, w1 = tiles_of(b)[0], tiles_of(b)[-1] + 1
                v.wait_ge(sem("attn_mm"), b + 1)
                v.tensor_tensor(w3(bufA)[:, w0:w1, :], h[:, w0:w1, :], w3(ps[:, c0:c0 + n_]), ALU.add).then_inc(sem("r1"), 1)
            v.wait_ge(sem("r1"), NB)
            ln_stats(2, w3(bufA))

            def affine(src, ready, base, g_row, b_row, s, done):
                for b, (c0, n_) in enumerate(BANKS):
                    w0, w1 = tiles_of(b)[0], tiles_of(b)[-1] + 1
                    v.wait_ge(ready, base + w1)
                    a = w3(src)[:, w0:w1, :]
                    v.tensor_tensor(a, a, rows[:, g_row:g_row + 1, :].to_broadcast([P, w1 - w0, D]), ALU.mult).then_inc(s, 1)
                    v.wait_ge(s, b + 1)
                    v.tensor_tensor(a, a, rows[:, b_row:b_row + 1, :].to_broadcast([P, w1 - w0, D]), ALU.add).then_inc(done, 1)
            affine(bufA, sem("normed"), 2 * NW, 1, 2, sem("aff1"), sem("x1"))
            evacuate(bufB, sem("x1T_mm"), 0, sem("x1T_out"))
            v.wait_ge(sem("x1T_out"), NB)
            v.tensor_tensor(w3(bufA), w3(bufA), rows[:, 3:4, :].to_broadcast([P, NW, D]), ALU.add).then_inc(sem("x1_bf2"), 1)
            v.wait_ge(sem("x1_bf2"), 1)
            for b, (c0, n_) in enumerate(BANKS):
                v.wait_ge(sem("ffn_mm"), b + 1)
                v.tensor_tensor(bufB[:, c0:c0 + n_], bufA[:, c0:c0 + n_], ps[:, c0:c0 + n_], ALU.add).then_inc(sem("r2"), 1)
            v.wait_ge(sem("r2"), NB)
            ln_stats(3, w3(bufB))
            affine(bufB, sem("normed"), 3 * NW, 4, 5, sem("aff2"), sem("y1"))
            v.wait_ge(sem("y1"), NB)
            xf = x[:, :, :].rearrange("p w f -> p (w f)")
            v.tensor_tensor(xf, xf, bufB, ALU.add).then_inc(sem("x_new"), 1)

            v.wait_ge(sem("x_new"), NB + 1)
            ln_stats(4, x)
            evacuate(hT, sem("hT_mm"), 2 * NB, sem("hT_out"))
            v.tensor_tensor(rows[:, 6, :], rows[:, 6, :], rows[:, 7, :], ALU.add).then_inc(sem("b_both"), 1)
            v.wait_ge(sem("b_both"), 1)
            for w in range(NW):
                c0 = (4 + w % 4) * BANK
                v.wait_ge(sem("gcn_mm"), w + 1)
                v.tensor_tensor(w3(bufB)[:, w, :], ps[:, c0:c0 + D], rows[:, 6, :], ALU.add).then_inc(sem("lin_out"), 1)
            onehots_for(sem("s2_summed"), sem("s2_onehot"))
            v.wait_ge(sem("s2_summed"), NG)
            for b, (c0, n_) in enumerate(BANKS):
                v.tensor_tensor(bufC[:, c0:c0 + n_], bufA[:, c0:c0 + n_], ps[:, c0:c0 + n_], ALU.add).then_inc(sem("g_sum"), 1)
            for w in range(NW):
                v.wait_ge(sem("g_sum"), w // 4 + 1)
                v.scalar_tensor_tensor(w3(bufC)[:, w, :], w3(bufC)[:, w, :], dinv[:, w:w + 1], w3(bufB)[:, w, :], ALU.mult, ALU.add).then_inc(sem("g_lin"), 1)
            v.wait_ge(sem("g_lin"), NW)
            v.scalar_tensor_tensor(xf, bufC, 0.0, xf, ALU.max, ALU.add).then_inc(sem("x_new"), 1)

            v.wait_ge(sem("x_new"), NB + 2)
            ln_stats(5, x)
            evacuate(hT, sem("hT_mm"), 3 * NB, sem("hT_out"))
            v.tensor_tensor(x[:, :, :], x[:, :, :], rows[:, 8:9, :].to_broadcast([P, NW, D]), ALU.add).then_inc(sem("x_b2"), 1)

            def add_edges(k, j, first):
                g = k * UNROLL + j
                if not (first and j < RING):
                    hold(v, sem("e_summed"), g + 1 - RING, "v")
                make_onehot(onehot[:, j % RING, :], g, sem("e_onehot"))
                v.wait_ge(sem(f"gathered{j % RING}"), all_gathered(3, k, j))
                v.wait_ge(sem(f"ring_in{j % RING}"), (NG // RING) * 16 + slot_uses(k, j) * 16 * U)
                v.tensor_tensor(ring[j % RING], ring[j % RING], gath_lo[j % RING], ALU.add).then_inc(sem("e_added"), 1)
            over_groups(v, add_edges)
            v.wait_ge(sem("e_summed"), NG)
            for b, (c0, w) in enumerate(BANKS):
                v.tensor_tensor(bufA[:, c0:c0 + w], ps[:, c0:c0 + w], hT[:, c0:c0 + w], ALU.add).then_inc(sem("gine_sum"), 1)
            bn_coeffs(bufB, col['L3_gnn_gamma'], col['L3_gnn_beta'], sem("bn3"), sem("gine_z"), NB)
            v.wait_ge(sem("x_b2"), 1)
            for b, (c0, n_) in enumerate(BANKS):
                w0, w1 = tiles_of(b)[0], tiles_of(b)[-1] + 1
                v.wait_ge(sem("out_mm"), b + 1)
                v.tensor_tensor(h[:, w0:w1, :], x[:, w0:w1, :], w3(ps[:, c0:c0 + n_]), ALU.add).then_inc(sem("final"), 1)

        @block.scalar
        def _(a):
            def normalise(i, src3, dst3, func):
                a.wait_ge(sem("ln_v"), i * LAYERS_LN + 2 * NW + 1)
                a.activation(rstd[:, :], rstd[:, :], ACT.Sqrt).then_inc(sem("ln_sqrt"), 1)
                a.wait_ge(sem("ln_v"), (i + 1) * LAYERS_LN)
                for w in range(NW):
                    a.activation(dst3[:, w, :], src3[:, w, :], func, bias=shift[:, w:w + 1], scale=rstd[:, w:w + 1]).then_inc(sem("normed"), 1)

            def bank_act(dst, ready, done, func, **kw):
                for b, (c0, n) in enumerate(BANKS):
                    a.wait_ge(ready, b + 1)
                    a.activation(dst[:, c0:c0 + n], ps[:, c0:c0 + n], func, **kw).then_inc(done, 1)

            def bn_apply(src, dst, s, done):
                a.wait_ge(s, NB + 2)
                a.activation(bn[:, 4:5], bn[:, 4:5], ACT.Sqrt).then_inc(sem("bn_sqrt"), 1)
                a.wait_ge(s, NB + 6)
                for b, (c0, n) in enumerate(BANKS):
                    a.activation(dst[:, c0:c0 + n], src[:, c0:c0 + n], ACT.Identity, bias=bn[:, 3:4], scale=bn[:, 2:3]).then_inc(done, 1)

            normalise(0, x, h, ACT.Relu)
            bank_act(bufB, sem("gin_mm1"), sem("gin_z1"), ACT.Relu, bias=col['L0_gnn_b1'])
            bank_act(bufC, sem("gin_mm2"), sem("gin_z2"), ACT.Identity, bias=col['L0_gnn_b2'])
            bn_apply(bufC, bufB, sem("bn0"), sem("gin_bn"))

            normalise(1, x, h, ACT.Relu)
            for w in range(0, NW, 2):
                a.wait_ge(sem("qkv_mm"), w + 1)
                if w:
                    a.wait_ge(sem("qkv_out"), w)
                a.activation(qkv3[:, w, :], ps[:, (w % 7) * BANK:(w % 7) * BANK + 3 * D], ACT.Copy).then_inc(sem("qkv_out"), 1)

            def turn(g, sl):
                a.wait_ge(sem("a_turned"), g + 1)
                a.activation(onehotT[:, sl, :], ps[:, sl * BANK:(sl + 1) * BANK], ACT.Copy).then_inc(sem("a_onehotT"), 1)

            def max_out(g):
                hold(a, sem("a_max_mm"), g + 1, "a")
                a.activation(step_max[:, bass.DynSlice(g * U, U), :], ps[:, B7:B7 + U * MC].rearrange("p (u c) -> p u c", c=MC),
                             ACT.Copy).then_inc(sem("a_max_out"), 1)

            turn(0, 0)

            def attend(k, j, first):
                g = k * UNROLL + j
                turn(g + 1, (j + 1) % 2)
                a.activation(start_now[:, j % 2, :].rearrange("p (u e) -> p u e", e=HEADS),
                             startS[:, bass.DynSlice(g * U, U)].unsqueeze(2).to_broadcast([P, U, HEADS]), ACT.Copy).then_inc(sem("a_start"), 1)
                hold(a, sem("a_score"), g + 1, "a")
                a.activation(score[:, bass.DynSlice(g * U * HEADS, U * HEADS)], score_now[:, j % 2, :], ACT.Copy)
                a.wait_ge(sem("a_turned_s"), g + 1)
                a.activation(seg_start[:, j % 2, :], ps[0:U * HEADS, 5 * BANK:5 * BANK + P], ACT.Copy).then_inc(sem("a_flags"), 1)
                if not (first and j == 0):
                    max_out(g - 1)
            over_groups(a, attend)
            max_out(NG - 1)

            a.wait_ge(sem("fac_v"), 4)
            a.activation(dinv[:, :], dinv[:, :], ACT.Sqrt).then_inc(sem("deg_sqrt"), 1)
            a.wait_ge(sem("fac_v"), 8)
            a.activation(f_edge[:, :], f_edge[:, :], ACT.Exp).then_inc(sem("f_exp"), 1)
            a.activation(f_loop[:, :], f_loop[:, :], ACT.Exp).then_inc(sem("f_exp"), 1)

            def turn_c(g, par):
                a.wait_ge(sem("c_turned"), g + 1)
                a.activation(onehotT[:, par, :], ps[:, B7:B7 + U * P], ACT.Copy).then_inc(sem("c_onehotT"), 1)

            turn_c(0, 0)

            def soften(k, j, first):
                g = k * UNROLL + j
                a.wait_ge(sem("c_d"), g + 1)
                a.activation(p_exp[:, j % 2, :], d_exp[:, j % 2, :], ACT.Exp).then_inc(sem("c_exp"), 1)
                turn_c(g + 1, (j + 1) % 2)
            over_groups(a, soften)

            normalise(2, w3(bufA), w3(bufA), ACT.Identity)
            for b, (c0, n) in enumerate(BANKS):
                for c in range(HC):
                    i = b * HC + c
                    dst = bufC[:, c0:c0 + n] if c == HC - 1 else qkv[:, c * NPAD + c0:c * NPAD + c0 + n]
                    a.wait_ge(sem("ffn1_mm"), i + 1)
                    a.activation(dst, ps[:, (i % 7) * BANK:(i % 7) * BANK + n], ACT.Gelu, bias=bf1[c]).then_inc(sem("ffn1_out"), 1)
            normalise(3, w3(bufB), w3(bufB), ACT.Identity)

            normalise(4, x, h, ACT.Relu)
            for w in range(NW):
                c0 = (w % 4) * BANK
                a.wait_ge(sem("gcn_mm"), w + 1)
                a.activation(w3(bufA)[:, w, :], ps[:, c0:c0 + D], ACT.Copy, scale=dinv[:, w:w + 1]).then_inc(sem("g2_out"), 1)

            normalise(5, x, h, ACT.Relu)

            def relu_edges(k, j, first):
                a.wait_ge(sem("e_added"), k * UNROLL + j + 1)
                a.activation(ring[j % RING], ring[j % RING], ACT.Relu).then_inc(sem("e_relu"), 1)
            over_groups(a, relu_edges)
            bank_act(bufB, sem("gine_mm"), sem("gine_z"), ACT.Relu, bias=col['L3_gnn_b1'])
            bn_apply(bufB, bufC, sem("bn3"), sem("gine_bn"))

        @block.tensor
        def _(pe):
            regs = [pe.alloc_register(f"window{i}") for i in range(2 * U)]

            def windows(k, j):
                pe.load(regs[j % 2 * U:(j % 2 + 1) * U], step_window[0:1, bass.DynSlice(k * UNROLL + j, 1), :].rearrange("a g u -> a (g u)"))
                return windows_again(j)

            def windows_again(j):
                return [pe.snap(regs[j % 2 * U + u], min_val=0, max_val=NW - 1) for u in range(U)]

            def transpose(dst, src, **kw):
                return pe.matmul(dst, src, ident[0:src.shape[0], 0:src.shape[0]], start=True, stop=True, is_transpose=True, **kw)

            def turn_rows(src3, ready, value, done, free=None):
                for b, (c0, n) in enumerate(BANKS):
                    pe.wait_ge(ready, value(b))
                    for w in tiles_of(b):
                        i = transpose(ps[:, w * P:(w + 1) * P], src3[:, w, :])
                    i.then_inc(done, 1)

            def clear_sums():
                for b in range(NB):
                    i = pe.matmul(ps[:, b * BANK:(b + 1) * BANK], zeros[:, 0:P], zeros[:, :], start=True, stop=False, skip_group_check=True)
                i.then_inc(sem("cleared"), 1)

            def bank_mm(lhsT, rhs, ready, done):
                for b, (c0, n) in enumerate(BANKS):
                    pe.wait_ge(ready, b + 1)
                    pe.matmul(ps[:, c0:c0 + n], lhsT, rhs[:, c0:c0 + n], start=True, stop=True).then_inc(done, 1)

            pe.wait_ge(sem("before_ready"), 1)
            for c, k in enumerate(CHUNKS[:NCH]):
                pe.matmul(ps[0:NW - 1, 0:1], before[0:k, c, :], ones[0:k, 0:1], start=c == 0, stop=c == NCH - 1)
            for c, k in enumerate(CHUNKS[:NCH]):
                i = pe.matmul(ps[0:1, BANK:BANK + NW - 1], ones[0:k, 0:1], before[0:k, c, :], start=c == 0, stop=c == NCH - 1)
            i.then_inc(sem("counts_ready"), 1)
            pe.wait_ge(sem("reached_ready"), 1)
            pe.matmul(ps[:, 2 * BANK:2 * BANK + NS], ones[0:NW - 1, :], fromW[0:NW - 1, :], start=True, stop=True).then_inc(sem("window_ready"), 1)
            pe.wait_ge(sem("select_ready"), 1)
            for i_, tab in enumerate(tabs):
                for c, k in enumerate(CHUNKS):
                    i = pe.matmul(ps[:, (3 + i_) * BANK:(3 + i_) * BANK + NS], tab[0:k, c, :], sel[0:k, c, :], start=c == 0, stop=c == NC5 - 1)
                i.then_inc(sem("selected"), 1)
            pe.wait_ge(sem("weights_in"), 16 * (12 + len(ROWS) + len(COLS) + HC))
            for i_ in range(3):
                i = pe.matmul(ps[:, i_ * BANK:i_ * BANK + 3 * D], ones[0:1, :], rows_in[0:1, i_ * 3 * D:(i_ + 1) * 3 * D], start=True, stop=True)
            i.then_inc(sem("rows_spread"), 1)

            def sum_groups(phase, onehot_done, summed, by_feature, msg, ready):
                def body(k, j, first):
                    g = k * UNROLL + j
                    pe.wait_ge(onehot_done, g + 1)
                    ready(k, j)
                    win = windows(k, j)
                    for u in range(U):
                        o = onehot[:, j % RING, u * P:(u + 1) * P]
                        m = msg(j % RING, u)
                        i = pe.matmul(acc[:, bass.DynSlice(win[u] * P, P)], m if by_feature else o, o if by_feature else m,
                                      start=False, stop=False, skip_group_check=True)
                    i.then_inc(summed, 1)
                over_groups(pe, body)

            def gathered(phase):
                return lambda k, j: pe.wait_ge(sem(f"gathered{j % RING}"), all_gathered(phase, k, j))

            pe.wait_ge(sem("rows_ready"), 3)
            pe.wait_ge(sem("step_tables"), 5)
            turn_rows(h, sem("normed"), lambda b: tiles_of(b)[-1] + 1, sem("hT_mm"))
            pe.wait_ge(sem("hT_out"), NB)
            clear_sums()
            sum_groups(0, sem("s0_onehot"), sem("s0_summed"), True, lambda slot, u: gath[:, slot * U + u, 0:D], gathered(0))
            bank_mm(Wt[:, W_GIN1, :], bufA, sem("gin_sum"), sem("gin_mm1"))
            bank_mm(Wt[:, W_GIN2, :], bufB, sem("gin_z1"), sem("gin_mm2"))
            turn_rows(w3(bufA), sem("gin_y"), lambda b: b + 1, sem("gin_yT"))

            turn_rows(h, sem("normed"), lambda b: NW + tiles_of(b)[-1] + 1, sem("hT_mm"))
            pe.wait_ge(sem("wq_scaled"), 1)
            for w in range(NW):
                pe.wait_ge(sem("hT_out"), 2 * NB)
                if w >= 7:
                    pe.wait_ge(sem("qkv_out"), w - 6)
                c0 = (w % 7) * BANK
                for i_, s in enumerate((W_Q, W_V, W_K)):
                    i = pe.matmul(ps[:, c0 + i_ * D:c0 + (i_ + 1) * D], hT[:, w * P:(w + 1) * P], Wt[:, s, :], start=True, stop=True)
                i.then_inc(sem("qkv_mm"), 1)

            def turn(g, sl, j):
                pe.wait_ge(sem("a_onehot"), g + 1)
                for u in range(U):
                    i = transpose(ps[:, sl * BANK + u * P:sl * BANK + (u + 1) * P], onehot[:, j, u * P:(u + 1) * P])
                i.then_inc(sem("a_turned"), 1)

            def max_back(g, sl):
                pe.wait_ge(sem("a_scan"), g + 1)
                pe.matmul(ps[:, 6 * BANK:6 * BANK + U * HEADS], seg_max[:, sl, :], ident[0:U * HEADS, 0:U * HEADS], start=True, stop=True).then_inc(sem("a_back"), 1)

            def max_to_nodes(g, j):
                pe.wait_ge(sem("a_last"), g + 1)
                for u in range(U):
                    i = pe.matmul(ps[:, B7 + u * MC:B7 + (u + 1) * MC], onehot[:, j % RING, u * P:(u + 1) * P],
                                  seg_last[:, j % 2, u * MC:(u + 1) * MC], start=True, stop=True)
                i.then_inc(sem("a_max_mm"), 1)

            pe.wait_ge(sem("qkv_out"), NW)
            turn(0, 0, 0)

            def attend(k, j, first):
                g = k * UNROLL + j
                sl = j % 2
                win = windows(k, j)
                pe.wait_ge(sem("a_onehotT"), g + 1)
                if not (first and j == 0):
                    pe.wait_ge(sem("a_prod"), g)
                for u in range(U):
                    i = pe.matmul(ps[:, 2 * BANK + u * D:2 * BANK + (u + 1) * D], onehotT[:, sl, u * P:(u + 1) * P],
                                  qkv[:, bass.DynSlice(win[u] * 3 * D + 2 * D, D)], start=True, stop=True)
                i.then_inc(sem("a_k"), 1)
                turn(g + 1, (j + 1) % 2, (j + 1) % RING)
                if not (first and j == 0):
                    max_back(g - 1, (j - 1) % 2)
                pe.wait_ge(sem("a_score"), g + 1)
                pe.wait_ge(sem("a_start"), g + 1)
                pe.matmul(ps[0:U * HEADS, 4 * BANK:4 * BANK + P], score_now[:, sl, :], ident[:, :], start=True, stop=True)
                pe.matmul(ps[0:U * HEADS, 5 * BANK:5 * BANK + P], start_now[:, sl, :], ident[:, :], start=True, stop=True).then_inc(sem("a_turned_s"), 1)
                if not (first and j == 0):
                    if not (first and j == 1):
                        pe.wait_ge(sem("a_max_out"), g - 1)
                    max_to_nodes(g - 1, (j - 1) % UNROLL)
            over_groups(pe, attend)
            max_back(NG - 1, (NG - 1) % 2)
            pe.wait_ge(sem("a_max_out"), NG - 1)
            max_to_nodes(NG - 1, UNROLL - 1)

            pe.wait_ge(sem("a_max_out"), NG)
            pe.wait_ge(sem("m_ready"), 1)
            clear_sums()

            def turn_c(g, j):
                pe.wait_ge(sem("c_onehot"), g + 1)
                for u in range(U):
                    i = transpose(ps[:, B7 + u * P:B7 + (u + 1) * P], onehot[:, j % RING, u * P:(u + 1) * P])
                i.then_inc(sem("c_turned"), 1)

            def sum_steps(win, j, us):
                for u in us:
                    o = onehot[:, j % RING, u * P:(u + 1) * P]
                    pe.matmul(acc[:, bass.DynSlice(win[u] * P, P)], o, weighted[:, j % 2, u * D:(u + 1) * D], start=False, stop=False, skip_group_check=True)
                    i = pe.matmul(ps[:, bass.DynSlice(win[u] * HEADS + DEN, HEADS)], o, p_exp[:, j % 2, u * HEADS:(u + 1) * HEADS],
                                  start=False, stop=False, skip_group_check=True)
                return i

            turn_c(0, 0)

            def soften(k, j, first):
                g = k * UNROLL + j
                has_last = not (first and j == 0)
                if has_last:
                    win_last = windows_again(j + 1)
                win = windows(k, j)
                pe.wait_ge(sem("c_onehotT"), g + 1)
                for u in range(U):
                    i = pe.matmul(ps[:, B7 + u * HEADS:B7 + (u + 1) * HEADS], onehotT[:, j % 2, u * P:(u + 1) * P],
                                  m_node[:, bass.DynSlice(win[u] * HEADS, HEADS)], start=True, stop=True)
                i.then_inc(sem("c_m"), 1)
                if has_last:
                    pe.wait_ge(sem("c_weighted"), g)
                    sum_steps(win_last, (j - 1) % UNROLL, range(0, U // 2))
                pe.wait_ge(sem("c_d"), g + 1)
                turn_c(g + 1, j + 1)
                if has_last:
                    sum_steps(win_last, (j - 1) % UNROLL, range(U // 2, U)).then_inc(sem("c_summed"), 1)
            over_groups(pe, soften)
            pe.wait_ge(sem("c_weighted"), NG)
            sum_steps(windows_again(UNROLL - 1), UNROLL - 1, range(U)).then_inc(sem("c_summed"), 1)

            turn_rows(w3(bufA), sem("o_all"), lambda b: b + 1, sem("oT_mm"))

            def window_mm(src, slot, ready, done):
                for b in range(NB):
                    pe.wait_ge(ready, b + 1)
                    for w in tiles_of(b):
                        i = pe.matmul(ps[:, w * P:(w + 1) * P], src[:, w * P:(w + 1) * P], Wt[:, slot, :], start=True, stop=True)
                    i.then_inc(done, 1)
            window_mm(bufB, W_O, sem("oT_out"), sem("attn_mm"))
            turn_rows(w3(bufA), sem("x1"), lambda b: b + 1, sem("x1T_mm"))
            pe.wait_ge(sem("x1T_out"), NB)
            for b, (c0, n) in enumerate(BANKS):
                for c in range(HC):
                    i = b * HC + c
                    if i >= 7:
                        pe.wait_ge(sem("ffn1_out"), i - 6)
                    pe.matmul(ps[:, (i % 7) * BANK:(i % 7) * BANK + n], Wt[:, W_F1 + c, :], bufB[:, c0:c0 + n], start=True, stop=True).then_inc(sem("ffn1_mm"), 1)
            pe.wait_ge(sem("ffn1_out"), NB * HC)
            for b in range(NB):
                for w in tiles_of(b):
                    for c in range(HC):
                        src = bufC[:, w * P:(w + 1) * P] if c == HC - 1 else qkv[:, c * NPAD + w * P:c * NPAD + (w + 1) * P]
                        i = pe.matmul(ps[:, w * P:(w + 1) * P], src, Wt[:, W_F2 + c, :], start=c == 0, stop=c == HC - 1)
                i.then_inc(sem("ffn_mm"), 1)

            turn_rows(h, sem("normed"), lambda b: 4 * NW + tiles_of(b)[-1] + 1, sem("hT_mm"))
            pe.wait_ge(sem("hT_out"), 3 * NB)
            for w in range(NW):
                if w >= 4:
                    pe.wait_ge(sem("g2_out"), w - 3)
                    pe.wait_ge(sem("lin_out"), w - 3)
                pe.matmul(ps[:, w % 4 * BANK:w % 4 * BANK + D], hT[:, w * P:(w + 1) * P], Wt[:, W_GCN, :], start=True, stop=True)
                pe.matmul(ps[:, (4 + w % 4) * BANK:(4 + w % 4) * BANK + D], hT[:, w * P:(w + 1) * P], Wt[:, W_LIN, :], start=True, stop=True).then_inc(sem("gcn_mm"), 1)
            pe.wait_ge(sem("g2_out"), NW)
            pe.wait_ge(sem("lin_out"), NW)
            clear_sums()
            sum_groups(2, sem("s2_onehot"), sem("s2_summed"), False, lambda slot, u: gath[:, slot * U + u, 0:D], gathered(2))

            turn_rows(h, sem("normed"), lambda b: 5 * NW + tiles_of(b)[-1] + 1, sem("hT_mm"))
            pe.wait_ge(sem("hT_out"), 4 * NB)
            clear_sums()
            sum_groups(3, sem("e_onehot"), sem("e_summed"), True, lambda slot, u: gath[:, slot * U + u, D:2 * D],
                       lambda k, j: pe.wait_ge(sem("e_relu"), k * UNROLL + j + 1))
            bank_mm(Wt[:, W_E1, :], bufA, sem("gine_sum"), sem("gine_mm"))
            window_mm(bufC, W_E2, sem("gine_bn"), sem("out_mm"))


_INS = ['x', 'src', 'dst', 'edge_attr_128', 'L0_gnn_W1', 'L0_gnn_b1', 'L0_gnn_W2', 'L0_gnn_b2', 'L0_gnn_gamma',
        'L0_gnn_beta', 'L1_gnn_Wq', 'L1_gnn_Wk', 'L1_gnn_Wv', 'L1_gnn_Wo', 'L1_gnn_bo', 'L1_gnn_Wf1', 'L1_gnn_bf1',
        'L1_gnn_Wf2', 'L1_gnn_bf2', 'L1_gnn_g1', 'L1_gnn_b1', 'L1_gnn_g2', 'L1_gnn_b2', 'L2_gnn_W_gcn',
        'L2_gnn_b_gcn', 'L2_gnn_W_lin', 'L2_gnn_b_lin', 'L3_gnn_W1', 'L3_gnn_b1', 'L3_gnn_gamma', 'L3_gnn_beta',
        'L3_gnn_W2', 'L3_gnn_b2']


def kernel(**inputs):
    import numpy as _np
    import concourse.bacc as _bacc
    from concourse.bass_utils import run_bass_kernel_spmd as _run

    nc = _bacc.Bacc("TRN2", target_bir_lowering=False, num_devices=1)
    arrays, t = {}, {}
    for name in _INS:
        a = _np.ascontiguousarray(inputs[name])
        arrays[f"in_{name}"] = a
        t[name] = nc.dram_tensor(f"in_{name}", a.shape, mybir.dt.from_np(a.dtype), kind="ExternalInput").ap()
    out = nc.dram_tensor("out", (N_NODES, D), F32, kind="ExternalOutput").ap()
    gnn_kernel(nc, t, out)
    r = _run(nc, [arrays], core_ids=[0])
    return r.results[0]["out"]
```

```python
from contextlib import ExitStack

import concourse.bass as bass
from concourse import mybir

F32 = mybir.dt.float32
I32 = mybir.dt.int32
BF16 = mybir.dt.bfloat16
ALU = mybir.AluOpType
ACT = mybir.ActivationFunctionType
AX = mybir.AxisListType

P = 128
N_NODES = 3125
N_EDGES = 53125
D = 128
HEADS = 8
HD = D // HEADS
NW = -(-N_NODES // P)
NPAD = NW * P
NT = -(-N_EDGES // P)
LAST_TILE = NT - 1
LAST_ROW = N_EDGES - P
OVERLAP = LAST_TILE * P - LAST_ROW
NS = NT + NW - 1
U = 4
RING = 5
UNROLL = 2 * RING
NG = NS // U
BODIES = NG // UNROLL
assert BODIES * UNROLL * U == NS
NCH = (NT - 1) // P + 1
LASTCH = (NT - 1) - (NCH - 1) * P
CHUNKS = [P] * (NCH - 1) + [LASTCH, 1]
HID = 4 * D
HC = HID // P
LN_EPS = 1e-5
BN_EPS = 1e-5
NONE = -1e30
BANK = 512
BANKS = [(b * BANK, min(BANK, NPAD - b * BANK)) for b in range(-(-NPAD // BANK))]
NB = len(BANKS)
B7 = 7 * BANK
CNT = NPAD
RANGES = P // HEADS
TR = -(-NS // RANGES)
NSP = RANGES * TR
LINE = TR * P
LB = LINE // BANK
BT = BANK // P
assert LB * BANK == LINE and LB <= 7 and UNROLL > LB + 1
SQRT_HD = HD ** 0.5
LAYERS_LN = 53


def gnn_kernel(nc, t, out):
    ctx = ExitStack()
    with ctx:
        def sb(name, shape, dt=F32):
            return ctx.enter_context(nc.sbuf_tensor(name, shape, dt))

        sems = {}

        def sem(name):
            if name not in sems:
                sems[name] = ctx.enter_context(nc.semaphore(name))
            return sems[name]

        h0_rows = nc.dram_tensor("h0_rows", [NPAD, D], F32, kind="Internal").ap()
        qv_rows = nc.dram_tensor("qv_rows", [NPAD, 2 * D], F32, kind="Internal").ap()
        g2_rows = nc.dram_tensor("g2_rows", [NPAD, D], F32, kind="Internal").ap()
        h3_rows = nc.dram_tensor("h3_rows", [NPAD, D], F32, kind="Internal").ap()
        node_count = nc.dram_tensor("node_count", [NPAD, 1], F32, kind="Internal").ap()
        dst_sorted = nc.dram_tensor("dst_sorted", [N_EDGES, 1], I32, kind="Internal").ap()
        src_sorted = nc.dram_tensor("src_sorted", [N_EDGES, 1], I32, kind="Internal").ap()
        order = nc.dram_tensor("order", [N_EDGES, 1], I32, kind="Internal").ap()
        edges_sorted = nc.dram_tensor("edges_sorted", [N_EDGES, D], F32, kind="Internal").ap()
        max_rows = nc.dram_tensor("max_rows", [P * NSP, HEADS], F32, kind="Internal").ap()
        den_rows = nc.dram_tensor("den_rows", [P * NSP, HEADS], F32, kind="Internal").ap()
        v_park = nc.dram_tensor("v_park", [NG * P, U * D], F32, kind="Internal").ap()

        x = sb("x", [P, NW, D])
        h = sb("h", [P, NW, D])
        hT_wide = sb("hT", [P, LINE])
        hT = hT_wide[:, 0:NPAD]
        scratch = sb("scratch", [P, 3 * NPAD])
        bufA, bufB, bufC = (scratch[:, i * NPAD:(i + 1) * NPAD] for i in range(3))
        qkv = sb("qkv", [P, NW * 3 * D])
        qkv3 = qkv[:, :].rearrange("p (w c) -> p w c", w=NW)
        score = sb("score", [P, NSP * HEADS])
        gath = sb("gath", [P, RING * U, 2 * D])
        gath_lo = [gath[:, j * U:(j + 1) * U, 0:D] for j in range(RING)]
        ring = [gath[:, j * U:(j + 1) * U, D:2 * D] for j in range(RING)]
        onehot = sb("onehot", [P, RING, U * P])
        onehotT = hT[:, 0:2 * U * P].rearrange("p (s c) -> p s c", s=2)
        product = hT[:, 2 * U * P:3 * U * P]
        pen = hT_wide[:, 3 * U * P:3 * U * P + LINE // 2 + 1].bitcast(BF16)
        by_slot = hT_wide[:, :]
        line_a, line_b = scratch[:, 0:LINE], scratch[:, LINE:2 * LINE]
        row_at = [2 * LINE]

        def line_row(n=P + 1):
            a = scratch[0:1, row_at[0]:row_at[0] + n]
            row_at[0] += n
            return a

        key_first, key_last, no_start, joined, joined_pen, through, through_pen, back, back_pen, \
            row_in, row_out, row_back, row_carry = (line_row() for _ in range(13))
        upto = scratch[:, row_at[0]:row_at[0] + P]
        key_wide, key_line = scratch[:, 0:LINE], scratch[:, LINE:2 * LINE]
        Wt = sb("Wt", [P, 18, D])
        W_GIN1, W_GIN2, W_Q, W_K, W_V, W_O, W_F1, W_F2, W_GCN, W_LIN, W_E1, W_E2 = \
            0, 1, 2, 3, 4, 5, 6, 10, 14, 15, 16, 17
        ROWS = ['L1_gnn_bo', 'L1_gnn_g1', 'L1_gnn_b1', 'L1_gnn_bf2', 'L1_gnn_g2', 'L1_gnn_b2',
                'L2_gnn_b_gcn', 'L2_gnn_b_lin', 'L3_gnn_b2']
        rows_in = scratch[0:1, 2 * NPAD:2 * NPAD + len(ROWS) * D]
        rows = sb("rows", [P, len(ROWS), D])
        COLS = ['L0_gnn_b1', 'L0_gnn_b2', 'L0_gnn_gamma', 'L0_gnn_beta', 'L3_gnn_b1',
                'L3_gnn_gamma', 'L3_gnn_beta']
        cols = sb("cols", [P, len(COLS) + HC])
        col = {n: cols[:, i:i + 1] for i, n in enumerate(COLS)}
        bf1 = [cols[:, len(COLS) + c:len(COLS) + c + 1] for c in range(HC)]
        ident = sb("ident", [P, P])
        ones = sb("ones", [P, P])
        zeros = sb("zeros", [1, BANK])
        iota_node = sb("iota_node", [P, P])
        dloc = sb("dloc", [P, NSP])
        key = sb("key", [P, NSP])
        keep = sb("keep", [P, LINE + 2], BF16)
        line_ends = sb("line_ends", [P, 3])
        carry = sb("carry", [P, 1])
        lane = sb("lane", [P, 1])
        window_no = sb("window_no", [P, NW])
        count = sb("count", [P, NW])
        slot_row = sb("slot_row", [P, NW], I32)
        cum, pos, total, total_cum, late = (sb(n_, [P, NW]) for n_ in ("cum", "pos", "total", "total_cum", "late"))
        last_edge = sb("last_edge", [P, 2, NW], I32)
        m_node3 = sb("m_node", [P, NW, HEADS])
        m_node = m_node3[:, :, :].rearrange("p w e -> p (w e)")
        den3 = sb("den", [P, NW, HEADS])
        den = den3[:, :, :].rearrange("p w e -> p (w e)")
        srcS = sb("srcS", [P, NS + RING * U])
        step_window = sb("step_window", [1, NG, U], I32)
        step_row = sb("step_row", [1, NG, U], I32)
        idx_stage = sb("idx_stage", [P, 2, RING * U], I32)
        stat = sb("stat", [P, NW, 6])
        mv = sb("mv", [P, NW, 2])
        rstd = sb("rstd", [P, NW])
        shift = sb("shift", [P, NW])
        bn = sb("bn", [P, 8])
        score_loop = sb("score_loop", [P, NW, HEADS])
        m_all = sb("m_all", [P, NW * HEADS])
        f_edge = sb("f_edge", [P, NW * HEADS])
        f_loop = sb("f_loop", [P, NW * HEADS])
        dinv = sb("dinv", [P, NW])
        unsorted = sb("unsorted", [1, 1], I32)
        so_rowI, so_row, so_eq, so_part, so_lower, so_upper, so_attr = (gath[:, i, 0:P] for i in range(7))
        so_rowI = so_rowI.bitcast(I32)
        so_dstI, so_srcI, so_updI, so_posI, so_idI, so_ordI = (gath[:, 8, i:i + 1].bitcast(I32) for i in range(6))
        so_dst, so_have, so_low, so_up, so_new, so_pos, so_upd, so_id, so_cnt, so_far = (gath[:, 9, i:i + 1] for i in range(10))
        so_hist, so_cum, so_base = hT[0:1, :], bufA[0:1, :], bufB[0:1, :]

        tq = [0]

        def early(n, rows_=P):
            a = qkv[0:rows_, tq[0]:tq[0] + n]
            tq[0] += n
            return a

        NC5 = len(CHUNKS)
        dstI, srcI = early(NC5 * P).bitcast(I32), early(NC5 * P).bitcast(I32)
        dstT, srcT = (early(NC5 * P).rearrange("p (c j) -> p c j", c=NC5) for _ in range(2))
        last_keys = early(P)
        dstI = dstI.rearrange("p (c j) -> p c j", c=NC5)
        srcI = srcI.rearrange("p (c j) -> p c j", c=NC5)
        sel = early(NC5 * NS).rearrange("p (c s) -> p c s", c=NC5)
        iota_s, tileF, winF, thr, before, fromW = (early(n) for n in (NS, NS, NS, NW - 1, NC5 * (NW - 1), NS))
        before = before.rearrange("p (c w) -> p c w", c=NC5)
        iota_back = early(NS)
        tile_id = early(NC5)
        cntF = early(1)
        rowF = early(NS)
        nextF = gath[:, 14:14 + NCH // 2, :].rearrange("p a (b j) -> p (a b) j", j=P)
        nextI = gath[:, 10:10 + NCH // 2, :].rearrange("p a (b j) -> p (a b) j", j=P).bitcast(I32)
        falls = bufA[:, 0:NC5 * P].rearrange("p (c j) -> p c j", c=NC5)
        falls_sum = early(1)

        ps = ctx.enter_context(nc.psum_tensor("ps", [P, 8 * BANK], F32))
        acc = ps[:, 0:NPAD]

        block = ctx.enter_context(nc.Block())

        def hold(eng, s, value, name):
            eng.wait_ge(s, value)
            eng.sem_inc(sem("held_" + name), 1)

        def tiles_of(b):
            return range(4 * b, min(4 * b + 4, NW))

        def w3(a):
            return a.rearrange("p (w f) -> p w f", f=D)

        def over_groups(eng, body):
            for j in range(UNROLL):
                body(0, j, True)
            with eng.Fori(1, BODIES) as k:
                for j in range(UNROLL):
                    body(k, j, False)

        def slot_uses(k, j):
            return k * (UNROLL // RING) + j // RING + 1

        def all_gathered(phase, k, j):
            return (slot_uses(k, j) + phase * (NG // RING)) * 16 * U

        def load_indices(eng, dst_in, src_in, done):
            full = (NCH - 1) * P
            for src_ap, table in ((dst_in, dstI), (src_in, srcI)):
                eng.dma_start(table[:, 0:NCH - 1, :], src_ap[0:full * P].rearrange("(c p j) -> p c j", p=P, j=P)).then_inc(done, 16)
                eng.dma_start(table[0:LASTCH, NCH - 1, :], src_ap[full * P:(full + LASTCH) * P].rearrange("(p j) -> p j", j=P)).then_inc(done, 16)
                eng.dma_start(table[0:1, NCH, :], src_ap[LAST_ROW:N_EDGES].rearrange("(p j) -> p j", j=P)).then_inc(done, 16)

        INDEX_LOADS = 16 * 6
        FIRST_LOADS = INDEX_LOADS + 16 * 2

        def sort_tiles(eng, half, body):
            with eng.Fori(0, NT - 1) as tile:
                body(tile + half * NT, tile, tile * P, P)
            body((half + 1) * NT - 1, NT - 1, (NT - 1) * P, N_EDGES - (NT - 1) * P)

        STAGES = 2 * BODIES + 1

        @block.sync
        def _(sp):
            load_indices(sp, t['dst'], t['src'], sem("indices_in"))
            full = (NCH - 1) * P
            sp.dma_start(nextI[:, 0:NCH - 1, :], t['dst'][1:full * P + 1].rearrange("(c p j) -> p c j", p=P, j=P)).then_inc(sem("indices_in"), 16)
            sp.dma_start(nextI[0:LASTCH, NCH - 1, :], t['dst'][full * P + 1:(full + LASTCH) * P + 1].rearrange("(p j) -> p j", j=P)).then_inc(sem("indices_in"), 16)
            sp.wait_ge(sem("x_cleared"), 1)
            sp.dma_start(x[:, 0:NW - 1, :],
                         t['x'][0:(NW - 1) * P, :].rearrange("(w p) f -> p w f", p=P)).then_inc(sem("x_in"), 16)
            sp.dma_start(x[0:N_NODES - (NW - 1) * P, NW - 1, :],
                         t['x'][(NW - 1) * P:N_NODES, :]).then_inc(sem("x_in"), 16)
            n_w = 0
            for slot, name in ((W_GIN1, 'L0_gnn_W1'), (W_GIN2, 'L0_gnn_W2'), (W_Q, 'L1_gnn_Wq'), (W_K, 'L1_gnn_Wk'),
                               (W_V, 'L1_gnn_Wv'), (W_O, 'L1_gnn_Wo'), (W_GCN, 'L2_gnn_W_gcn'), (W_LIN, 'L2_gnn_W_lin'),
                               (W_E1, 'L3_gnn_W1'), (W_E2, 'L3_gnn_W2')):
                sp.dma_start(Wt[:, slot, :], t[name]).then_inc(sem("weights_in"), 16)
            sp.dma_start(Wt[:, W_F1:W_F1 + HC, :],
                         t['L1_gnn_Wf1'].rearrange("k (c f) -> k c f", c=HC)).then_inc(sem("weights_in"), 16)
            sp.dma_start(Wt[:, W_F2:W_F2 + HC, :],
                         t['L1_gnn_Wf2'].rearrange("(c k) f -> k c f", c=HC)).then_inc(sem("weights_in"), 16)
            for i, name in enumerate(ROWS):
                sp.dma_start(rows_in[0:1, i * D:(i + 1) * D], t[name].rearrange("(a f) -> a f", a=1)).then_inc(sem("weights_in"), 16)
            for name in COLS:
                sp.dma_start(col[name], t[name].rearrange("(f a) -> f a", a=1)).then_inc(sem("weights_in"), 16)
            for c in range(HC):
                sp.dma_start(bf1[c], t['L1_gnn_bf1'][c * P:(c + 1) * P].rearrange("(f a) -> f a", a=1)).then_inc(sem("weights_in"), 16)

            def store_rows(dram, src3, ready, base, width):
                for c in range(0, NW, 5):
                    sp.wait_ge(ready, base + c + 5)
                    sp.dma_start(dram[c * P:(c + 5) * P, :].rearrange("(w p) f -> p w f", p=P),
                                 src3[:, c:c + 5, 0:width]).then_inc(sem("table_stored"), 16)

            store_rows(h0_rows, h, sem("normed"), 0, D)
            store_rows(qv_rows, qkv3, sem("qkv_out"), 0, 2 * D)

            def park(k, j, first):
                sp.wait_ge(sem(f"gathered{j % RING}"), all_gathered(1, k, j))
                sp.dma_start(v_park[bass.DynSlice((k * UNROLL + j) * P, P), :].rearrange("p (u f) -> p u f", u=U),
                             ring[j % RING]).then_inc(sem(f"parked{j % RING}"), 16)
            over_groups(sp, park)

            for j in range(RING):
                sp.wait_ge(sem(f"parked{j}"), (NG // RING) * 16)

            def unpark(k, j, first):
                if not (first and j < RING):
                    hold(sp, sem("c_summed"), k * UNROLL + j + 1 - RING, "sp")
                sp.dma_start(ring[j % RING], v_park[bass.DynSlice((k * UNROLL + j) * P, P), :].rearrange("p (u f) -> p u f", u=U)).then_inc(sem(f"ring_in{j % RING}"), 16)
            over_groups(sp, unpark)

            store_rows(g2_rows, w3(bufA), sem("g2_out"), 0, D)
            store_rows(h3_rows, h, sem("normed"), 5 * NW, D)

            regs = [sp.alloc_register(f"edge_row{i}") for i in range(U)]

            flag = sp.alloc_register("sp_unsorted")
            sp.wait_ge(sem("flag_ready"), 1)
            sp.load([flag], unsorted[0:1, 0:1])

            def load_edges(k, j, first, attr=None):
                if first and j < RING:
                    hold(sp, sem("c_summed"), NG, "sp")
                else:
                    hold(sp, sem("e_summed"), k * UNROLL + j + 1 - RING, "sp")
                sp.load(regs, step_row[0:1, bass.DynSlice(k * UNROLL + j, 1), :].rearrange("a g u -> a (g u)"))
                for u in range(U):
                    r = sp.snap(regs[u], min_val=0, max_val=LAST_ROW)
                    sp.dma_start(ring[j % RING][:, u, :], attr[bass.DynSlice(r, P), :]).then_inc(sem(f"ring_in{j % RING}"), 16)
            with sp.If_ne(flag, 0):
                over_groups(sp, lambda k, j, first: load_edges(k, j, first, edges_sorted))
            with sp.Else():
                over_groups(sp, lambda k, j, first: load_edges(k, j, first, t['edge_attr_128']))

            for b in range(NB):
                w0, w1 = tiles_of(b)[0], tiles_of(b)[-1] + 1
                sp.wait_ge(sem("final"), b + 1)
                if w1 * P <= N_NODES:
                    sp.dma_start(out[w0 * P:w1 * P, :].rearrange("(w p) f -> p w f", p=P), h[:, w0:w1, :]).then_inc(sem("stored"), 16)
                else:
                    sp.dma_start(out[w0 * P:N_NODES, :], h[0:N_NODES - w0 * P, w0, :]).then_inc(sem("stored"), 16)
            sp.wait_ge(sem("stored"), 16 * NB)

        @block.gpsimd
        def _(pool):
            pool.memset(x[:, NW - 1, :], 0.0).then_inc(sem("x_cleared"), 1)
            pool.memset(ident[:, :], 0.0).then_inc(sem("pool_zero"), 1)
            pool.memset(ones[:, :], 1.0).then_inc(sem("consts"), 1)
            pool.memset(zeros[:, :], 0.0).then_inc(sem("consts"), 1)
            pool.wait_ge(sem("pool_zero"), 1)
            pool.affine_select(out=ident[:, :], in_=ident[:, :], compare_op=ALU.not_equal, fill=1.0, base=0,
                               pattern=[[-1, P]], channel_multiplier=1).then_inc(sem("consts"), 1)
            imp = dict(allow_small_or_imprecise_dtypes=True)
            pool.iota(iota_node[:, :], [[1, P]], base=0, channel_multiplier=0, **imp).then_inc(sem("consts"), 1)
            pool.iota(iota_s, [[1, NS]], base=0, channel_multiplier=0, **imp).then_inc(sem("consts"), 1)
            pool.iota(iota_back[0:NW - 1, :], [[1, NS]], base=-1, channel_multiplier=-1, **imp).then_inc(sem("consts"), 1)
            pool.iota(thr, [[P, NW - 1]], base=P, channel_multiplier=0, **imp).then_inc(sem("consts"), 1)
            pool.iota(tile_id, [[P, NC5]], base=0, channel_multiplier=1, **imp).then_inc(sem("consts"), 1)
            pool.iota(window_no[:, :], [[1, NW]], base=0, channel_multiplier=0, **imp).then_inc(sem("consts"), 1)
            pool.iota(lane[:, :], [[0, 1]], base=0, channel_multiplier=1, **imp).then_inc(sem("consts"), 1)

            def gather(phase, table, width, free_sem, parked=False):
                def body(k, j, first):
                    g = k * UNROLL + j
                    if j % RING == 0:
                        hold(pool, sem("idx_staged"), phase * STAGES + 2 * k + j // RING + 1, "pool")
                    if not (first and j < RING):
                        hold(pool, free_sem, g + 1 - RING, "pool")
                        if parked:
                            hold(pool, sem(f"parked{j % RING}"), (slot_uses(k, j) - 1) * 16, "pool")
                    for u in range(U):
                        i = j % RING * U + u
                        pool.indirect_dma_start(gath[:, i, 0:width], None, table[:, :],
                                                bass.IndirectOffsetOnAxis(ap=idx_stage[:, j // RING, i:i + 1], axis=0)
                                                ).then_inc(sem(f"gathered{j % RING}"), 16)
                over_groups(pool, body)

            def sort_edges():
                def pass_tile(half):
                    def body(nth, tile, row0, n):
                        rows_ = bass.DynSlice(row0, n)
                        pool.dma_start(so_dstI[0:n, :], t['dst'][rows_].rearrange("(p a) -> p a", a=1)).then_inc(sem("so_in"), 16)
                        pool.dma_start(so_srcI[0:n, :], t['src'][rows_].rearrange("(p a) -> p a", a=1)).then_inc(sem("so_in"), 16)
                        pool.dma_start(so_rowI[0:n, 0:n], t['dst'][rows_].partition_broadcast(n)).then_inc(sem("so_in"), 16)
                        hold(pool, sem("so_in"), (nth + 1) * 48, "pool")
                        pool.indirect_dma_start(so_have[0:n, :], None, node_count[:, :], bass.IndirectOffsetOnAxis(ap=so_dstI[0:n, :], axis=0)).then_inc(sem("so_have"), 16)
                        hold(pool, sem("so_ready"), nth + 1, "pool")
                        pool.indirect_dma_start(node_count[:, :], bass.IndirectOffsetOnAxis(ap=so_updI[0:n, :], axis=0), so_new[0:n, :], None,
                                                bounds_check=NPAD - 1, oob_is_err=False).then_inc(sem("so_counted"), 16)
                        if half:
                            for dram, column in ((dst_sorted, so_dstI), (src_sorted, so_srcI), (order, so_idI)):
                                pool.indirect_dma_start(dram[:, :], bass.IndirectOffsetOnAxis(ap=so_posI[0:n, :], axis=0), column[0:n, :], None).then_inc(sem("so_placed"), 16)
                            hold(pool, sem("so_placed"), (tile + 1) * 48, "pool")
                        hold(pool, sem("so_counted"), (nth + 1) * 16, "pool")
                    return body

                counts = node_count.rearrange("(a n) b -> a (n b)", a=1)
                pool.memset(so_hist, 0.0).then_inc(sem("so_zero"), 1)
                hold(pool, sem("so_zero"), 1, "pool")
                pool.dma_start(counts, so_hist).then_inc(sem("so_table"), 16)
                hold(pool, sem("so_table"), 16, "pool")
                sort_tiles(pool, 0, pass_tile(0))
                pool.dma_start(so_hist, counts).then_inc(sem("so_table"), 16)
                hold(pool, sem("so_based"), 1, "pool")
                pool.dma_start(counts, so_base).then_inc(sem("so_table"), 16)
                hold(pool, sem("so_table"), 48, "pool")
                sort_tiles(pool, 1, pass_tile(1))

                def permute(nth, tile, row0, n):
                    rows_ = bass.DynSlice(row0, n)
                    pool.dma_start(so_ordI[0:n, :], order[rows_, :]).then_inc(sem("so_attr"), 16)
                    hold(pool, sem("so_attr"), tile * 48 + 16, "pool")
                    pool.indirect_dma_start(so_attr[0:n, :], None, t['edge_attr_128'][:, :], bass.IndirectOffsetOnAxis(ap=so_ordI[0:n, :], axis=0)).then_inc(sem("so_attr"), 16)
                    hold(pool, sem("so_attr"), tile * 48 + 32, "pool")
                    pool.dma_start(edges_sorted[rows_, :], so_attr[0:n, :]).then_inc(sem("so_attr"), 16)
                    hold(pool, sem("so_attr"), tile * 48 + 48, "pool")
                sort_tiles(pool, 0, permute)
                load_indices(pool, dst_sorted.rearrange("n a -> (n a)"), src_sorted.rearrange("n a -> (n a)"), sem("indices_again"))

            flag = pool.alloc_register("pool_unsorted")
            pool.wait_ge(sem("flag_ready"), 1)
            pool.load([flag], unsorted[0:1, 0:1])
            with pool.If_ne(flag, 0):
                sort_edges()
            with pool.Else():
                pool.sem_inc(sem("indices_again"), INDEX_LOADS)

            pool.wait_ge(sem("step_tables"), 4)
            pool.wait_ge(sem("table_stored"), 5 * 16)
            gather(0, h0_rows, D, sem("s0_summed"))
            pool.wait_ge(sem("table_stored"), 10 * 16)
            gather(1, qv_rows, 2 * D, sem("a_prod"), parked=True)
            def by_node(dram, into, turned, store, picked):
                hold(pool, turned, LB, "pool")
                pool.dma_start(dram.rearrange("(p s) e -> p (s e)", p=P), by_slot).then_inc(store, 16)
                hold(pool, store, 16, "pool")
                for w in range(NW):
                    pool.indirect_dma_start(into[:, w, :], None, dram[:, :],
                                            bass.IndirectOffsetOnAxis(ap=slot_row[:, w:w + 1], axis=0)).then_inc(picked, 16)

            pool.wait_ge(sem("slots_known"), 1)
            by_node(max_rows, m_node3, sem("m_by_slot"), sem("m_stored"), sem("m_picked"))
            by_node(den_rows, den3, sem("den_by_slot"), sem("den_stored"), sem("den_picked"))
            pool.wait_ge(sem("f_ready"), 1)
            pool.tensor_tensor(qkv3[:, :, D:2 * D].rearrange("p w (e d) -> p w e d", d=HD),
                               qkv3[:, :, D:2 * D].rearrange("p w (e d) -> p w e d", d=HD),
                               f_loop[:, :].rearrange("p (w e) -> p w e", e=HEADS).unsqueeze(3).to_broadcast([P, NW, HEADS, HD]),
                               ALU.mult).then_inc(sem("loop_share"), 1)
            pool.wait_ge(sem("table_stored"), 15 * 16)
            gather(2, g2_rows, D, sem("s2_summed"))
            pool.wait_ge(sem("table_stored"), 20 * 16)
            gather(3, h3_rows, D, sem("e_added"))

        @block.vector
        def _(v):
            def ln_stats(i, src3):
                s = sem("ln_v")
                b = i * LAYERS_LN
                for w in range(NW):
                    v.bn_stats(stat[:, w, :], src3[:, w, :]).then_inc(s, 1)
                v.wait_ge(s, b + NW)
                for w in range(NW):
                    v.bn_aggr(mv[:, w, :], stat[:, w, :]).then_inc(s, 1)
                v.wait_ge(s, b + 2 * NW)
                v.tensor_scalar(rstd[:, :], mv[:, :, 1], LN_EPS, None, ALU.add).then_inc(s, 1)
                v.wait_ge(sem("ln_sqrt"), i + 1)
                v.reciprocal(rstd[:, :], rstd[:, :]).then_inc(s, 1)
                v.wait_ge(s, b + 2 * NW + 2)
                v.scalar_tensor_tensor(shift[:, :], mv[:, :, 0], -1.0, rstd[:, :], ALU.mult, ALU.mult).then_inc(s, 1)

            def evacuate(dst, ready, base, done, src=None):
                for b, (c0, n) in enumerate(BANKS):
                    v.wait_ge(ready, base + b + 1)
                    v.tensor_copy(dst[:, c0:c0 + n], ps[:, c0:c0 + n]).then_inc(done, 1)

            def make_onehot(dst, g_expr, done, numbers=iota_node):
                for u in range(U):
                    i = v.tensor_scalar(dst[:, u * P:(u + 1) * P], numbers[:, :],
                                        dloc[:, bass.DynSlice(g_expr * U + u, 1)], None, ALU.is_equal)
                i.then_inc(done, 1)

            def bn_coeffs(z, gamma, beta, s, z_done, z_value):
                v.wait_ge(z_done, z_value)
                for b, (c0, n) in enumerate(BANKS):
                    n = min(n, N_NODES - c0)
                    v.bn_stats(stat[:, b, :], z[:, c0:c0 + n]).then_inc(s, 1)
                v.wait_ge(s, NB)
                v.bn_aggr(bn[:, 0:2], stat[:, 0:NB, :].rearrange("p b c -> p (b c)")).then_inc(s, 1)
                v.wait_ge(s, NB + 1)
                v.tensor_scalar(bn[:, 4:5], bn[:, 1:2], BN_EPS, None, ALU.add).then_inc(s, 1)
                v.wait_ge(sem("bn_sqrt"), 1 if z_done is sem("gin_z2") else 2)
                v.reciprocal(bn[:, 5:6], bn[:, 4:5]).then_inc(s, 1)
                v.wait_ge(s, NB + 3)
                v.tensor_tensor(bn[:, 2:3], bn[:, 5:6], gamma, ALU.mult).then_inc(s, 1)
                v.wait_ge(s, NB + 4)
                v.tensor_tensor(bn[:, 6:7], bn[:, 0:1], bn[:, 2:3], ALU.mult).then_inc(s, 1)
                v.wait_ge(s, NB + 5)
                v.tensor_tensor(bn[:, 3:4], beta, bn[:, 6:7], ALU.subtract).then_inc(s, 1)

            q = sem("pro_v")
            n = [0]

            def step(i):
                n[0] += 1
                i.then_inc(q, 1)

            def settle():
                v.wait_ge(q, n[0])

            v.wait_ge(sem("consts"), 10)
            step(v.memset(dloc[:, NS:NSP], -1.0))
            step(v.memset(key[:, NS:NSP], -2e6))
            step(v.memset(score[:, NS * HEADS:NSP * HEADS], 0.0))
            step(v.memset(srcS[:, NS:NS + RING * U], 0.0))
            v.wait_ge(sem("consts"), 10)
            v.wait_ge(sem("indices_in"), FIRST_LOADS)
            step(v.memset(falls, 0.0))
            for c, k in enumerate(CHUNKS):
                step(v.tensor_copy(dstT[0:k, c, :], dstI[0:k, c, :]))
            for c, k in enumerate(CHUNKS[:NCH]):
                step(v.tensor_copy(nextF[0:k, c, :], nextI[0:k, c, :]))
            settle()
            for c, k in enumerate(CHUNKS[:NCH]):
                step(v.tensor_tensor(falls[0:k, c, :], dstT[0:k, c, :], nextF[0:k, c, :], ALU.is_gt))
            step(v.tensor_tensor(falls[0:1, NCH, 0:P - 1], dstT[0:1, NCH, 0:P - 1], dstT[0:1, NCH, 1:P], ALU.is_gt))
            settle()
            step(v.tensor_reduce(falls_sum, falls.rearrange("p c j -> p (c j)"), AX.X, ALU.add))
            settle()
            v.sem_inc(sem("falls_ready"), 1)
            v.wait_ge(sem("falls_added"), 1)
            v.tensor_copy(unsorted[:, :], ps[0:1, 0:1]).then_inc(sem("flag_ready"), 1)
            v.wait_ge(sem("flag_ready"), 1)
            flag = v.alloc_register("v_unsorted")
            v.load([flag], unsorted[0:1, 0:1])

            def sort_edges():
                z = sem("so_v")
                done = [0]

                def op(i, after):
                    i.then_inc(z, 1)
                    done[0] += 1
                    v.wait_ge(z, after + done[0])

                op(v.tensor_scalar(so_lower, iota_node[:, :], tile_id[:, 0:1], None, ALU.is_lt), 0)
                op(v.tensor_scalar(so_upper, iota_node[:, :], tile_id[:, 0:1], None, ALU.is_gt), 0)
                op(v.tensor_copy(so_far, tile_id[:, 0:1]), 0)
                MASKS, OPS = 3, [16, 18]

                def pass_tile(half):
                    def body(nth, tile, row0, n):
                        at = MASKS + half * (NT * OPS[0] + 2) + tile * OPS[half]
                        done[0] = 0
                        r = slice(0, n)
                        v.wait_ge(sem("so_in"), (nth + 1) * 48)
                        v.wait_ge(z, at)
                        op(v.tensor_copy(so_dst[r, :], so_dstI[r, :]), at)
                        op(v.tensor_copy(so_row[r, 0:n], so_rowI[r, 0:n]), at)
                        op(v.tensor_scalar(so_eq[r, 0:n], so_row[r, 0:n], so_dst[r, :], None, ALU.is_equal), at)
                        op(v.tensor_tensor(so_part[r, 0:n], so_eq[r, 0:n], so_lower[r, 0:n], ALU.mult), at)
                        op(v.tensor_reduce(so_low[r, :], so_part[r, 0:n], AX.X, ALU.add), at)
                        op(v.tensor_tensor(so_part[r, 0:n], so_eq[r, 0:n], so_upper[r, 0:n], ALU.mult), at)
                        op(v.tensor_reduce(so_up[r, :], so_part[r, 0:n], AX.X, ALU.add), at)
                        v.wait_ge(sem("so_have"), (nth + 1) * 16)
                        op(v.tensor_tensor(so_pos[r, :], so_have[r, :], so_low[r, :], ALU.add), at)
                        op(v.tensor_copy(so_posI[r, :], so_pos[r, :]), at)
                        op(v.tensor_tensor(so_cnt[r, :], so_low[r, :], so_up[r, :], ALU.add), at)
                        op(v.tensor_scalar(so_cnt[r, :], so_cnt[r, :], 1.0, None, ALU.add), at)
                        op(v.tensor_tensor(so_new[r, :], so_have[r, :], so_cnt[r, :], ALU.add), at)
                        op(v.tensor_scalar(so_upd[r, :], so_up[r, :], 0.0, None, ALU.is_gt), at)
                        op(v.tensor_scalar(so_upd[r, :], so_upd[r, :], 1e6, None, ALU.mult), at)
                        op(v.tensor_tensor(so_upd[r, :], so_upd[r, :], so_dst[r, :], ALU.add), at)
                        op(v.tensor_copy(so_updI[r, :], so_upd[r, :]), at)
                        if half:
                            op(v.tensor_copy(so_idI[:, :], so_far), at)
                            op(v.tensor_scalar(so_far, so_far, float(P), None, ALU.add), at)
                        assert done[0] == OPS[half]
                        v.sem_inc(sem("so_ready"), 1)
                    return body

                sort_tiles(v, 0, pass_tile(0))
                v.wait_ge(sem("so_table"), 32)
                at = MASKS + NT * OPS[0]
                done[0] = 0
                op(v.tensor_tensor_scan(so_cum, so_hist, so_hist, 0.0, ALU.add, ALU.bypass), at)
                op(v.tensor_tensor(so_base, so_cum, so_hist, ALU.subtract), at)
                v.sem_inc(sem("so_based"), 1)
                sort_tiles(v, 1, pass_tile(1))

            with v.If_ne(flag, 0):
                sort_edges()
            with v.Else():
                v.sem_inc(sem("sort_skipped"), 1)
            v.wait_ge(sem("indices_again"), INDEX_LOADS)
            for c, k in enumerate(CHUNKS):
                step(v.tensor_copy(dstT[0:k, c, :], dstI[0:k, c, :]))
                step(v.tensor_copy(srcT[0:k, c, :], srcI[0:k, c, :]))
            settle()
            step(v.tensor_copy(last_keys[0:1, 0:OVERLAP], dstT[0:1, NCH, OVERLAP - 1:OVERLAP].to_broadcast([1, OVERLAP])))
            step(v.tensor_copy(last_keys[0:1, OVERLAP:P], dstT[0:1, NCH, OVERLAP:P]))
            settle()
            step(v.memset(dstT[0:1, NCH, 0:OVERLAP], -1e6))
            for c, k in enumerate(CHUNKS[:NCH]):
                step(v.tensor_scalar(before[0:k, c, :], thr[0:k, :], dstT[0:k, c, P - 1:P], None, ALU.is_gt))
            settle()
            v.sem_inc(sem("before_ready"), 1)
            v.wait_ge(sem("counts_ready"), 1)
            step(v.tensor_copy(cntF[0:NW - 1, :], ps[0:NW - 1, 0:1]))
            settle()
            step(v.tensor_scalar(fromW[0:NW - 1, :], iota_back[0:NW - 1, :], cntF[0:NW - 1, :], None, ALU.is_ge))
            settle()
            v.sem_inc(sem("reached_ready"), 1)
            v.wait_ge(sem("window_ready"), 1)
            step(v.tensor_copy(winF, ps[:, 2 * BANK:2 * BANK + NS]))
            settle()
            step(v.tensor_tensor(tileF, iota_s, winF, ALU.subtract))
            settle()
            for c in range(NCH):
                step(v.tensor_scalar(sel[:, c, :], tileF, tile_id[:, c:c + 1], None, ALU.is_equal))
            step(v.tensor_scalar(sel[0:1, NCH, :], tileF[0:1, :], float(LAST_TILE), None, ALU.is_equal))
            settle()
            v.sem_inc(sem("select_ready"), 1)
            step(v.tensor_copy(step_window[:, :, :], winF[0:1, :].rearrange("p (g u) -> p g u", u=U)))
            step(v.tensor_scalar(rowF[0:1, :], tileF[0:1, :], float(P), float(LAST_ROW), ALU.mult, ALU.min))
            settle()
            step(v.tensor_copy(step_row[:, :, :], rowF[0:1, :].rearrange("p (g u) -> p g u", u=U)))
            v.wait_ge(sem("selected"), 1)
            v.scalar_tensor_tensor(dloc[:, 0:NS], winF, -float(P), ps[:, 3 * BANK:3 * BANK + NS], ALU.mult, ALU.add).then_inc(sem("step_tables"), 1)
            v.wait_ge(sem("selected"), 2)
            v.tensor_copy(srcS[:, 0:NS], ps[:, 4 * BANK:4 * BANK + NS]).then_inc(sem("step_tables"), 1)
            v.wait_ge(sem("selected"), 3)
            v.scalar_tensor_tensor(key[:, 0:NS], winF, -float(P), ps[:, 5 * BANK:5 * BANK + NS], ALU.mult, ALU.add).then_inc(sem("step_tables"), 1)
            settle()
            v.sem_inc(sem("step_tables"), 1)
            v.wait_ge(sem("weights_in"), 16 * (12 + len(ROWS) + len(COLS) + HC))
            v.tensor_scalar(Wt[:, W_Q, :], Wt[:, W_Q, :], 1.0 / SQRT_HD, None, ALU.mult).then_inc(sem("wq_scaled"), 1)
            v.wait_ge(sem("rows_spread"), 1)
            for i in range(3):
                v.tensor_copy(rows[:, 3 * i:3 * i + 3, :].rearrange("p r f -> p (r f)"), ps[:, i * BANK:i * BANK + 3 * D]).then_inc(sem("rows_ready"), 1)

            v.wait_ge(sem("x_in"), 32)
            ln_stats(0, x)
            evacuate(hT, sem("hT_mm"), 0, sem("hT_out"))

            def find_segments():
                v.wait_ge(sem("key_line"), LB)
                step(v.tensor_tensor(keep[:, 1:LINE], key_line[:, 1:LINE], key_line[:, 0:LINE - 1], ALU.is_equal))
                step(v.memset(keep[:, 0:1], 1.0))
                step(v.memset(keep[:, LINE:LINE + 2], 1.0))
                step(v.tensor_copy(line_ends[:, 0:1], key_line[:, 0:1]))
                step(v.tensor_copy(line_ends[:, 1:2], key_line[:, LINE - 1:LINE]))
                settle()
                v.tensor_reduce(line_ends[:, 2:3], keep[:, 0:LINE], AX.X, ALU.min).then_inc(sem("ends_known"), 1)

            def onehots_for(summed, made, inserted=None):
                def body(k, j, first):
                    if first and j == LB + 1 and inserted:
                        inserted()
                    if not (first and j < RING):
                        hold(v, summed, k * UNROLL + j + 1 - RING, "v")
                    make_onehot(onehot[:, j % RING, :], k * UNROLL + j, made)
                over_groups(v, body)

            onehots_for(sem("s0_summed"), sem("s0_onehot"), find_segments)
            v.wait_ge(sem("s0_summed"), NG)
            v.tensor_copy(count[:, :], ps[:, CNT:CNT + NW]).then_inc(sem("count_out"), 1)
            for b, (c0, w) in enumerate(BANKS):
                v.tensor_tensor(bufA[:, c0:c0 + w], ps[:, c0:c0 + w], hT[:, c0:c0 + w], ALU.add).then_inc(sem("gin_sum"), 1)
            bn_coeffs(bufC, col['L0_gnn_gamma'], col['L0_gnn_beta'], sem("bn0"), sem("gin_z2"), NB)
            for b, (c0, w) in enumerate(BANKS):
                v.wait_ge(sem("gin_bn"), b + 1)
                v.tensor_tensor(bufA[:, c0:c0 + w], bufB[:, c0:c0 + w], hT[:, c0:c0 + w], ALU.add).then_inc(sem("gin_y"), 1)
            for b, (c0, w) in enumerate(BANKS):
                v.wait_ge(sem("gin_yT"), b + 1)
                xs = x[:, tiles_of(b)[0]:tiles_of(b)[-1] + 1, :].rearrange("p w f -> p (w f)")
                v.tensor_tensor(xs, xs, ps[:, c0:c0 + w], ALU.add).then_inc(sem("x_new"), 1)

            v.wait_ge(sem("x_new"), NB)
            ln_stats(1, x)
            evacuate(hT, sem("hT_mm"), NB, sem("hT_out"))
            for w in range(1, NW, 2):
                v.wait_ge(sem("qkv_mm"), w + 1)
                v.wait_ge(sem("qkv_out"), w)
                v.tensor_copy(qkv3[:, w, :], ps[:, (w % 7) * BANK:(w % 7) * BANK + 3 * D]).then_inc(sem("qkv_out"), 1)
            v.wait_ge(sem("qkv_out"), NW)
            v.tensor_tensor(w3(bufC), qkv3[:, :, 0:D], qkv3[:, :, 2 * D:3 * D], ALU.mult).then_inc(sem("loop_v"), 1)
            v.wait_ge(sem("loop_v"), 1)
            v.tensor_reduce(score_loop[:, :, :].rearrange("p w e -> p (w e)"), bufC.rearrange("p (g d) -> p g d", d=HD), AX.X, ALU.add).then_inc(sem("loop_v"), 1)

            def node_slots():
                def op(i):
                    step(i)
                    settle()
                v.wait_ge(sem("count_out"), 1)
                op(v.tensor_scalar(dinv[:, :], count[:, :], 1.0, None, ALU.add))
                v.tensor_scalar(dinv[:, :], dinv[:, :], 1.0, None, ALU.max).then_inc(sem("deg_ready"), 1)
                op(v.tensor_scalar(upto, iota_node[:, :], lane[:, 0:1], None, ALU.is_ge))
                v.sem_inc(sem("upto_ready"), 1)
                v.wait_ge(sem("counted"), 1)
                op(v.tensor_copy(total[:, :], ps[:, B7 + 416:B7 + 416 + NW]))
                op(v.tensor_tensor_scan(total_cum[:, :], total[:, :], total[:, :], 0.0, ALU.add, ALU.bypass))
                op(v.tensor_tensor(total_cum[:, :], total_cum[:, :], total[:, :], ALU.subtract))
                op(v.scalar_tensor_tensor(cum[:, :], ps[:, B7 + 384:B7 + 384 + NW], -1.0, total_cum[:, :], ALU.add, ALU.add))
                op(v.tensor_scalar(cum[:, :], cum[:, :], 0.0, None, ALU.max))
                op(v.tensor_copy(last_edge[:, 0, :], cum[:, :]))
                op(v.tensor_scalar(last_edge[:, 1, :], last_edge[:, 0, :], P - 1, None, ALU.bitwise_and))
                op(v.tensor_copy(pos[:, :], last_edge[:, 1, :]))
                op(v.tensor_tensor(cum[:, :], cum[:, :], pos[:, :], ALU.subtract))
                op(v.tensor_scalar(late[:, :], cum[:, :], float(LAST_TILE * P), float(OVERLAP), ALU.is_ge, ALU.mult))
                op(v.tensor_tensor(pos[:, :], pos[:, :], late[:, :], ALU.add))
                op(v.scalar_tensor_tensor(cum[:, :], cum[:, :], 1.0 / P, window_no[:, :], ALU.mult, ALU.add))
                op(v.scalar_tensor_tensor(cum[:, :], pos[:, :], float(NSP), cum[:, :], ALU.mult, ALU.add))
                op(v.tensor_copy(slot_row[:, :], cum[:, :]))
                v.sem_inc(sem("slots_known"), 1)

            def by_head(row):
                return row[:, 0:P].rearrange("p (r e) -> p e r", e=HEADS)

            def as_heads(row):
                return row.rearrange("p (e r) -> p e r", e=HEADS)

            def line_joints():
                v.wait_ge(sem("counted"), 1)
                for i, row in enumerate((key_first, key_last, no_start)):
                    step(v.tensor_copy(as_heads(row[:, 0:P]), by_head(ps[0:1, B7 + i * P:B7 + (i + 1) * P])))
                step(v.memset(joined, 0.0))
                step(v.memset(back, 0.0))
                settle()
                step(v.tensor_tensor(joined[:, 1:P], key_first[:, 1:P], key_last[:, 0:P - 1], ALU.is_equal))
                settle()
                step(v.tensor_tensor(through[:, 0:P], joined[:, 0:P], no_start[:, 0:P], ALU.mult))
                step(v.tensor_tensor(back[:, 0:P - 1], joined[:, 1:P], no_start[:, 0:P - 1], ALU.mult))
                step(v.tensor_scalar(joined_pen, joined, -NONE, NONE, ALU.mult, ALU.add))
                settle()
                step(v.tensor_scalar(through_pen[:, 0:P], through[:, 0:P], -NONE, NONE, ALU.mult, ALU.add))
                step(v.tensor_scalar(back_pen[:, 0:P], back[:, 0:P], -NONE, NONE, ALU.mult, ALU.add))
                step(v.memset(row_out[:, 0:1], NONE))
                step(v.memset(row_back[:, P:P + 1], NONE))
                step(v.tensor_scalar(pen, keep[:, 0:LINE + 2], -NONE, NONE, ALU.mult, ALU.add))
                settle()

            make_onehot(onehot[:, 0, :], 0, sem("a_onehot"))
            node_slots()
            line_joints()

            def attend(k, j, first):
                g = k * UNROLL + j
                if not (first and j < RING - 1):
                    hold(v, sem("a_turned"), g + 2 - RING, "v")
                make_onehot(onehot[:, (j + 1) % RING, :], g + 1, sem("a_onehot"))
                if not (first and j == 0):
                    v.wait_ge(sem("a_score"), g)
                v.wait_ge(sem(f"gathered{j % RING}"), all_gathered(1, k, j))
                v.wait_ge(sem("a_k"), g + 1)
                k_at = (2 + j % 2) * BANK
                v.tensor_tensor(product.rearrange("p (u f) -> p u f", u=U), ps[:, k_at:k_at + U * D].rearrange("p (u f) -> p u f", u=U),
                                gath_lo[j % RING], ALU.mult).then_inc(sem("a_prod"), 1)
                hold(v, sem("a_prod"), g + 1, "v")
                v.tensor_reduce(score[:, bass.DynSlice(g * U * HEADS, U * HEADS)], product.rearrange("p (g d) -> p g d", d=HD),
                                AX.X, ALU.add).then_inc(sem("a_score"), 1)
            over_groups(v, attend)

            def steps_of(a, b, e=HEADS):
                return a.rearrange("p (r t e) -> p t r e", r=RANGES, e=e)[:, BT * b:BT * (b + 1)]

            def bank_of(a, b):
                return a[:, b * BANK:(b + 1) * BANK].rearrange("p (t r e) -> p t r e", t=BT, e=HEADS)

            step(v.tensor_scalar(key[:, :], dloc[:, :], -1e5, NONE, ALU.is_lt, ALU.mult))
            settle()
            v.wait_ge(sem("a_score"), NG)
            for b in range(LB):
                v.tensor_tensor(bank_of(line_a, b), steps_of(score[:, :], b),
                                steps_of(key[:, :], b, 1).to_broadcast([P, BT, RANGES, HEADS]), ALU.add).then_inc(sem("l_copied"), 1)
            scores = ps[:, 0:LINE]

            def scan_lines(out_, flags, data, initial, op0, op1, done):
                v.tensor_tensor_scan(out_, flags, data, initial, op0, op1).then_inc(done, 1)

            def carry_over(nth, row_scan, row_shift):
                v.wait_ge(sem("row_mm"), nth + 1)
                v.tensor_copy(as_heads(row_in[:, 0:P]), by_head(ps[0:1, B7:B7 + P])).then_inc(sem("row_v"), 1)
                v.wait_ge(sem("row_v"), 3 * nth + 1)
                row_scan().then_inc(sem("row_v"), 1)
                v.wait_ge(sem("row_v"), 3 * nth + 2)
                row_shift(by_head(row_carry)).then_inc(sem("row_v"), 1)
                v.wait_ge(sem("carry_mm"), nth + 1)
                v.tensor_copy(carry[:, :], ps[:, B7 + P:B7 + P + 1]).then_inc(sem("carry_out"), 1)
                v.wait_ge(sem("carry_out"), nth + 1)

            back_pens = pen[:, 1:LINE + 1][:, ::-1]
            v.wait_ge(sem("l_turned"), LB)
            scan_lines(line_a, pen[:, 0:LINE], scores, NONE, ALU.add, ALU.max, sem("l_scan"))
            carry_over(0, lambda: v.tensor_tensor_scan(row_out[:, 1:P + 1], through_pen[:, 0:P], row_in[:, 0:P], NONE, ALU.add, ALU.max),
                       lambda o: v.tensor_tensor(o, as_heads(row_out[:, 0:P]), as_heads(joined_pen[:, 0:P]), ALU.add))
            scan_lines(line_a, pen[:, 0:LINE], scores, carry[:, 0:1], ALU.add, ALU.max, sem("l_scan"))
            v.wait_ge(sem("l_scan"), 2)
            scan_lines(line_b[:, ::-1], back_pens, line_a[:, ::-1], NONE, ALU.add, ALU.max, sem("l_scan"))
            carry_over(1, lambda: v.tensor_tensor_scan(row_back[:, 0:P][:, ::-1], back_pen[:, 0:P][:, ::-1], row_in[:, 0:P][:, ::-1], NONE, ALU.add, ALU.max),
                       lambda o: v.tensor_tensor(o, as_heads(row_back[:, 1:P + 1]), as_heads(joined_pen[:, 1:P + 1]), ALU.add))
            scan_lines(line_b[:, ::-1], back_pens, line_a[:, ::-1], carry[:, 0:1], ALU.add, ALU.max, sem("l_scan"))
            v.wait_ge(sem("l_scan"), 4)
            for b in range(LB):
                c = slice(b * BANK, (b + 1) * BANK)
                v.tensor_tensor(line_a[:, c], ps[:, c], line_b[:, c], ALU.subtract).then_inc(sem("l_less"), 1)
            step(v.memset(row_out[:, 0:1], 0.0))
            v.wait_ge(sem("l_exp"), LB)
            scan_lines(score[:, :], keep[:, 0:LINE], line_a, 0.0, ALU.mult, ALU.add, sem("l_scan"))
            settle()
            carry_over(2, lambda: v.tensor_tensor_scan(row_out[:, 1:P + 1], through[:, 0:P], row_in[:, 0:P], 0.0, ALU.mult, ALU.add),
                       lambda o: v.tensor_tensor(o, as_heads(row_out[:, 0:P]), as_heads(joined[:, 0:P]), ALU.mult))
            v.wait_ge(sem("m_turned"), LB)
            scan_lines(line_b, keep[:, 0:LINE], line_a, carry[:, 0:1], ALU.mult, ALU.add, sem("l_scan"))
            v.wait_ge(sem("deg_sqrt"), 1)
            v.reciprocal(dinv[:, :], dinv[:, :]).then_inc(sem("dinv_ready"), 1)

            def weigh(k, j, first):
                g = k * UNROLL + j
                if not (first and j < RING):
                    hold(v, sem("c_summed"), g + 1 - RING, "v")
                make_onehot(onehot[:, j % RING, :], g, sem("c_onehot"))
                hold(v, sem(f"ring_in{j % RING}"), slot_uses(k, j) * 16, "v")
                v.tensor_tensor(ring[j % RING].rearrange("p u (e d) -> p u e d", d=HD),
                                ring[j % RING].rearrange("p u (e d) -> p u e d", d=HD),
                                score[:, bass.DynSlice(g * U * HEADS, U * HEADS)].rearrange("p (u e) -> p u e", u=U).unsqueeze(3).to_broadcast([P, U, HEADS, HD]),
                                ALU.mult).then_inc(sem("c_weighted"), 1)
            v.wait_ge(sem("p_by_slot"), LB)
            over_groups(v, weigh)

            v.wait_ge(sem("c_summed"), NG)
            def fac(i):
                step(i)
                settle()
            sl = score_loop[:, :, :].rearrange("p w e -> p (w e)")
            v.wait_ge(sem("loop_v"), 2)
            v.wait_ge(sem("m_picked"), NW * 16)
            fac(v.tensor_scalar(late[:, :], count[:, :], 0.0, NONE, ALU.is_equal, ALU.mult))
            fac(v.tensor_tensor(m_node3[:, :, :], m_node3[:, :, :], late[:, :].unsqueeze(2).to_broadcast([P, NW, HEADS]), ALU.add))
            fac(v.tensor_tensor(m_all[:, :], m_node, sl, ALU.max))
            fac(v.tensor_tensor(f_edge[:, :], m_node, m_all[:, :], ALU.subtract))
            fac(v.tensor_tensor(f_loop[:, :], sl, m_all[:, :], ALU.subtract))
            v.sem_inc(sem("f_args"), 1)
            v.wait_ge(sem("f_exp"), 2)
            v.wait_ge(sem("den_picked"), NW * 16)
            fac(v.tensor_tensor(den, den, f_edge[:, :], ALU.mult))
            fac(v.tensor_tensor(den, den, f_loop[:, :], ALU.add))
            fac(v.tensor_scalar(den, den, 1e-8, None, ALU.add))
            fac(v.reciprocal(den, den))
            v.tensor_tensor(f_loop[:, :], f_loop[:, :], den, ALU.mult).then_inc(sem("f_ready"), 1)
            fac(v.tensor_tensor(f_edge[:, :], f_edge[:, :], den, ALU.mult))
            for b, (c0, n_) in enumerate(BANKS):
                w0, nw = tiles_of(b)[0], len(tiles_of(b))
                v.tensor_tensor(bufA[:, c0:c0 + n_].rearrange("p (g d) -> p g d", d=HD), ps[:, c0:c0 + n_].rearrange("p (g d) -> p g d", d=HD),
                                f_edge[:, w0 * HEADS:(w0 + nw) * HEADS].unsqueeze(2).to_broadcast([P, nw * HEADS, HD]), ALU.mult).then_inc(sem("o_edge"), 1)
            v.wait_ge(sem("rows_ready"), 3)
            v.tensor_tensor(h[:, :, :], h[:, :, :], rows[:, 0:1, :].to_broadcast([P, NW, D]), ALU.add).then_inc(sem("h_bo"), 1)
            v.wait_ge(sem("loop_share"), 1)
            for b, (c0, n_) in enumerate(BANKS):
                w0, w1 = tiles_of(b)[0], tiles_of(b)[-1] + 1
                v.wait_ge(sem("o_edge"), b + 1)
                v.tensor_tensor(w3(bufA)[:, w0:w1, :], w3(bufA)[:, w0:w1, :], qkv3[:, w0:w1, D:2 * D], ALU.add).then_inc(sem("o_all"), 1)
            evacuate(bufB, sem("oT_mm"), 0, sem("oT_out"))
            v.wait_ge(sem("h_bo"), 1)
            for b, (c0, n_) in enumerate(BANKS):
                w0, w1 = tiles_of(b)[0], tiles_of(b)[-1] + 1
                v.wait_ge(sem("attn_mm"), b + 1)
                v.tensor_tensor(w3(bufA)[:, w0:w1, :], h[:, w0:w1, :], w3(ps[:, c0:c0 + n_]), ALU.add).then_inc(sem("r1"), 1)
            v.wait_ge(sem("r1"), NB)
            ln_stats(2, w3(bufA))

            def affine(src, ready, base, g_row, b_row, s, done):
                for b, (c0, n_) in enumerate(BANKS):
                    w0, w1 = tiles_of(b)[0], tiles_of(b)[-1] + 1
                    v.wait_ge(ready, base + w1)
                    a = w3(src)[:, w0:w1, :]
                    v.tensor_tensor(a, a, rows[:, g_row:g_row + 1, :].to_broadcast([P, w1 - w0, D]), ALU.mult).then_inc(s, 1)
                    v.wait_ge(s, b + 1)
                    v.tensor_tensor(a, a, rows[:, b_row:b_row + 1, :].to_broadcast([P, w1 - w0, D]), ALU.add).then_inc(done, 1)
            affine(bufA, sem("normed"), 2 * NW, 1, 2, sem("aff1"), sem("x1"))
            evacuate(bufB, sem("x1T_mm"), 0, sem("x1T_out"))
            v.wait_ge(sem("x1T_out"), NB)
            v.tensor_tensor(w3(bufA), w3(bufA), rows[:, 3:4, :].to_broadcast([P, NW, D]), ALU.add).then_inc(sem("x1_bf2"), 1)
            v.wait_ge(sem("x1_bf2"), 1)
            for b, (c0, n_) in enumerate(BANKS):
                v.wait_ge(sem("ffn_mm"), b + 1)
                v.tensor_tensor(bufB[:, c0:c0 + n_], bufA[:, c0:c0 + n_], ps[:, c0:c0 + n_], ALU.add).then_inc(sem("r2"), 1)
            v.wait_ge(sem("r2"), NB)
            ln_stats(3, w3(bufB))
            affine(bufB, sem("normed"), 3 * NW, 4, 5, sem("aff2"), sem("y1"))
            v.wait_ge(sem("y1"), NB)
            xf = x[:, :, :].rearrange("p w f -> p (w f)")
            v.tensor_tensor(xf, xf, bufB, ALU.add).then_inc(sem("x_new"), 1)

            v.wait_ge(sem("x_new"), NB + 1)
            ln_stats(4, x)
            evacuate(hT, sem("hT_mm"), 2 * NB, sem("hT_out"))
            v.tensor_tensor(rows[:, 6, :], rows[:, 6, :], rows[:, 7, :], ALU.add).then_inc(sem("b_both"), 1)
            v.wait_ge(sem("b_both"), 1)
            for w in range(NW):
                c0 = (4 + w % 4) * BANK
                v.wait_ge(sem("gcn_mm"), w + 1)
                v.tensor_tensor(w3(bufB)[:, w, :], ps[:, c0:c0 + D], rows[:, 6, :], ALU.add).then_inc(sem("lin_out"), 1)
            onehots_for(sem("s2_summed"), sem("s2_onehot"))
            v.wait_ge(sem("s2_summed"), NG)
            for b, (c0, n_) in enumerate(BANKS):
                v.tensor_tensor(bufC[:, c0:c0 + n_], bufA[:, c0:c0 + n_], ps[:, c0:c0 + n_], ALU.add).then_inc(sem("g_sum"), 1)
            for w in range(NW):
                v.wait_ge(sem("g_sum"), w // 4 + 1)
                v.scalar_tensor_tensor(w3(bufC)[:, w, :], w3(bufC)[:, w, :], dinv[:, w:w + 1], w3(bufB)[:, w, :], ALU.mult, ALU.add).then_inc(sem("g_lin"), 1)
            v.wait_ge(sem("g_lin"), NW)
            v.scalar_tensor_tensor(xf, bufC, 0.0, xf, ALU.max, ALU.add).then_inc(sem("x_new"), 1)

            v.wait_ge(sem("x_new"), NB + 2)
            ln_stats(5, x)
            evacuate(hT, sem("hT_mm"), 3 * NB, sem("hT_out"))
            v.tensor_tensor(x[:, :, :], x[:, :, :], rows[:, 8:9, :].to_broadcast([P, NW, D]), ALU.add).then_inc(sem("x_b2"), 1)

            def add_edges(k, j, first):
                g = k * UNROLL + j
                if not (first and j < RING):
                    hold(v, sem("e_summed"), g + 1 - RING, "v")
                make_onehot(onehot[:, j % RING, :], g, sem("e_onehot"))
                v.wait_ge(sem(f"gathered{j % RING}"), all_gathered(3, k, j))
                v.wait_ge(sem(f"ring_in{j % RING}"), (NG // RING) * 16 + slot_uses(k, j) * 16 * U)
                v.tensor_tensor(ring[j % RING], ring[j % RING], gath_lo[j % RING], ALU.add).then_inc(sem("e_added"), 1)
            over_groups(v, add_edges)
            v.wait_ge(sem("e_summed"), NG)
            for b, (c0, w) in enumerate(BANKS):
                v.tensor_tensor(bufA[:, c0:c0 + w], ps[:, c0:c0 + w], hT[:, c0:c0 + w], ALU.add).then_inc(sem("gine_sum"), 1)
            bn_coeffs(bufB, col['L3_gnn_gamma'], col['L3_gnn_beta'], sem("bn3"), sem("gine_z"), NB)
            v.wait_ge(sem("x_b2"), 1)
            for b, (c0, n_) in enumerate(BANKS):
                w0, w1 = tiles_of(b)[0], tiles_of(b)[-1] + 1
                v.wait_ge(sem("out_mm"), b + 1)
                v.tensor_tensor(h[:, w0:w1, :], x[:, w0:w1, :], w3(ps[:, c0:c0 + n_]), ALU.add).then_inc(sem("final"), 1)

        @block.scalar
        def _(a):
            def normalise(i, src3, dst3, func):
                a.wait_ge(sem("ln_v"), i * LAYERS_LN + 2 * NW + 1)
                a.activation(rstd[:, :], rstd[:, :], ACT.Sqrt).then_inc(sem("ln_sqrt"), 1)
                a.wait_ge(sem("ln_v"), (i + 1) * LAYERS_LN)
                for w in range(NW):
                    a.activation(dst3[:, w, :], src3[:, w, :], func, bias=shift[:, w:w + 1], scale=rstd[:, w:w + 1]).then_inc(sem("normed"), 1)

            def bank_act(dst, ready, done, func, **kw):
                for b, (c0, n) in enumerate(BANKS):
                    a.wait_ge(ready, b + 1)
                    a.activation(dst[:, c0:c0 + n], ps[:, c0:c0 + n], func, **kw).then_inc(done, 1)

            def bn_apply(src, dst, s, done):
                a.wait_ge(s, NB + 2)
                a.activation(bn[:, 4:5], bn[:, 4:5], ACT.Sqrt).then_inc(sem("bn_sqrt"), 1)
                a.wait_ge(s, NB + 6)
                for b, (c0, n) in enumerate(BANKS):
                    a.activation(dst[:, c0:c0 + n], src[:, c0:c0 + n], ACT.Identity, bias=bn[:, 3:4], scale=bn[:, 2:3]).then_inc(done, 1)

            def stage(half, first_col, used, value):
                if value is not None:
                    hold(a, used, value, "a")
                a.activation(idx_stage[:, half, :], srcS[:, first_col], ACT.Copy).then_inc(sem("idx_staged"), 1)

            def stage_in(k, j, first, used):
                if j == 0:
                    stage(1, bass.DynSlice(k * UNROLL * U + RING * U, RING * U), used, None if first else k * UNROLL)
                elif j == RING:
                    stage(0, bass.DynSlice(k * UNROLL * U + UNROLL * U, RING * U), used, k * UNROLL + RING)

            def stage_all(used):
                stage(0, slice(0, RING * U), None, None)
                over_groups(a, lambda k, j, first: stage_in(k, j, first, used))

            normalise(0, x, h, ACT.Relu)
            a.wait_ge(sem("step_tables"), 4)
            stage(0, slice(0, RING * U), None, None)
            for b in range(LB):
                a.activation(key_wide[:, b * BANK:(b + 1) * BANK].rearrange("p (t r e) -> p t r e", t=BT, e=HEADS),
                             key[:, :].rearrange("p (r t) -> p t r", r=RANGES)[:, BT * b:BT * (b + 1)].unsqueeze(3).to_broadcast([P, BT, RANGES, HEADS]),
                             ACT.Copy).then_inc(sem("key_wide"), 1)

            def stage_and_turn(k, j, first):
                stage_in(k, j, first, sem("s0_summed"))
                if first and j < LB:
                    a.wait_ge(sem("key_turned"), j + 1)
                    a.activation(key_line[:, j * BANK:(j + 1) * BANK], ps[:, B7:B7 + BANK], ACT.Copy).then_inc(sem("key_line"), 1)
            over_groups(a, stage_and_turn)
            bank_act(bufB, sem("gin_mm1"), sem("gin_z1"), ACT.Relu, bias=col['L0_gnn_b1'])
            bank_act(bufC, sem("gin_mm2"), sem("gin_z2"), ACT.Identity, bias=col['L0_gnn_b2'])
            bn_apply(bufC, bufB, sem("bn0"), sem("gin_bn"))

            normalise(1, x, h, ACT.Relu)
            for w in range(0, NW, 2):
                a.wait_ge(sem("qkv_mm"), w + 1)
                if w:
                    a.wait_ge(sem("qkv_out"), w)
                a.activation(qkv3[:, w, :], ps[:, (w % 7) * BANK:(w % 7) * BANK + 3 * D], ACT.Copy).then_inc(sem("qkv_out"), 1)

            def turn(g, sl):
                a.wait_ge(sem("a_turned"), g + 1)
                a.activation(onehotT[:, sl, :], ps[:, sl * BANK:(sl + 1) * BANK], ACT.Copy).then_inc(sem("a_onehotT"), 1)

            stage(0, slice(0, RING * U), None, None)
            turn(0, 0)

            def attend(k, j, first):
                stage_in(k, j, first, sem("a_prod"))
                turn(k * UNROLL + j + 1, (j + 1) % 2)
            over_groups(a, attend)
            a.wait_ge(sem("deg_ready"), 1)
            a.activation(dinv[:, :], dinv[:, :], ACT.Sqrt).then_inc(sem("deg_sqrt"), 1)

            for b in range(LB):
                c = slice(b * BANK, (b + 1) * BANK)
                a.wait_ge(sem("l_less"), b + 1)
                a.activation(line_a[:, c], line_a[:, c], ACT.Exp).then_inc(sem("l_exp"), 1)

            def back_by_slot(dst, b, at, done):
                a.activation(dst.rearrange("p (r t e) -> p t r e", r=RANGES, e=HEADS)[:, BT * b:BT * (b + 1)],
                             ps[:, at:at + BANK].rearrange("p (t r e) -> p t r e", t=BT, e=HEADS), ACT.Copy).then_inc(done, 1)

            for b in range(LB):
                a.wait_ge(sem("m_turned"), b + 1)
                back_by_slot(by_slot, b, b * BANK, sem("m_by_slot"))
            a.wait_ge(sem("l_scan"), 5)
            for b in range(LB):
                a.wait_ge(sem("p_turned"), b + 1)
                back_by_slot(score[:, :], b, b * BANK, sem("p_by_slot"))
            hold(a, sem("m_stored"), 16, "a")
            for b in range(LB):
                a.wait_ge(sem("den_turned"), b + 1)
                back_by_slot(by_slot, b, B7, sem("den_by_slot"))

            a.wait_ge(sem("f_args"), 1)
            a.activation(f_edge[:, :], f_edge[:, :], ACT.Exp).then_inc(sem("f_exp"), 1)
            a.activation(f_loop[:, :], f_loop[:, :], ACT.Exp).then_inc(sem("f_exp"), 1)

            normalise(2, w3(bufA), w3(bufA), ACT.Identity)
            for b, (c0, n) in enumerate(BANKS):
                for c in range(HC):
                    i = b * HC + c
                    dst = bufC[:, c0:c0 + n] if c == HC - 1 else qkv[:, c * NPAD + c0:c * NPAD + c0 + n]
                    a.wait_ge(sem("ffn1_mm"), i + 1)
                    a.activation(dst, ps[:, (i % 7) * BANK:(i % 7) * BANK + n], ACT.Gelu, bias=bf1[c]).then_inc(sem("ffn1_out"), 1)
            normalise(3, w3(bufB), w3(bufB), ACT.Identity)

            normalise(4, x, h, ACT.Relu)
            for w in range(NW):
                c0 = (w % 4) * BANK
                a.wait_ge(sem("gcn_mm"), w + 1)
                a.activation(w3(bufA)[:, w, :], ps[:, c0:c0 + D], ACT.Copy, scale=dinv[:, w:w + 1]).then_inc(sem("g2_out"), 1)

            stage_all(sem("s2_summed"))

            normalise(5, x, h, ACT.Relu)
            stage(0, slice(0, RING * U), None, None)

            def relu_edges(k, j, first):
                stage_in(k, j, first, sem("e_added"))
                a.wait_ge(sem("e_added"), k * UNROLL + j + 1)
                a.activation(ring[j % RING], ring[j % RING], ACT.Relu).then_inc(sem("e_relu"), 1)
            over_groups(a, relu_edges)
            bank_act(bufB, sem("gine_mm"), sem("gine_z"), ACT.Relu, bias=col['L3_gnn_b1'])
            bn_apply(bufB, bufC, sem("bn3"), sem("gine_bn"))

        @block.tensor
        def _(pe):
            regs = [pe.alloc_register(f"window{i}") for i in range(2 * U)]

            def windows(k, j):
                pe.load(regs[j % 2 * U:(j % 2 + 1) * U], step_window[0:1, bass.DynSlice(k * UNROLL + j, 1), :].rearrange("a g u -> a (g u)"))
                return windows_again(j)

            def windows_again(j):
                return [pe.snap(regs[j % 2 * U + u], min_val=0, max_val=NW - 1) for u in range(U)]

            def transpose(dst, src, **kw):
                return pe.matmul(dst, src, ident[0:src.shape[0], 0:src.shape[0]], start=True, stop=True, is_transpose=True, **kw)

            def turn_rows(src3, ready, value, done, free=None):
                for b, (c0, n) in enumerate(BANKS):
                    pe.wait_ge(ready, value(b))
                    for w in tiles_of(b):
                        i = transpose(ps[:, w * P:(w + 1) * P], src3[:, w, :])
                    i.then_inc(done, 1)

            def clear_sums():
                for b in range(NB):
                    i = pe.matmul(ps[:, b * BANK:(b + 1) * BANK], zeros[:, 0:P], zeros[:, :], start=True, stop=False, skip_group_check=True)
                i.then_inc(sem("cleared"), 1)

            def bank_mm(lhsT, rhs, ready, done):
                for b, (c0, n) in enumerate(BANKS):
                    pe.wait_ge(ready, b + 1)
                    pe.matmul(ps[:, c0:c0 + n], lhsT, rhs[:, c0:c0 + n], start=True, stop=True).then_inc(done, 1)

            pe.wait_ge(sem("consts"), 10)
            pe.wait_ge(sem("falls_ready"), 1)
            pe.matmul(ps[0:1, 0:1], ones[:, 0:1], falls_sum, start=True, stop=True).then_inc(sem("falls_added"), 1)
            pe.wait_ge(sem("before_ready"), 1)
            for c, k in enumerate(CHUNKS[:NCH]):
                i = pe.matmul(ps[0:NW - 1, 0:1], before[0:k, c, :], ones[0:k, 0:1], start=c == 0, stop=c == NCH - 1)
            i.then_inc(sem("counts_ready"), 1)
            pe.wait_ge(sem("reached_ready"), 1)
            pe.matmul(ps[:, 2 * BANK:2 * BANK + NS], ones[0:NW - 1, :], fromW[0:NW - 1, :], start=True, stop=True).then_inc(sem("window_ready"), 1)
            pe.wait_ge(sem("select_ready"), 1)
            for i_, tab in enumerate((dstT, srcT, dstT)):
                for c, k in enumerate(CHUNKS):
                    part = last_keys[0:1, :] if i_ == 2 and c == NCH else tab[0:k, c, :]
                    i = pe.matmul(ps[:, (3 + i_) * BANK:(3 + i_) * BANK + NS], part, sel[0:k, c, :], start=c == 0, stop=c == NC5 - 1)
                i.then_inc(sem("selected"), 1)
            pe.wait_ge(sem("weights_in"), 16 * (12 + len(ROWS) + len(COLS) + HC))
            for i_ in range(3):
                i = pe.matmul(ps[:, i_ * BANK:i_ * BANK + 3 * D], ones[0:1, :], rows_in[0:1, i_ * 3 * D:(i_ + 1) * 3 * D], start=True, stop=True)
            i.then_inc(sem("rows_spread"), 1)

            def sum_groups(phase, onehot_done, summed, by_feature, msg, ready, counts=False, inserted=None):
                def body(k, j, first):
                    g = k * UNROLL + j
                    pe.wait_ge(onehot_done, g + 1)
                    ready(k, j)
                    win = windows(k, j)
                    for u in range(U):
                        o = onehot[:, j % RING, u * P:(u + 1) * P]
                        m = msg(j % RING, u)
                        i = pe.matmul(acc[:, bass.DynSlice(win[u] * P, P)], m if by_feature else o, o if by_feature else m,
                                      start=False, stop=False, skip_group_check=True)
                        if counts:
                            i = pe.matmul(ps[:, bass.DynSlice(win[u] + CNT, 1)], o, ones[:, 0:1], start=False, stop=False, skip_group_check=True)
                    i.then_inc(summed, 1)
                    if first and inserted:
                        inserted(j)
                over_groups(pe, body)

            def turn_bank(src, b, at, done):
                for t_ in range(BT):
                    c = b * BANK + t_ * P
                    i = pe.matmul(ps[:, at + t_ * P:at + (t_ + 1) * P], src[:, c:c + P], ident[:, :], start=True, stop=True)
                i.then_inc(done, 1)

            def turn_keys(j):
                if j < LB:
                    pe.wait_ge(sem("key_wide"), j + 1)
                    if j:
                        pe.wait_ge(sem("key_line"), j)
                    turn_bank(key_wide, j, B7, sem("key_turned"))

            def turn_denominators(j):
                if j < LB:
                    if j == 0:
                        pe.wait_ge(sem("l_scan"), 6)
                    else:
                        pe.wait_ge(sem("den_by_slot"), j)
                    turn_bank(line_b, j, B7, sem("den_turned"))

            def gathered(phase):
                return lambda k, j: pe.wait_ge(sem(f"gathered{j % RING}"), all_gathered(phase, k, j))

            pe.wait_ge(sem("rows_ready"), 3)
            pe.wait_ge(sem("step_tables"), 4)
            turn_rows(h, sem("normed"), lambda b: tiles_of(b)[-1] + 1, sem("hT_mm"))
            pe.wait_ge(sem("hT_out"), NB)
            clear_sums()
            sum_groups(0, sem("s0_onehot"), sem("s0_summed"), True, lambda slot, u: gath[:, slot * U + u, 0:D], gathered(0),
                       counts=True, inserted=turn_keys)
            bank_mm(Wt[:, W_GIN1, :], bufA, sem("gin_sum"), sem("gin_mm1"))
            bank_mm(Wt[:, W_GIN2, :], bufB, sem("gin_z1"), sem("gin_mm2"))
            turn_rows(w3(bufA), sem("gin_y"), lambda b: b + 1, sem("gin_yT"))

            turn_rows(h, sem("normed"), lambda b: NW + tiles_of(b)[-1] + 1, sem("hT_mm"))
            pe.wait_ge(sem("wq_scaled"), 1)
            for w in range(NW):
                pe.wait_ge(sem("hT_out"), 2 * NB)
                if w >= 7:
                    pe.wait_ge(sem("qkv_out"), w - 6)
                c0 = (w % 7) * BANK
                for i_, s in enumerate((W_Q, W_V, W_K)):
                    i = pe.matmul(ps[:, c0 + i_ * D:c0 + (i_ + 1) * D], hT[:, w * P:(w + 1) * P], Wt[:, s, :], start=True, stop=True)
                i.then_inc(sem("qkv_mm"), 1)

            def turn(g, sl, j):
                pe.wait_ge(sem("a_onehot"), g + 1)
                for u in range(U):
                    i = transpose(ps[:, sl * BANK + u * P:sl * BANK + (u + 1) * P], onehot[:, j, u * P:(u + 1) * P])
                i.then_inc(sem("a_turned"), 1)

            pe.wait_ge(sem("ends_known"), 1)
            for i_ in range(3):
                pe.matmul(ps[0:1, B7 + i_ * P:B7 + (i_ + 1) * P], line_ends[:, i_:i_ + 1], ident[:, :], start=True, stop=True)
            pe.wait_ge(sem("upto_ready"), 1)
            pe.matmul(ps[:, B7 + 384:B7 + 384 + NW], upto, count[:, :], start=True, stop=True)
            pe.matmul(ps[:, B7 + 416:B7 + 416 + NW], ones[:, :], count[:, :], start=True, stop=True).then_inc(sem("counted"), 1)
            turn(0, 0, 0)

            def attend(k, j, first):
                g = k * UNROLL + j
                sl = j % 2
                win = windows(k, j)
                pe.wait_ge(sem("a_onehotT"), g + 1)
                if not (first and j < 2):
                    pe.wait_ge(sem("a_prod"), g - 1)
                k_at = (2 + sl) * BANK
                for u in range(U):
                    i = pe.matmul(ps[:, k_at + u * D:k_at + (u + 1) * D], onehotT[:, sl, u * P:(u + 1) * P],
                                  qkv[:, bass.DynSlice(win[u] * 3 * D + 2 * D, D)], start=True, stop=True)
                i.then_inc(sem("a_k"), 1)
                turn(g + 1, (j + 1) % 2, (j + 1) % RING)
            over_groups(pe, attend)

            pe.wait_ge(sem("a_onehotT"), NG + 1)
            for b in range(LB):
                pe.wait_ge(sem("l_copied"), b + 1)
                turn_bank(line_a, b, b * BANK, sem("l_turned"))

            def carry_over(nth, scan, column):
                pe.wait_ge(sem("l_scan"), scan)
                pe.matmul(ps[0:1, B7:B7 + P], column, ident[:, :], start=True, stop=True).then_inc(sem("row_mm"), 1)
                pe.wait_ge(sem("row_v"), 3 * (nth + 1))
                pe.matmul(ps[:, B7 + P:B7 + P + 1], row_carry[:, 0:P], ones[0:1, 0:1], start=True, stop=True).then_inc(sem("carry_mm"), 1)
            carry_over(0, 1, line_a[:, LINE - 1:LINE])
            carry_over(1, 3, line_b[:, 0:1])
            for b in range(LB):
                pe.wait_ge(sem("l_less"), b + 1)
                turn_bank(line_b, b, b * BANK, sem("m_turned"))
            carry_over(2, 5, score[:, LINE - 1:LINE])
            for b in range(LB):
                pe.wait_ge(sem("l_exp"), b + 1)
                pe.wait_ge(sem("m_by_slot"), b + 1)
                turn_bank(line_a, b, b * BANK, sem("p_turned"))

            pe.wait_ge(sem("p_by_slot"), LB)
            clear_sums()
            sum_groups(1, sem("c_onehot"), sem("c_summed"), False, lambda slot, u: gath[:, slot * U + u, D:2 * D],
                       lambda k, j: pe.wait_ge(sem("c_weighted"), k * UNROLL + j + 1), inserted=turn_denominators)

            turn_rows(w3(bufA), sem("o_all"), lambda b: b + 1, sem("oT_mm"))

            def window_mm(src, slot, ready, done):
                for b in range(NB):
                    pe.wait_ge(ready, b + 1)
                    for w in tiles_of(b):
                        i = pe.matmul(ps[:, w * P:(w + 1) * P], src[:, w * P:(w + 1) * P], Wt[:, slot, :], start=True, stop=True)
                    i.then_inc(done, 1)
            window_mm(bufB, W_O, sem("oT_out"), sem("attn_mm"))
            turn_rows(w3(bufA), sem("x1"), lambda b: b + 1, sem("x1T_mm"))
            pe.wait_ge(sem("x1T_out"), NB)
            for b, (c0, n) in enumerate(BANKS):
                for c in range(HC):
                    i = b * HC + c
                    if i >= 7:
                        pe.wait_ge(sem("ffn1_out"), i - 6)
                    pe.matmul(ps[:, (i % 7) * BANK:(i % 7) * BANK + n], Wt[:, W_F1 + c, :], bufB[:, c0:c0 + n], start=True, stop=True).then_inc(sem("ffn1_mm"), 1)
            pe.wait_ge(sem("ffn1_out"), NB * HC)
            for b in range(NB):
                for w in tiles_of(b):
                    for c in range(HC):
                        src = bufC[:, w * P:(w + 1) * P] if c == HC - 1 else qkv[:, c * NPAD + w * P:c * NPAD + (w + 1) * P]
                        i = pe.matmul(ps[:, w * P:(w + 1) * P], src, Wt[:, W_F2 + c, :], start=c == 0, stop=c == HC - 1)
                i.then_inc(sem("ffn_mm"), 1)

            turn_rows(h, sem("normed"), lambda b: 4 * NW + tiles_of(b)[-1] + 1, sem("hT_mm"))
            pe.wait_ge(sem("hT_out"), 3 * NB)
            for w in range(NW):
                if w >= 4:
                    pe.wait_ge(sem("g2_out"), w - 3)
                    pe.wait_ge(sem("lin_out"), w - 3)
                pe.matmul(ps[:, w % 4 * BANK:w % 4 * BANK + D], hT[:, w * P:(w + 1) * P], Wt[:, W_GCN, :], start=True, stop=True)
                pe.matmul(ps[:, (4 + w % 4) * BANK:(4 + w % 4) * BANK + D], hT[:, w * P:(w + 1) * P], Wt[:, W_LIN, :], start=True, stop=True).then_inc(sem("gcn_mm"), 1)
            pe.wait_ge(sem("g2_out"), NW)
            pe.wait_ge(sem("lin_out"), NW)
            clear_sums()
            sum_groups(2, sem("s2_onehot"), sem("s2_summed"), False, lambda slot, u: gath[:, slot * U + u, 0:D], gathered(2))

            turn_rows(h, sem("normed"), lambda b: 5 * NW + tiles_of(b)[-1] + 1, sem("hT_mm"))
            pe.wait_ge(sem("hT_out"), 4 * NB)
            clear_sums()
            sum_groups(3, sem("e_onehot"), sem("e_summed"), True, lambda slot, u: gath[:, slot * U + u, D:2 * D],
                       lambda k, j: pe.wait_ge(sem("e_relu"), k * UNROLL + j + 1))
            bank_mm(Wt[:, W_E1, :], bufA, sem("gine_sum"), sem("gine_mm"))
            window_mm(bufC, W_E2, sem("gine_bn"), sem("out_mm"))


_INS = ['x', 'src', 'dst', 'edge_attr_128', 'L0_gnn_W1', 'L0_gnn_b1', 'L0_gnn_W2', 'L0_gnn_b2', 'L0_gnn_gamma',
        'L0_gnn_beta', 'L1_gnn_Wq', 'L1_gnn_Wk', 'L1_gnn_Wv', 'L1_gnn_Wo', 'L1_gnn_bo', 'L1_gnn_Wf1', 'L1_gnn_bf1',
        'L1_gnn_Wf2', 'L1_gnn_bf2', 'L1_gnn_g1', 'L1_gnn_b1', 'L1_gnn_g2', 'L1_gnn_b2', 'L2_gnn_W_gcn',
        'L2_gnn_b_gcn', 'L2_gnn_W_lin', 'L2_gnn_b_lin', 'L3_gnn_W1', 'L3_gnn_b1', 'L3_gnn_gamma', 'L3_gnn_beta',
        'L3_gnn_W2', 'L3_gnn_b2']


def kernel(**inputs):
    import numpy as _np
    import concourse.bacc as _bacc
    from concourse.bass_utils import run_bass_kernel_spmd as _run

    nc = _bacc.Bacc("TRN2", target_bir_lowering=False, num_devices=1)
    arrays, t = {}, {}
    for name in _INS:
        a = _np.ascontiguousarray(inputs[name])
        arrays[f"in_{name}"] = a
        t[name] = nc.dram_tensor(f"in_{name}", a.shape, mybir.dt.from_np(a.dtype), kind="ExternalInput").ap()
    out = nc.dram_tensor("out", (N_NODES, D), F32, kind="ExternalOutput").ap()
    gnn_kernel(nc, t, out)
    r = _run(nc, [arrays], core_ids=[0])
    return r.results[0]["out"]
```

```python
from contextlib import ExitStack

import concourse.bass as bass
from concourse import mybir

F32 = mybir.dt.float32
I32 = mybir.dt.int32
BF16 = mybir.dt.bfloat16
ALU = mybir.AluOpType
ACT = mybir.ActivationFunctionType
AX = mybir.AxisListType

P = 128
N_NODES = 3125
N_EDGES = 53125
D = 128
HEADS = 8
HD = D // HEADS
NW = -(-N_NODES // P)
NPAD = NW * P
NT = -(-N_EDGES // P)
LAST_TILE = NT - 1
LAST_ROW = N_EDGES - P
OVERLAP = LAST_TILE * P - LAST_ROW
NS = NT + NW - 1
U = 4
RING = 5
UNROLL = 2 * RING
NG = NS // U
BODIES = NG // UNROLL
HALFWAY = BODIES - 3
assert BODIES * UNROLL * U == NS
NCH = (NT - 1) // P + 1
LASTCH = (NT - 1) - (NCH - 1) * P
CHUNKS = [P] * (NCH - 1) + [LASTCH, 1]
HID = 4 * D
HC = HID // P
LN_EPS = 1e-5
BN_EPS = 1e-5
NONE = -1e30
BANK = 512
BANKS = [(b * BANK, min(BANK, NPAD - b * BANK)) for b in range(-(-NPAD // BANK))]
NB = len(BANKS)
B7 = 7 * BANK
CNT = NPAD
RANGES = P // HEADS
TR = -(-NS // RANGES)
NSP = RANGES * TR
LINE = TR * P
LB = LINE // BANK
BT = BANK // P
assert LB * BANK == LINE and LB <= 7 and UNROLL > LB + 1
SQRT_HD = HD ** 0.5
PARTS = [range(0, 2), range(2, 4), range(4, NB)]


def gnn_kernel(nc, t, out):
    ctx = ExitStack()
    with ctx:
        def sb(name, shape, dt=F32):
            return ctx.enter_context(nc.sbuf_tensor(name, shape, dt))

        sems = {}

        def sem(name):
            if name not in sems:
                sems[name] = ctx.enter_context(nc.semaphore(name))
            return sems[name]

        h0_rows = nc.dram_tensor("h0_rows", [NPAD, D], F32, kind="Internal").ap()
        qv_rows = nc.dram_tensor("qv_rows", [NPAD, 2 * D], F32, kind="Internal").ap()
        g2_rows = nc.dram_tensor("g2_rows", [NPAD, D], F32, kind="Internal").ap()
        h3_rows = nc.dram_tensor("h3_rows", [NPAD, D], F32, kind="Internal").ap()
        node_count = nc.dram_tensor("node_count", [NPAD, 1], F32, kind="Internal").ap()
        dst_sorted = nc.dram_tensor("dst_sorted", [N_EDGES, 1], I32, kind="Internal").ap()
        src_sorted = nc.dram_tensor("src_sorted", [N_EDGES, 1], I32, kind="Internal").ap()
        order = nc.dram_tensor("order", [N_EDGES, 1], I32, kind="Internal").ap()
        edges_sorted = nc.dram_tensor("edges_sorted", [N_EDGES, D], F32, kind="Internal").ap()
        max_rows = nc.dram_tensor("max_rows", [P * NSP, HEADS], F32, kind="Internal").ap()
        den_rows = nc.dram_tensor("den_rows", [P * NSP, HEADS], F32, kind="Internal").ap()
        v_park = nc.dram_tensor("v_park", [NG * P, U * D], F32, kind="Internal").ap()

        x = sb("x", [P, NW, D])
        h = sb("h", [P, NW, D])
        hT_wide = sb("hT", [P, LINE])
        hT = hT_wide[:, 0:NPAD]
        scratch = sb("scratch", [P, 3 * NPAD])
        bufA, bufB, bufC = (scratch[:, i * NPAD:(i + 1) * NPAD] for i in range(3))
        qkv = sb("qkv", [P, NW * 3 * D])
        qkv3 = qkv[:, :].rearrange("p (w c) -> p w c", w=NW)
        score = sb("score", [P, NSP * HEADS])
        gath = sb("gath", [P, RING * U, 2 * D])
        gath_lo = [gath[:, j * U:(j + 1) * U, 0:D] for j in range(RING)]
        ring = [gath[:, j * U:(j + 1) * U, D:2 * D] for j in range(RING)]
        values = ring + gath_lo
        onehot = sb("onehot", [P, RING, U * P])
        onehotT = hT[:, 0:2 * U * P].rearrange("p (s c) -> p s c", s=2)
        product = hT[:, 2 * U * P:3 * U * P]
        pen = hT_wide[:, 3 * U * P:3 * U * P + LINE // 2 + 1].bitcast(BF16)
        by_slot = hT_wide[:, :]
        line_a, line_b = scratch[:, 0:LINE], scratch[:, LINE:2 * LINE]
        row_at = [2 * LINE]

        def line_row(n=P + 1):
            a = scratch[0:1, row_at[0]:row_at[0] + n]
            row_at[0] += n
            return a

        key_first, key_last, no_start, joined, joined_pen, through, through_pen, back, back_pen, \
            row_in, row_out, row_back, row_carry = (line_row() for _ in range(13))
        upto = scratch[:, row_at[0]:row_at[0] + P]
        key_wide, key_line = scratch[:, 0:LINE], scratch[:, LINE:2 * LINE]
        Wt = sb("Wt", [P, 18, D])
        W_GIN1, W_GIN2, W_Q, W_K, W_V, W_O, W_F1, W_F2, W_GCN, W_LIN, W_E1, W_E2 = \
            0, 1, 2, 3, 4, 5, 6, 10, 14, 15, 16, 17
        ROWS = ['L1_gnn_bo', 'L1_gnn_g1', 'L1_gnn_b1', 'L1_gnn_bf2', 'L1_gnn_g2', 'L1_gnn_b2',
                'L2_gnn_b_gcn', 'L2_gnn_b_lin', 'L3_gnn_b2']
        rows_in = scratch[0:1, 2 * NPAD:2 * NPAD + len(ROWS) * D]
        rows = sb("rows", [P, len(ROWS), D])
        COLS = ['L0_gnn_b1', 'L0_gnn_b2', 'L0_gnn_gamma', 'L0_gnn_beta', 'L3_gnn_b1',
                'L3_gnn_gamma', 'L3_gnn_beta']
        cols = sb("cols", [P, len(COLS) + HC])
        col = {n: cols[:, i:i + 1] for i, n in enumerate(COLS)}
        bf1 = [cols[:, len(COLS) + c:len(COLS) + c + 1] for c in range(HC)]
        ident = sb("ident", [P, P])
        ones = sb("ones", [P, P])
        zeros = sb("zeros", [1, BANK])
        iota_node = sb("iota_node", [P, P])
        dloc = sb("dloc", [P, NSP])
        key = sb("key", [P, NSP])
        keep = sb("keep", [P, LINE + 2], BF16)
        line_ends = sb("line_ends", [P, 3])
        carry = sb("carry", [P, 1])
        lane = sb("lane", [P, 1])
        window_no = sb("window_no", [P, NW])
        count = sb("count", [P, NW])
        slot_row = sb("slot_row", [P, NW], I32)
        cum, pos, total, total_cum, late = (sb(n_, [P, NW]) for n_ in ("cum", "pos", "total", "total_cum", "late"))
        last_edge = sb("last_edge", [P, 2, NW], I32)
        m_node3 = sb("m_node", [P, NW, HEADS])
        m_node = m_node3[:, :, :].rearrange("p w e -> p (w e)")
        den3 = sb("den", [P, NW, HEADS])
        den = den3[:, :, :].rearrange("p w e -> p (w e)")
        srcS = sb("srcS", [P, NS + RING * U])
        step_columns = sb("step_columns", [1, NG, U], I32)
        step_row = sb("step_row", [1, NG, U], I32)
        idx_stage = sb("idx_stage", [P, 2, RING * U], I32)
        stat = sb("stat", [P, NW, 6])
        mv = sb("mv", [P, NW, 2])
        rstd = sb("rstd", [P, NW])
        shift = sb("shift", [P, NW])
        bn = sb("bn", [P, 8])
        score_loop = sb("score_loop", [P, NW, HEADS])
        m_all = sb("m_all", [P, NW * HEADS])
        f_edge = sb("f_edge", [P, NW * HEADS])
        f_loop = sb("f_loop", [P, NW * HEADS])
        dinv = sb("dinv", [P, NW])
        unsorted = sb("unsorted", [1, 1], I32)
        so_rowI, so_row, so_eq, so_part, so_lower, so_upper, so_attr = (gath[:, i, 0:P] for i in range(7))
        so_rowI = so_rowI.bitcast(I32)
        so_dstI, so_srcI, so_updI, so_posI, so_idI, so_ordI = (gath[:, 8, i:i + 1].bitcast(I32) for i in range(6))
        so_dst, so_have, so_low, so_up, so_new, so_pos, so_upd, so_id, so_cnt, so_far = (gath[:, 9, i:i + 1] for i in range(10))
        so_hist, so_cum, so_base = hT[0:1, :], bufA[0:1, :], bufB[0:1, :]

        tq = [0]

        def early(n, rows_=P):
            a = qkv[0:rows_, tq[0]:tq[0] + n]
            tq[0] += n
            return a

        NC5 = len(CHUNKS)
        dstI, srcI = early(NC5 * P).bitcast(I32), early(NC5 * P).bitcast(I32)
        dstT, srcT = (early(NC5 * P).rearrange("p (c j) -> p c j", c=NC5) for _ in range(2))
        last_keys = early(P)
        dstI = dstI.rearrange("p (c j) -> p c j", c=NC5)
        srcI = srcI.rearrange("p (c j) -> p c j", c=NC5)
        sel = early(NC5 * NS).rearrange("p (c s) -> p c s", c=NC5)
        iota_s, tileF, winF, thr, before, fromW = (early(n) for n in (NS, NS, NS, NW - 1, NC5 * (NW - 1), NS))
        before = before.rearrange("p (c w) -> p c w", c=NC5)
        iota_back = early(NS)
        tile_id = early(NC5)
        cntF = early(1)
        rowF = early(NS)
        nextF = gath[:, 14:14 + NCH // 2, :].rearrange("p a (b j) -> p (a b) j", j=P)
        nextI = gath[:, 10:10 + NCH // 2, :].rearrange("p a (b j) -> p (a b) j", j=P).bitcast(I32)
        falls = bufA[:, 0:NC5 * P].rearrange("p (c j) -> p c j", c=NC5)
        falls_sum = early(1)

        ps = ctx.enter_context(nc.psum_tensor("ps", [P, 8 * BANK], F32))
        acc = ps[:, 0:NPAD]

        block = ctx.enter_context(nc.Block())

        def hold(eng, s, value, name):
            eng.wait_ge(s, value)
            eng.sem_inc(sem("held_" + name), 1)

        def tiles_of(b):
            return range(4 * b, min(4 * b + 4, NW))

        def windows_in(p):
            return range(4 * PARTS[p][0], tiles_of(PARTS[p][-1])[-1] + 1)

        def product_bank(i):
            return (2 + i % 5) * BANK

        def qkv_move(i):
            c = slice(0, 2 * D) if i < NW else slice(2 * D, 3 * D)
            c0 = product_bank(i)
            return qkv3[:, i % NW, c], ps[:, c0:c0 + c.stop - c.start]

        def w3(a):
            return a.rearrange("p (w f) -> p w f", f=D)

        def over_groups(eng, body, halfway=None):
            for j in range(UNROLL):
                body(0, j, True)
            bounds = (1, HALFWAY, BODIES) if halfway else (1, BODIES)
            for lo, hi in zip(bounds, bounds[1:]):
                with eng.Fori(lo, hi) as k:
                    for j in range(UNROLL):
                        body(k, j, False)
                if halfway and hi == HALFWAY:
                    halfway()

        def odd_groups(k, j):
            return (k - 1) * (UNROLL // 2) + j // 2 + 1

        def slot_uses(k, j):
            return k * (UNROLL // RING) + j // RING + 1

        def value_in(j):
            return sem(f"ring_in{j}" if j < RING else f"ring_in_lo{j - RING}")

        def all_gathered(phase, k, j):
            return (slot_uses(k, j) + phase * (NG // RING)) * 16 * U

        def load_indices(eng, dst_in, src_in, done):
            full = (NCH - 1) * P
            for src_ap, table in ((dst_in, dstI), (src_in, srcI)):
                eng.dma_start(table[:, 0:NCH - 1, :], src_ap[0:full * P].rearrange("(c p j) -> p c j", p=P, j=P)).then_inc(done, 16)
                eng.dma_start(table[0:LASTCH, NCH - 1, :], src_ap[full * P:(full + LASTCH) * P].rearrange("(p j) -> p j", j=P)).then_inc(done, 16)
                eng.dma_start(table[0:1, NCH, :], src_ap[LAST_ROW:N_EDGES].rearrange("(p j) -> p j", j=P)).then_inc(done, 16)

        INDEX_LOADS = 16 * 6
        FIRST_LOADS = INDEX_LOADS + 16 * 2

        def sort_tiles(eng, half, body):
            with eng.Fori(0, NT - 1) as tile:
                body(tile + half * NT, tile, tile * P, P)
            body((half + 1) * NT - 1, NT - 1, (NT - 1) * P, N_EDGES - (NT - 1) * P)

        STAGES = 2 * BODIES + 1

        @block.sync
        def _(sp):
            load_indices(sp, t['dst'], t['src'], sem("indices_in"))
            full = (NCH - 1) * P
            sp.dma_start(nextI[:, 0:NCH - 1, :], t['dst'][1:full * P + 1].rearrange("(c p j) -> p c j", p=P, j=P)).then_inc(sem("indices_in"), 16)
            sp.dma_start(nextI[0:LASTCH, NCH - 1, :], t['dst'][full * P + 1:(full + LASTCH) * P + 1].rearrange("(p j) -> p j", j=P)).then_inc(sem("indices_in"), 16)
            sp.wait_ge(sem("x_cleared"), 1)
            sp.dma_start(x[:, 0:NW - 1, :],
                         t['x'][0:(NW - 1) * P, :].rearrange("(w p) f -> p w f", p=P)).then_inc(sem("x_in"), 16)
            sp.dma_start(x[0:N_NODES - (NW - 1) * P, NW - 1, :],
                         t['x'][(NW - 1) * P:N_NODES, :]).then_inc(sem("x_in"), 16)
            for slot, name in ((W_GIN1, 'L0_gnn_W1'), (W_GIN2, 'L0_gnn_W2'), (W_Q, 'L1_gnn_Wq'), (W_K, 'L1_gnn_Wk'),
                               (W_V, 'L1_gnn_Wv'), (W_O, 'L1_gnn_Wo'), (W_GCN, 'L2_gnn_W_gcn'), (W_LIN, 'L2_gnn_W_lin'),
                               (W_E1, 'L3_gnn_W1'), (W_E2, 'L3_gnn_W2')):
                sp.dma_start(Wt[:, slot, :], t[name]).then_inc(sem("weights_in"), 16)
            sp.dma_start(Wt[:, W_F1:W_F1 + HC, :],
                         t['L1_gnn_Wf1'].rearrange("k (c f) -> k c f", c=HC)).then_inc(sem("weights_in"), 16)
            sp.dma_start(Wt[:, W_F2:W_F2 + HC, :],
                         t['L1_gnn_Wf2'].rearrange("(c k) f -> k c f", c=HC)).then_inc(sem("weights_in"), 16)
            for i, name in enumerate(ROWS):
                sp.dma_start(rows_in[0:1, i * D:(i + 1) * D], t[name].rearrange("(a f) -> a f", a=1)).then_inc(sem("weights_in"), 16)
            for name in COLS:
                sp.dma_start(col[name], t[name].rearrange("(f a) -> f a", a=1)).then_inc(sem("weights_in"), 16)
            for c in range(HC):
                sp.dma_start(bf1[c], t['L1_gnn_bf1'][c * P:(c + 1) * P].rearrange("(f a) -> f a", a=1)).then_inc(sem("weights_in"), 16)

            def store_rows(dram, src3, ready, base, width):
                for c in range(0, NW, 5):
                    sp.wait_ge(ready, base + c + 5)
                    sp.dma_start(dram[c * P:(c + 5) * P, :].rearrange("(w p) f -> p w f", p=P),
                                 src3[:, c:c + 5, 0:width]).then_inc(sem("table_stored"), 16)

            store_rows(h0_rows, h, sem("normed"), 0, D)
            store_rows(qv_rows, qkv3, sem("qv_out"), 0, 2 * D)

            def park(k, j, first):
                sp.wait_ge(sem(f"gathered{j % RING}"), all_gathered(1, k, j))
                sp.dma_start(v_park[bass.DynSlice((k * UNROLL + j) * P, P), :].rearrange("p (u f) -> p u f", u=U),
                             ring[j % RING]).then_inc(sem(f"parked{j % RING}"), 16)
            over_groups(sp, park)

            for j in range(RING):
                sp.wait_ge(sem(f"parked{j}"), (NG // RING) * 16)

            def unpark(k, j, first):
                if not first:
                    hold(sp, sem("c_summed"), (k - 1) * UNROLL + j + 1, "sp")
                elif j == RING:
                    hold(sp, sem("a_prod"), NG, "sp")
                sp.dma_start(values[j], v_park[bass.DynSlice((k * UNROLL + j) * P, P), :].rearrange("p (u f) -> p u f", u=U)).then_inc(value_in(j), 16)
            over_groups(sp, unpark)

            store_rows(g2_rows, w3(bufA), sem("g2_out"), 0, D)
            store_rows(h3_rows, h, sem("normed"), 5 * NW, D)

            regs = [sp.alloc_register(f"edge_row{i}") for i in range(U)]

            flag = sp.alloc_register("sp_unsorted")
            sp.wait_ge(sem("flag_ready"), 1)
            sp.load([flag], unsorted[0:1, 0:1])

            def load_edges(k, j, first, attr=None):
                if first and j < RING:
                    hold(sp, sem("c_summed"), NG, "sp")
                else:
                    hold(sp, sem("e_summed"), k * UNROLL + j + 1 - RING, "sp")
                sp.load(regs, step_row[0:1, bass.DynSlice(k * UNROLL + j, 1), :].rearrange("a g u -> a (g u)"))
                for u in range(U):
                    r = sp.snap(regs[u], min_val=0, max_val=LAST_ROW)
                    sp.dma_start(ring[j % RING][:, u, :], attr[bass.DynSlice(r, P), :]).then_inc(sem(f"ring_in{j % RING}"), 16)
            with sp.If_ne(flag, 0):
                over_groups(sp, lambda k, j, first: load_edges(k, j, first, edges_sorted))
            with sp.Else():
                over_groups(sp, lambda k, j, first: load_edges(k, j, first, t['edge_attr_128']))

            for b in range(NB):
                w0, w1 = tiles_of(b)[0], tiles_of(b)[-1] + 1
                sp.wait_ge(sem("final"), b + 1)
                if w1 * P <= N_NODES:
                    sp.dma_start(out[w0 * P:w1 * P, :].rearrange("(w p) f -> p w f", p=P), h[:, w0:w1, :]).then_inc(sem("stored"), 16)
                else:
                    sp.dma_start(out[w0 * P:N_NODES, :], h[0:N_NODES - w0 * P, w0, :]).then_inc(sem("stored"), 16)
            sp.wait_ge(sem("stored"), 16 * NB)

        @block.gpsimd
        def _(pool):
            pool.memset(x[:, NW - 1, :], 0.0).then_inc(sem("x_cleared"), 1)
            pool.memset(ident[:, :], 0.0).then_inc(sem("pool_zero"), 1)
            pool.memset(ones[:, :], 1.0).then_inc(sem("consts"), 1)
            pool.memset(zeros[:, :], 0.0).then_inc(sem("consts"), 1)
            pool.wait_ge(sem("pool_zero"), 1)
            pool.affine_select(out=ident[:, :], in_=ident[:, :], compare_op=ALU.not_equal, fill=1.0, base=0,
                               pattern=[[-1, P]], channel_multiplier=1).then_inc(sem("consts"), 1)
            imp = dict(allow_small_or_imprecise_dtypes=True)
            pool.iota(iota_node[:, :], [[1, P]], base=0, channel_multiplier=0, **imp).then_inc(sem("consts"), 1)
            pool.iota(iota_s, [[1, NS]], base=0, channel_multiplier=0, **imp).then_inc(sem("consts"), 1)
            pool.iota(iota_back[0:NW - 1, :], [[1, NS]], base=-1, channel_multiplier=-1, **imp).then_inc(sem("consts"), 1)
            pool.iota(thr, [[P, NW - 1]], base=P, channel_multiplier=0, **imp).then_inc(sem("consts"), 1)
            pool.iota(tile_id, [[P, NC5]], base=0, channel_multiplier=1, **imp).then_inc(sem("consts"), 1)
            pool.iota(window_no[:, :], [[1, NW]], base=0, channel_multiplier=0, **imp).then_inc(sem("consts"), 1)
            pool.iota(lane[:, :], [[0, 1]], base=0, channel_multiplier=1, **imp).then_inc(sem("consts"), 1)

            def gather(phase, table, width, free_sem, parked=False):
                def body(k, j, first):
                    g = k * UNROLL + j
                    if j % RING == 0:
                        hold(pool, sem("idx_staged"), phase * STAGES + 2 * k + j // RING + 1, "pool")
                    if not (first and j < RING):
                        hold(pool, free_sem, g + 1 - RING, "pool")
                        if parked:
                            hold(pool, sem(f"parked{j % RING}"), (slot_uses(k, j) - 1) * 16, "pool")
                    for u in range(U):
                        i = j % RING * U + u
                        pool.indirect_dma_start(gath[:, i, 0:width], None, table[:, :],
                                                bass.IndirectOffsetOnAxis(ap=idx_stage[:, j // RING, i:i + 1], axis=0)
                                                ).then_inc(sem(f"gathered{j % RING}"), 16)
                over_groups(pool, body)

            def sort_edges():
                def pass_tile(half):
                    def body(nth, tile, row0, n):
                        rows_ = bass.DynSlice(row0, n)
                        pool.dma_start(so_dstI[0:n, :], t['dst'][rows_].rearrange("(p a) -> p a", a=1)).then_inc(sem("so_in"), 16)
                        pool.dma_start(so_srcI[0:n, :], t['src'][rows_].rearrange("(p a) -> p a", a=1)).then_inc(sem("so_in"), 16)
                        pool.dma_start(so_rowI[0:n, 0:n], t['dst'][rows_].partition_broadcast(n)).then_inc(sem("so_in"), 16)
                        hold(pool, sem("so_in"), (nth + 1) * 48, "pool")
                        pool.indirect_dma_start(so_have[0:n, :], None, node_count[:, :], bass.IndirectOffsetOnAxis(ap=so_dstI[0:n, :], axis=0)).then_inc(sem("so_have"), 16)
                        hold(pool, sem("so_ready"), nth + 1, "pool")
                        pool.indirect_dma_start(node_count[:, :], bass.IndirectOffsetOnAxis(ap=so_updI[0:n, :], axis=0), so_new[0:n, :], None,
                                                bounds_check=NPAD - 1, oob_is_err=False).then_inc(sem("so_counted"), 16)
                        if half:
                            for dram, column in ((dst_sorted, so_dstI), (src_sorted, so_srcI), (order, so_idI)):
                                pool.indirect_dma_start(dram[:, :], bass.IndirectOffsetOnAxis(ap=so_posI[0:n, :], axis=0), column[0:n, :], None).then_inc(sem("so_placed"), 16)
                            hold(pool, sem("so_placed"), (tile + 1) * 48, "pool")
                        hold(pool, sem("so_counted"), (nth + 1) * 16, "pool")
                    return body

                counts = node_count.rearrange("(a n) b -> a (n b)", a=1)
                pool.memset(so_hist, 0.0).then_inc(sem("so_zero"), 1)
                hold(pool, sem("so_zero"), 1, "pool")
                pool.dma_start(counts, so_hist).then_inc(sem("so_table"), 16)
                hold(pool, sem("so_table"), 16, "pool")
                sort_tiles(pool, 0, pass_tile(0))
                pool.dma_start(so_hist, counts).then_inc(sem("so_table"), 16)
                hold(pool, sem("so_based"), 1, "pool")
                pool.dma_start(counts, so_base).then_inc(sem("so_table"), 16)
                hold(pool, sem("so_table"), 48, "pool")
                sort_tiles(pool, 1, pass_tile(1))

                def permute(nth, tile, row0, n):
                    rows_ = bass.DynSlice(row0, n)
                    pool.dma_start(so_ordI[0:n, :], order[rows_, :]).then_inc(sem("so_attr"), 16)
                    hold(pool, sem("so_attr"), tile * 48 + 16, "pool")
                    pool.indirect_dma_start(so_attr[0:n, :], None, t['edge_attr_128'][:, :], bass.IndirectOffsetOnAxis(ap=so_ordI[0:n, :], axis=0)).then_inc(sem("so_attr"), 16)
                    hold(pool, sem("so_attr"), tile * 48 + 32, "pool")
                    pool.dma_start(edges_sorted[rows_, :], so_attr[0:n, :]).then_inc(sem("so_attr"), 16)
                    hold(pool, sem("so_attr"), tile * 48 + 48, "pool")
                sort_tiles(pool, 0, permute)
                load_indices(pool, dst_sorted.rearrange("n a -> (n a)"), src_sorted.rearrange("n a -> (n a)"), sem("indices_again"))

            flag = pool.alloc_register("pool_unsorted")
            pool.wait_ge(sem("flag_ready"), 1)
            pool.load([flag], unsorted[0:1, 0:1])
            with pool.If_ne(flag, 0):
                sort_edges()
            with pool.Else():
                pool.sem_inc(sem("indices_again"), INDEX_LOADS)

            pool.wait_ge(sem("step_tables"), 4)
            pool.wait_ge(sem("table_stored"), 5 * 16)
            gather(0, h0_rows, D, sem("s0_summed"))
            pool.wait_ge(sem("table_stored"), 10 * 16)
            gather(1, qv_rows, 2 * D, sem("a_prod"), parked=True)
            def by_node(dram, into, turned, store, picked):
                hold(pool, turned, LB, "pool")
                pool.dma_start(dram.rearrange("(p s) e -> p (s e)", p=P), by_slot).then_inc(store, 16)
                hold(pool, store, 16, "pool")
                for w in range(NW):
                    pool.indirect_dma_start(into[:, w, :], None, dram[:, :],
                                            bass.IndirectOffsetOnAxis(ap=slot_row[:, w:w + 1], axis=0)).then_inc(picked, 16)

            pool.wait_ge(sem("rows_ready"), 3)
            pool.tensor_tensor(h[:, :, :], h[:, :, :], rows[:, 0:1, :].to_broadcast([P, NW, D]), ALU.add).then_inc(sem("biases_in"), 1)
            pool.tensor_tensor(x[:, :, :], x[:, :, :], rows[:, 5:6, :].to_broadcast([P, NW, D]), ALU.add).then_inc(sem("biases_in"), 1)
            pool.wait_ge(sem("slots_known"), 1)
            by_node(max_rows, m_node3, sem("m_by_slot"), sem("m_stored"), sem("m_picked"))
            by_node(den_rows, den3, sem("den_by_slot"), sem("den_stored"), sem("den_picked"))
            pool.wait_ge(sem("f_ready"), 1)
            pool.tensor_tensor(qkv3[:, :, D:2 * D].rearrange("p w (e d) -> p w e d", d=HD),
                               qkv3[:, :, D:2 * D].rearrange("p w (e d) -> p w e d", d=HD),
                               f_loop[:, :].rearrange("p (w e) -> p w e", e=HEADS).unsqueeze(3).to_broadcast([P, NW, HEADS, HD]),
                               ALU.mult).then_inc(sem("loop_share"), 1)
            pool.wait_ge(sem("x1T_mm"), NB)
            pool.tensor_tensor(w3(bufA), w3(bufA), rows[:, 3:4, :].to_broadcast([P, NW, D]), ALU.add).then_inc(sem("x1_bf2"), 1)
            pool.wait_ge(sem("table_stored"), 15 * 16)
            gather(2, g2_rows, D, sem("s2_summed"))
            pool.wait_ge(sem("table_stored"), 20 * 16)
            gather(3, h3_rows, D, sem("e_added"))

        @block.vector
        def _(v):
            q = sem("pro_v")
            n = [0]

            def step(i):
                n[0] += 1
                i.then_inc(q, 1)

            def settle():
                v.wait_ge(q, n[0])

            def ln_part(i, src3, p):
                ws = windows_in(p)
                r = slice(ws[0], ws[-1] + 1)
                for w in ws:
                    step(v.bn_stats(stat[:, w, :], src3[:, w, :]))
                settle()
                for w in ws:
                    step(v.bn_aggr(mv[:, w, :], stat[:, w, :]))
                settle()
                v.tensor_scalar(rstd[:, r], mv[:, r, 1], LN_EPS, None, ALU.add).then_inc(sem("ln_var"), 1)
                v.wait_ge(sem("ln_sqrt"), i * len(PARTS) + p + 1)
                step(v.reciprocal(rstd[:, r], rstd[:, r]))
                settle()
                v.scalar_tensor_tensor(shift[:, r], mv[:, r, 0], -1.0, rstd[:, r], ALU.mult, ALU.mult).then_inc(sem("ln_shift"), 1)

            def ln_stats(i, src3):
                for p in range(len(PARTS)):
                    ln_part(i, src3, p)

            def evacuate(dst, ready, base, done, src=None):
                for b, (c0, n) in enumerate(BANKS):
                    v.wait_ge(ready, base + b + 1)
                    v.tensor_copy(dst[:, c0:c0 + n], ps[:, c0:c0 + n]).then_inc(done, 1)

            def make_onehot(dst, g_expr, done, numbers=iota_node):
                for u in range(U):
                    i = v.tensor_scalar(dst[:, u * P:(u + 1) * P], numbers[:, :],
                                        dloc[:, bass.DynSlice(g_expr * U + u, 1)], None, ALU.is_equal)
                i.then_inc(done, 1)

            def bn_coeffs(z, gamma, beta, s, z_done):
                for b, (c0, n) in enumerate(BANKS):
                    v.wait_ge(z_done, b + 1)
                    n = min(n, N_NODES - c0)
                    v.bn_stats(stat[:, b, :], z[:, c0:c0 + n]).then_inc(s, 1)
                v.wait_ge(s, NB)
                v.bn_aggr(bn[:, 0:2], stat[:, 0:NB, :].rearrange("p b c -> p (b c)")).then_inc(s, 1)
                v.wait_ge(s, NB + 1)
                v.tensor_scalar(bn[:, 4:5], bn[:, 1:2], BN_EPS, None, ALU.add).then_inc(s, 1)
                v.wait_ge(sem("bn_sqrt"), 1 if z_done is sem("gin_z2") else 2)
                v.reciprocal(bn[:, 5:6], bn[:, 4:5]).then_inc(s, 1)
                v.wait_ge(s, NB + 3)
                v.tensor_tensor(bn[:, 2:3], bn[:, 5:6], gamma, ALU.mult).then_inc(s, 1)
                v.wait_ge(s, NB + 4)
                v.tensor_tensor(bn[:, 6:7], bn[:, 0:1], bn[:, 2:3], ALU.mult).then_inc(s, 1)
                v.wait_ge(s, NB + 5)
                v.tensor_tensor(bn[:, 3:4], beta, bn[:, 6:7], ALU.subtract).then_inc(s, 1)

            v.wait_ge(sem("consts"), 10)
            step(v.memset(dloc[:, NS:NSP], -1.0))
            step(v.memset(key[:, NS:NSP], -2e6))
            step(v.memset(score[:, NS * HEADS:NSP * HEADS], 0.0))
            step(v.memset(srcS[:, NS:NS + RING * U], 0.0))
            v.wait_ge(sem("consts"), 10)
            v.wait_ge(sem("indices_in"), FIRST_LOADS)
            step(v.memset(falls, 0.0))
            for c, k in enumerate(CHUNKS):
                step(v.tensor_copy(dstT[0:k, c, :], dstI[0:k, c, :]))
            for c, k in enumerate(CHUNKS[:NCH]):
                step(v.tensor_copy(nextF[0:k, c, :], nextI[0:k, c, :]))
            settle()
            for c, k in enumerate(CHUNKS[:NCH]):
                step(v.tensor_tensor(falls[0:k, c, :], dstT[0:k, c, :], nextF[0:k, c, :], ALU.is_gt))
            step(v.tensor_tensor(falls[0:1, NCH, 0:P - 1], dstT[0:1, NCH, 0:P - 1], dstT[0:1, NCH, 1:P], ALU.is_gt))
            settle()
            step(v.tensor_reduce(falls_sum, falls.rearrange("p c j -> p (c j)"), AX.X, ALU.add))
            settle()
            v.sem_inc(sem("falls_ready"), 1)
            v.wait_ge(sem("falls_added"), 1)
            v.tensor_copy(unsorted[:, :], ps[0:1, 0:1]).then_inc(sem("flag_ready"), 1)
            v.wait_ge(sem("flag_ready"), 1)
            flag = v.alloc_register("v_unsorted")
            v.load([flag], unsorted[0:1, 0:1])

            def sort_edges():
                z = sem("so_v")
                done = [0]

                def op(i, after):
                    i.then_inc(z, 1)
                    done[0] += 1
                    v.wait_ge(z, after + done[0])

                op(v.tensor_scalar(so_lower, iota_node[:, :], tile_id[:, 0:1], None, ALU.is_lt), 0)
                op(v.tensor_scalar(so_upper, iota_node[:, :], tile_id[:, 0:1], None, ALU.is_gt), 0)
                op(v.tensor_copy(so_far, tile_id[:, 0:1]), 0)
                MASKS, OPS = 3, [16, 18]

                def pass_tile(half):
                    def body(nth, tile, row0, n):
                        at = MASKS + half * (NT * OPS[0] + 2) + tile * OPS[half]
                        done[0] = 0
                        r = slice(0, n)
                        v.wait_ge(sem("so_in"), (nth + 1) * 48)
                        v.wait_ge(z, at)
                        op(v.tensor_copy(so_dst[r, :], so_dstI[r, :]), at)
                        op(v.tensor_copy(so_row[r, 0:n], so_rowI[r, 0:n]), at)
                        op(v.tensor_scalar(so_eq[r, 0:n], so_row[r, 0:n], so_dst[r, :], None, ALU.is_equal), at)
                        op(v.tensor_tensor(so_part[r, 0:n], so_eq[r, 0:n], so_lower[r, 0:n], ALU.mult), at)
                        op(v.tensor_reduce(so_low[r, :], so_part[r, 0:n], AX.X, ALU.add), at)
                        op(v.tensor_tensor(so_part[r, 0:n], so_eq[r, 0:n], so_upper[r, 0:n], ALU.mult), at)
                        op(v.tensor_reduce(so_up[r, :], so_part[r, 0:n], AX.X, ALU.add), at)
                        v.wait_ge(sem("so_have"), (nth + 1) * 16)
                        op(v.tensor_tensor(so_pos[r, :], so_have[r, :], so_low[r, :], ALU.add), at)
                        op(v.tensor_copy(so_posI[r, :], so_pos[r, :]), at)
                        op(v.tensor_tensor(so_cnt[r, :], so_low[r, :], so_up[r, :], ALU.add), at)
                        op(v.tensor_scalar(so_cnt[r, :], so_cnt[r, :], 1.0, None, ALU.add), at)
                        op(v.tensor_tensor(so_new[r, :], so_have[r, :], so_cnt[r, :], ALU.add), at)
                        op(v.tensor_scalar(so_upd[r, :], so_up[r, :], 0.0, None, ALU.is_gt), at)
                        op(v.tensor_scalar(so_upd[r, :], so_upd[r, :], 1e6, None, ALU.mult), at)
                        op(v.tensor_tensor(so_upd[r, :], so_upd[r, :], so_dst[r, :], ALU.add), at)
                        op(v.tensor_copy(so_updI[r, :], so_upd[r, :]), at)
                        if half:
                            op(v.tensor_copy(so_idI[:, :], so_far), at)
                            op(v.tensor_scalar(so_far, so_far, float(P), None, ALU.add), at)
                        assert done[0] == OPS[half]
                        v.sem_inc(sem("so_ready"), 1)
                    return body

                sort_tiles(v, 0, pass_tile(0))
                v.wait_ge(sem("so_table"), 32)
                at = MASKS + NT * OPS[0]
                done[0] = 0
                op(v.tensor_tensor_scan(so_cum, so_hist, so_hist, 0.0, ALU.add, ALU.bypass), at)
                op(v.tensor_tensor(so_base, so_cum, so_hist, ALU.subtract), at)
                v.sem_inc(sem("so_based"), 1)
                sort_tiles(v, 1, pass_tile(1))

            with v.If_ne(flag, 0):
                sort_edges()
            with v.Else():
                v.sem_inc(sem("sort_skipped"), 1)
            v.wait_ge(sem("indices_again"), INDEX_LOADS)
            for c, k in enumerate(CHUNKS):
                step(v.tensor_copy(dstT[0:k, c, :], dstI[0:k, c, :]))
                step(v.tensor_copy(srcT[0:k, c, :], srcI[0:k, c, :]))
            settle()
            step(v.memset(last_keys[0:1, :], 0.0))
            settle()
            step(v.tensor_scalar(last_keys[0:1, 0:OVERLAP], dstT[0:1, NCH, OVERLAP - 1:OVERLAP].to_broadcast([1, OVERLAP]), 1e6, None, ALU.add))
            settle()
            step(v.memset(dstT[0:1, NCH, 0:OVERLAP], -1e6))
            for c, k in enumerate(CHUNKS[:NCH]):
                step(v.tensor_scalar(before[0:k, c, :], thr[0:k, :], dstT[0:k, c, P - 1:P], None, ALU.is_gt))
            settle()
            v.sem_inc(sem("before_ready"), 1)
            v.wait_ge(sem("counts_ready"), 1)
            step(v.tensor_copy(cntF[0:NW - 1, :], ps[0:NW - 1, 0:1]))
            settle()
            step(v.tensor_scalar(fromW[0:NW - 1, :], iota_back[0:NW - 1, :], cntF[0:NW - 1, :], None, ALU.is_ge))
            settle()
            v.sem_inc(sem("reached_ready"), 1)
            v.wait_ge(sem("window_ready"), 1)
            step(v.tensor_copy(winF, ps[:, 2 * BANK:2 * BANK + NS]))
            settle()
            step(v.tensor_tensor(tileF, iota_s, winF, ALU.subtract))
            settle()
            for c in range(NCH):
                step(v.tensor_scalar(sel[:, c, :], tileF, tile_id[:, c:c + 1], None, ALU.is_equal))
            step(v.tensor_scalar(sel[0:1, NCH, :], tileF[0:1, :], float(LAST_TILE), None, ALU.is_equal))
            settle()
            v.sem_inc(sem("select_ready"), 1)
            step(v.tensor_scalar(step_columns[:, :, :].rearrange("p g u -> p (g u)"), winF[0:1, :], float(P), None, ALU.mult))
            step(v.tensor_scalar(rowF[0:1, :], tileF[0:1, :], float(P), float(LAST_ROW), ALU.mult, ALU.min))
            settle()
            step(v.tensor_copy(step_row[:, :, :], rowF[0:1, :].rearrange("p (g u) -> p g u", u=U)))
            v.wait_ge(sem("x_in"), 32)
            ln_stats(0, x)
            v.wait_ge(sem("selected"), 1)
            v.scalar_tensor_tensor(dloc[:, 0:NS], winF, -float(P), ps[:, 3 * BANK:3 * BANK + NS], ALU.mult, ALU.add).then_inc(sem("step_tables"), 1)
            v.wait_ge(sem("selected"), 2)
            v.tensor_copy(srcS[:, 0:NS], ps[:, 4 * BANK:4 * BANK + NS]).then_inc(sem("step_tables"), 1)
            v.wait_ge(sem("selected"), 3)
            v.wait_ge(sem("step_tables"), 1)
            v.tensor_tensor(key[:, 0:NS], dloc[:, 0:NS], ps[:, 5 * BANK:5 * BANK + NS], ALU.add).then_inc(sem("step_tables"), 1)
            settle()
            v.sem_inc(sem("step_tables"), 1)
            v.wait_ge(sem("weights_in"), 16 * (12 + len(ROWS) + len(COLS) + HC))
            v.tensor_scalar(Wt[:, W_Q, :], Wt[:, W_Q, :], 1.0 / SQRT_HD, None, ALU.mult).then_inc(sem("wq_scaled"), 1)
            v.wait_ge(sem("rows_spread"), 1)
            for i in range(3):
                v.tensor_copy(rows[:, 3 * i:3 * i + 3, :].rearrange("p r f -> p (r f)"), ps[:, i * BANK:i * BANK + 3 * D]).then_inc(sem("rows_ready"), 1)

            evacuate(hT, sem("hT_mm"), 0, sem("hT_out"))

            def find_segments():
                v.wait_ge(sem("key_line"), LB)
                step(v.tensor_tensor(keep[:, 1:LINE], key_line[:, 1:LINE], key_line[:, 0:LINE - 1], ALU.is_equal))
                step(v.memset(keep[:, 0:1], 1.0))
                step(v.memset(keep[:, LINE:LINE + 2], 1.0))
                step(v.tensor_copy(line_ends[:, 0:1], key_line[:, 0:1]))
                step(v.tensor_copy(line_ends[:, 1:2], key_line[:, LINE - 1:LINE]))
                settle()
                v.tensor_reduce(line_ends[:, 2:3], keep[:, 0:LINE], AX.X, ALU.min).then_inc(sem("ends_known"), 1)

            def onehots_for(summed, made, inserted=None):
                def body(k, j, first):
                    if first and j == LB + 1 and inserted:
                        inserted()
                    if not (first and j < RING):
                        hold(v, summed, k * UNROLL + j + 1 - RING, "v")
                    make_onehot(onehot[:, j % RING, :], k * UNROLL + j, made)
                over_groups(v, body)

            onehots_for(sem("s0_summed"), sem("s0_onehot"), find_segments)
            v.wait_ge(sem("s0_summed"), NG)
            v.tensor_copy(count[:, :], ps[:, CNT:CNT + NW]).then_inc(sem("count_out"), 1)
            for b, (c0, w) in enumerate(BANKS):
                v.tensor_tensor(bufA[:, c0:c0 + w], ps[:, c0:c0 + w], hT[:, c0:c0 + w], ALU.add).then_inc(sem("gin_sum"), 1)
            bn_coeffs(bufC, col['L0_gnn_gamma'], col['L0_gnn_beta'], sem("bn0"), sem("gin_z2"))
            for b, (c0, w) in enumerate(BANKS):
                v.wait_ge(sem("gin_bn"), b + 1)
                v.tensor_tensor(bufA[:, c0:c0 + w], bufB[:, c0:c0 + w], hT[:, c0:c0 + w], ALU.add).then_inc(sem("gin_y"), 1)
            part_ends = [p[-1] for p in PARTS]
            for b, (c0, w) in enumerate(BANKS):
                v.wait_ge(sem("gin_yT"), b + 1)
                xs = x[:, tiles_of(b)[0]:tiles_of(b)[-1] + 1, :].rearrange("p w f -> p (w f)")
                step(v.tensor_tensor(xs, xs, ps[:, c0:c0 + w], ALU.add))
            settle()

            def feed(p, base, move):
                for b in PARTS[p]:
                    c0, n_ = BANKS[b]
                    v.wait_ge(sem("hT_mm"), base + b + 1)
                    v.tensor_copy(hT[:, c0:c0 + n_], ps[:, b % 2 * BANK:b % 2 * BANK + n_]).then_inc(sem("hT_out"), 1)
                    for w in tiles_of(b - 1) if b else ():
                        move(w)
                if b == NB - 1:
                    for w in tiles_of(b):
                        move(w)

            def move_qv(w):
                v.wait_ge(sem("qkv_mm"), w + 1)
                v.tensor_copy(*qkv_move(w)).then_inc(sem("qv_out"), 1)
            for p in range(len(PARTS)):
                ln_part(1, x, p)
                if p:
                    feed(p - 1, NB, move_qv)
            feed(len(PARTS) - 1, NB, move_qv)
            v.wait_ge(sem("k_out"), NW)
            v.wait_ge(sem("qv_out"), NW)
            v.tensor_tensor(w3(bufC), qkv3[:, :, 0:D], qkv3[:, :, 2 * D:3 * D], ALU.mult).then_inc(sem("loop_v"), 1)
            v.wait_ge(sem("loop_v"), 1)
            v.tensor_reduce(score_loop[:, :, :].rearrange("p w e -> p (w e)"), bufC.rearrange("p (g d) -> p g d", d=HD), AX.X, ALU.add).then_inc(sem("loop_v"), 1)

            def node_slots():
                def op(i):
                    step(i)
                    settle()
                v.wait_ge(sem("count_out"), 1)
                op(v.tensor_scalar(dinv[:, :], count[:, :], 1.0, None, ALU.add))
                v.tensor_scalar(dinv[:, :], dinv[:, :], 1.0, None, ALU.max).then_inc(sem("deg_ready"), 1)
                op(v.tensor_scalar(upto, iota_node[:, :], lane[:, 0:1], None, ALU.is_ge))
                v.sem_inc(sem("upto_ready"), 1)
                v.wait_ge(sem("counted"), 1)
                op(v.tensor_copy(total[:, :], ps[:, B7 + 416:B7 + 416 + NW]))
                op(v.tensor_tensor_scan(total_cum[:, :], total[:, :], total[:, :], 0.0, ALU.add, ALU.bypass))
                op(v.tensor_tensor(total_cum[:, :], total_cum[:, :], total[:, :], ALU.subtract))
                op(v.scalar_tensor_tensor(cum[:, :], ps[:, B7 + 384:B7 + 384 + NW], -1.0, total_cum[:, :], ALU.add, ALU.add))
                op(v.tensor_scalar(cum[:, :], cum[:, :], 0.0, None, ALU.max))
                op(v.tensor_copy(last_edge[:, 0, :], cum[:, :]))
                op(v.tensor_scalar(last_edge[:, 1, :], last_edge[:, 0, :], P - 1, None, ALU.bitwise_and))
                op(v.tensor_copy(pos[:, :], last_edge[:, 1, :]))
                op(v.tensor_tensor(cum[:, :], cum[:, :], pos[:, :], ALU.subtract))
                op(v.tensor_scalar(late[:, :], cum[:, :], float(LAST_TILE * P), float(OVERLAP), ALU.is_ge, ALU.mult))
                op(v.tensor_tensor(pos[:, :], pos[:, :], late[:, :], ALU.add))
                op(v.scalar_tensor_tensor(cum[:, :], cum[:, :], 1.0 / P, window_no[:, :], ALU.mult, ALU.add))
                op(v.scalar_tensor_tensor(cum[:, :], pos[:, :], float(NSP), cum[:, :], ALU.mult, ALU.add))
                op(v.tensor_copy(slot_row[:, :], cum[:, :]))
                v.sem_inc(sem("slots_known"), 1)

            def by_head(row):
                return row[:, 0:P].rearrange("p (r e) -> p e r", e=HEADS)

            def as_heads(row):
                return row.rearrange("p (e r) -> p e r", e=HEADS)

            def line_joints():
                v.wait_ge(sem("counted"), 1)
                for i, row in enumerate((key_first, key_last, no_start)):
                    step(v.tensor_copy(as_heads(row[:, 0:P]), by_head(ps[0:1, B7 + i * P:B7 + (i + 1) * P])))
                step(v.memset(joined, 0.0))
                step(v.memset(back, 0.0))
                settle()
                step(v.tensor_tensor(joined[:, 1:P], key_first[:, 1:P], key_last[:, 0:P - 1], ALU.is_equal))
                settle()
                step(v.tensor_tensor(through[:, 0:P], joined[:, 0:P], no_start[:, 0:P], ALU.mult))
                step(v.tensor_tensor(back[:, 0:P - 1], joined[:, 1:P], no_start[:, 0:P - 1], ALU.mult))
                step(v.tensor_scalar(joined_pen, joined, -NONE, NONE, ALU.mult, ALU.add))
                settle()
                step(v.tensor_scalar(through_pen[:, 0:P], through[:, 0:P], -NONE, NONE, ALU.mult, ALU.add))
                step(v.tensor_scalar(back_pen[:, 0:P], back[:, 0:P], -NONE, NONE, ALU.mult, ALU.add))
                step(v.memset(row_out[:, 0:1], NONE))
                step(v.memset(row_back[:, P:P + 1], NONE))
                step(v.tensor_scalar(pen, keep[:, 0:LINE + 2], -NONE, NONE, ALU.mult, ALU.add))
                settle()

            make_onehot(onehot[:, 0, :], 0, sem("a_onehot"))
            node_slots()
            line_joints()

            def attend(k, j, first):
                g = k * UNROLL + j
                if not (first and j < RING - 1):
                    hold(v, sem("a_turned"), g + 2 - RING, "v")
                make_onehot(onehot[:, (j + 1) % RING, :], g + 1, sem("a_onehot"))
                if not (first and j == 0):
                    v.wait_ge(sem("a_score"), g)
                v.wait_ge(sem(f"gathered{j % RING}"), all_gathered(1, k, j))
                v.wait_ge(sem("a_k"), g + 1)
                k_at = (2 + j % 2) * BANK
                v.tensor_tensor(product.rearrange("p (u f) -> p u f", u=U), ps[:, k_at:k_at + U * D].rearrange("p (u f) -> p u f", u=U),
                                gath_lo[j % RING], ALU.mult).then_inc(sem("a_prod"), 1)
                hold(v, sem("a_prod"), g + 1, "v")
                v.tensor_reduce(score[:, bass.DynSlice(g * U * HEADS, U * HEADS)], product.rearrange("p (g d) -> p g d", d=HD),
                                AX.X, ALU.add).then_inc(sem("a_score"), 1)
            over_groups(v, attend)

            def steps_of(a, b, e=HEADS):
                return a.rearrange("p (r t e) -> p t r e", r=RANGES, e=e)[:, BT * b:BT * (b + 1)]

            def bank_of(a, b):
                return a[:, b * BANK:(b + 1) * BANK].rearrange("p (t r e) -> p t r e", t=BT, e=HEADS)

            step(v.tensor_scalar(key[:, :], dloc[:, :], -1e5, NONE, ALU.is_lt, ALU.mult))
            settle()
            v.wait_ge(sem("a_score"), NG)
            for b in range(LB):
                v.tensor_tensor(bank_of(line_a, b), steps_of(score[:, :], b),
                                steps_of(key[:, :], b, 1).to_broadcast([P, BT, RANGES, HEADS]), ALU.add).then_inc(sem("l_copied"), 1)
            scores = ps[:, 0:LINE]

            def scan_lines(out_, flags, data, initial, op0, op1, done):
                v.tensor_tensor_scan(out_, flags, data, initial, op0, op1).then_inc(done, 1)

            def carry_over(nth, row_scan, row_shift):
                v.wait_ge(sem("row_mm"), nth + 1)
                v.tensor_copy(as_heads(row_in[:, 0:P]), by_head(ps[0:1, B7:B7 + P])).then_inc(sem("row_v"), 1)
                v.wait_ge(sem("row_v"), 3 * nth + 1)
                row_scan().then_inc(sem("row_v"), 1)
                v.wait_ge(sem("row_v"), 3 * nth + 2)
                row_shift(by_head(row_carry)).then_inc(sem("row_v"), 1)
                v.wait_ge(sem("carry_mm"), nth + 1)
                v.tensor_copy(carry[:, :], ps[:, B7 + P:B7 + P + 1]).then_inc(sem("carry_out"), 1)
                v.wait_ge(sem("carry_out"), nth + 1)

            back_pens = pen[:, 1:LINE + 1][:, ::-1]
            v.wait_ge(sem("l_turned"), LB)
            scan_lines(line_a, pen[:, 0:LINE], scores, NONE, ALU.add, ALU.max, sem("l_scan"))
            carry_over(0, lambda: v.tensor_tensor_scan(row_out[:, 1:P + 1], through_pen[:, 0:P], row_in[:, 0:P], NONE, ALU.add, ALU.max),
                       lambda o: v.tensor_tensor(o, as_heads(row_out[:, 0:P]), as_heads(joined_pen[:, 0:P]), ALU.add))
            scan_lines(line_a, pen[:, 0:LINE], scores, carry[:, 0:1], ALU.add, ALU.max, sem("l_scan"))
            v.wait_ge(sem("l_scan"), 2)
            scan_lines(line_b[:, ::-1], back_pens, line_a[:, ::-1], NONE, ALU.add, ALU.max, sem("l_scan"))
            carry_over(1, lambda: v.tensor_tensor_scan(row_back[:, 0:P][:, ::-1], back_pen[:, 0:P][:, ::-1], row_in[:, 0:P][:, ::-1], NONE, ALU.add, ALU.max),
                       lambda o: v.tensor_tensor(o, as_heads(row_back[:, 1:P + 1]), as_heads(joined_pen[:, 1:P + 1]), ALU.add))
            scan_lines(line_b[:, ::-1], back_pens, line_a[:, ::-1], carry[:, 0:1], ALU.add, ALU.max, sem("l_scan"))
            v.wait_ge(sem("l_scan"), 4)
            for b in range(LB):
                c = slice(b * BANK, (b + 1) * BANK)
                v.tensor_tensor(line_a[:, c], ps[:, c], line_b[:, c], ALU.subtract).then_inc(sem("l_less"), 1)
            step(v.memset(row_out[:, 0:1], 0.0))
            v.wait_ge(sem("l_exp"), LB)
            scan_lines(score[:, :], keep[:, 0:LINE], line_a, 0.0, ALU.mult, ALU.add, sem("l_scan"))
            settle()
            carry_over(2, lambda: v.tensor_tensor_scan(row_out[:, 1:P + 1], through[:, 0:P], row_in[:, 0:P], 0.0, ALU.mult, ALU.add),
                       lambda o: v.tensor_tensor(o, as_heads(row_out[:, 0:P]), as_heads(joined[:, 0:P]), ALU.mult))
            v.wait_ge(sem("m_turned"), LB)
            scan_lines(line_b, keep[:, 0:LINE], line_a, carry[:, 0:1], ALU.mult, ALU.add, sem("l_scan"))
            v.wait_ge(sem("deg_sqrt"), 1)
            step(v.reciprocal(dinv[:, :], dinv[:, :]))

            def node_factors():
                def fac(i):
                    step(i)
                    settle()
                sl = score_loop[:, :, :].rearrange("p w e -> p (w e)")
                v.wait_ge(sem("loop_v"), 2)
                v.wait_ge(sem("m_picked"), NW * 16)
                fac(v.tensor_scalar(late[:, :], count[:, :], 0.0, NONE, ALU.is_equal, ALU.mult))
                fac(v.tensor_tensor(m_node3[:, :, :], m_node3[:, :, :], late[:, :].unsqueeze(2).to_broadcast([P, NW, HEADS]), ALU.add))
                fac(v.tensor_tensor(m_all[:, :], m_node, sl, ALU.max))
                fac(v.tensor_tensor(f_edge[:, :], m_node, m_all[:, :], ALU.subtract))
                fac(v.tensor_tensor(f_loop[:, :], sl, m_all[:, :], ALU.subtract))
                v.sem_inc(sem("f_args"), 1)
                v.wait_ge(sem("f_exp"), 2)
                v.wait_ge(sem("den_picked"), NW * 16)
                fac(v.tensor_tensor(den, den, f_edge[:, :], ALU.mult))
                fac(v.tensor_tensor(den, den, f_loop[:, :], ALU.add))
                fac(v.tensor_scalar(den, den, 1e-8, None, ALU.add))
                fac(v.reciprocal(den, den))
                v.tensor_tensor(f_loop[:, :], f_loop[:, :], den, ALU.mult).then_inc(sem("f_ready"), 1)
                fac(v.tensor_tensor(f_edge[:, :], f_edge[:, :], den, ALU.mult))

            def weigh(k, j, first):
                g = k * UNROLL + j
                if first or j % 2 == 0:
                    if not (first and j < RING):
                        hold(v, sem("c_summed"), g + 1 - RING, "v")
                    make_onehot(onehot[:, j % RING, :], g, sem("c_onehot"))
                hold(v, value_in(j), (k + 1) * 16, "v")
                v.tensor_tensor(values[j].rearrange("p u (e d) -> p u e d", d=HD),
                                values[j].rearrange("p u (e d) -> p u e d", d=HD),
                                score[:, bass.DynSlice(g * U * HEADS, U * HEADS)].rearrange("p (u e) -> p u e", u=U).unsqueeze(3).to_broadcast([P, U, HEADS, HD]),
                                ALU.mult).then_inc(sem("c_weighted"), 1)
            v.wait_ge(sem("p_by_slot"), LB)
            over_groups(v, weigh, node_factors)

            v.wait_ge(sem("c_summed"), NG)
            v.wait_ge(sem("loop_share"), 1)
            def add_loops(b):
                w0, w1 = tiles_of(b)[0], tiles_of(b)[-1] + 1
                v.wait_ge(sem("o_edge"), b + 1)
                v.tensor_tensor(w3(bufA)[:, w0:w1, :], w3(bufA)[:, w0:w1, :], qkv3[:, w0:w1, D:2 * D], ALU.add).then_inc(sem("o_all"), 1)
            for b, (c0, n_) in enumerate(BANKS):
                w0, nw = tiles_of(b)[0], len(tiles_of(b))
                v.tensor_tensor(bufA[:, c0:c0 + n_].rearrange("p (g d) -> p g d", d=HD), ps[:, c0:c0 + n_].rearrange("p (g d) -> p g d", d=HD),
                                f_edge[:, w0 * HEADS:(w0 + nw) * HEADS].unsqueeze(2).to_broadcast([P, nw * HEADS, HD]), ALU.mult).then_inc(sem("o_edge"), 1)
                if b:
                    add_loops(b - 1)
            add_loops(NB - 1)
            v.wait_ge(sem("biases_in"), 2)
            for b, (c0, n_) in enumerate(BANKS):
                w0, w1 = tiles_of(b)[0], tiles_of(b)[-1] + 1
                v.wait_ge(sem("attn_mm"), b + 1)
                step(v.tensor_tensor(w3(bufA)[:, w0:w1, :], h[:, w0:w1, :], w3(ps[:, c0:c0 + n_]), ALU.add))
                if b in part_ends:
                    settle()
                    ln_part(2, w3(bufA), part_ends.index(b))

            def x1_turned(b):
                c0, n_ = BANKS[b]
                v.wait_ge(sem("x1T_mm"), b + 1)
                v.tensor_copy(bufB[:, c0:c0 + n_], ps[:, b % 2 * BANK:b % 2 * BANK + n_]).then_inc(sem("x1T_out"), 1)
            for b, (c0, n_) in enumerate(BANKS):
                w0, w1 = tiles_of(b)[0], tiles_of(b)[-1] + 1
                v.wait_ge(sem("normed"), 2 * NW + w1)
                a = w3(bufA)[:, w0:w1, :]
                step(v.tensor_tensor(a, a, rows[:, 1:2, :].to_broadcast([P, w1 - w0, D]), ALU.mult))
                settle()
                v.tensor_tensor(a, a, rows[:, 2:3, :].to_broadcast([P, w1 - w0, D]), ALU.add).then_inc(sem("x1"), 1)
                if b:
                    x1_turned(b - 1)
            x1_turned(NB - 1)
            v.wait_ge(sem("x1_bf2"), 1)
            for b, (c0, n_) in enumerate(BANKS):
                v.wait_ge(sem("ffn_mm"), b + 1)
                step(v.tensor_tensor(bufB[:, c0:c0 + n_], bufA[:, c0:c0 + n_], ps[:, c0:c0 + n_], ALU.add))
                if b in part_ends:
                    settle()
                    ln_part(3, w3(bufB), part_ends.index(b))
            def move_g2(w):
                v.wait_ge(sem("gcn_mm"), w + 1)
                v.tensor_scalar(w3(bufA)[:, w, :], ps[:, product_bank(w):product_bank(w) + D], dinv[:, w:w + 1], None, ALU.mult).then_inc(sem("g2_out"), 1)
            for b, (c0, n_) in enumerate(BANKS):
                w0, w1 = tiles_of(b)[0], tiles_of(b)[-1] + 1
                v.wait_ge(sem("normed"), 3 * NW + w1)
                a = w3(bufB)[:, w0:w1, :]
                step(v.tensor_tensor(a, a, rows[:, 4:5, :].to_broadcast([P, w1 - w0, D]), ALU.mult))
                settle()
                step(v.tensor_tensor(x[:, w0:w1, :], x[:, w0:w1, :], a, ALU.add))
                if b in part_ends:
                    p = part_ends.index(b)
                    settle()
                    ln_part(4, x, p)
                    if p:
                        feed(p - 1, 2 * NB, move_g2)

            feed(len(PARTS) - 1, 2 * NB, move_g2)
            v.tensor_tensor(rows[:, 6, :], rows[:, 6, :], rows[:, 7, :], ALU.add).then_inc(sem("b_both"), 1)
            v.wait_ge(sem("b_both"), 1)
            for w in range(NW):
                c0 = product_bank(NW + w)
                v.wait_ge(sem("lin_mm"), w + 1)
                v.tensor_tensor(w3(bufB)[:, w, :], ps[:, c0:c0 + D], rows[:, 6, :], ALU.add).then_inc(sem("lin_out"), 1)
            v.wait_ge(sem("lin_out"), NW)
            v.wait_ge(sem("g2_out"), NW)
            for w in range(NW):
                step(v.scalar_tensor_tensor(w3(bufB)[:, w, :], w3(bufA)[:, w, :], dinv[:, w:w + 1], w3(bufB)[:, w, :], ALU.mult, ALU.add))
            onehots_for(sem("s2_summed"), sem("s2_onehot"))
            v.wait_ge(sem("s2_summed"), NG)
            settle()
            for b, (c0, n_) in enumerate(BANKS):
                for w in tiles_of(b):
                    step(v.scalar_tensor_tensor(w3(bufC)[:, w, :], ps[:, w * P:(w + 1) * P], dinv[:, w:w + 1], w3(bufB)[:, w, :], ALU.mult, ALU.add))
                settle()
                xs = x[:, tiles_of(b)[0]:tiles_of(b)[-1] + 1, :].rearrange("p w f -> p (w f)")
                step(v.scalar_tensor_tensor(xs, bufC[:, c0:c0 + n_], 0.0, xs, ALU.max, ALU.add))
                if b in part_ends:
                    settle()
                    ln_part(5, x, part_ends.index(b))

            evacuate(hT, sem("hT_mm"), 3 * NB, sem("hT_out"))
            v.wait_ge(sem("normed"), 6 * NW)
            v.tensor_tensor(x[:, :, :], x[:, :, :], rows[:, 8:9, :].to_broadcast([P, NW, D]), ALU.add).then_inc(sem("x_b2"), 1)

            def add_edges(k, j, first):
                g = k * UNROLL + j
                if not (first and j < RING):
                    hold(v, sem("e_summed"), g + 1 - RING, "v")
                make_onehot(onehot[:, j % RING, :], g, sem("e_onehot"))
                v.wait_ge(sem(f"gathered{j % RING}"), all_gathered(3, k, j))
                v.wait_ge(sem(f"ring_in{j % RING}"), BODIES * 16 + slot_uses(k, j) * 16 * U)
                v.tensor_tensor(ring[j % RING], ring[j % RING], gath_lo[j % RING], ALU.add).then_inc(sem("e_added"), 1)
            over_groups(v, add_edges)
            v.wait_ge(sem("e_summed"), NG)
            for b, (c0, w) in enumerate(BANKS):
                v.tensor_tensor(bufA[:, c0:c0 + w], ps[:, c0:c0 + w], hT[:, c0:c0 + w], ALU.add).then_inc(sem("gine_sum"), 1)
            bn_coeffs(bufB, col['L3_gnn_gamma'], col['L3_gnn_beta'], sem("bn3"), sem("gine_z"))
            v.wait_ge(sem("x_b2"), 1)
            for b, (c0, n_) in enumerate(BANKS):
                w0, w1 = tiles_of(b)[0], tiles_of(b)[-1] + 1
                v.wait_ge(sem("out_mm"), b + 1)
                v.tensor_tensor(h[:, w0:w1, :], x[:, w0:w1, :], w3(ps[:, c0:c0 + n_]), ALU.add).then_inc(sem("final"), 1)

        @block.scalar
        def _(a):
            def normalise(i, src3, dst3, func):
                def root(p):
                    ws = windows_in(p)
                    a.wait_ge(sem("ln_var"), i * len(PARTS) + p + 1)
                    a.activation(rstd[:, ws[0]:ws[-1] + 1], rstd[:, ws[0]:ws[-1] + 1], ACT.Sqrt).then_inc(sem("ln_sqrt"), 1)
                root(0)
                for p in range(len(PARTS)):
                    a.wait_ge(sem("ln_shift"), i * len(PARTS) + p + 1)
                    for w in windows_in(p):
                        if w == windows_in(p)[-2:][0] and p + 1 < len(PARTS):
                            root(p + 1)
                        a.activation(dst3[:, w, :], src3[:, w, :], func, bias=shift[:, w:w + 1], scale=rstd[:, w:w + 1]).then_inc(sem("normed"), 1)

            def bank_act(dst, ready, done, func, **kw):
                for b, (c0, n) in enumerate(BANKS):
                    a.wait_ge(ready, b + 1)
                    a.activation(dst[:, c0:c0 + n], ps[:, c0:c0 + n], func, **kw).then_inc(done, 1)

            def bn_apply(src, dst, s, done):
                a.wait_ge(s, NB + 2)
                a.activation(bn[:, 4:5], bn[:, 4:5], ACT.Sqrt).then_inc(sem("bn_sqrt"), 1)
                a.wait_ge(s, NB + 6)
                for b, (c0, n) in enumerate(BANKS):
                    a.activation(dst[:, c0:c0 + n], src[:, c0:c0 + n], ACT.Identity, bias=bn[:, 3:4], scale=bn[:, 2:3]).then_inc(done, 1)

            def stage(half, first_col, used, value):
                if value is not None:
                    hold(a, used, value, "a")
                a.activation(idx_stage[:, half, :], srcS[:, first_col], ACT.Copy).then_inc(sem("idx_staged"), 1)

            def stage_in(k, j, first, used):
                if j == 0:
                    stage(1, bass.DynSlice(k * UNROLL * U + RING * U, RING * U), used, None if first else k * UNROLL)
                elif j == RING:
                    stage(0, bass.DynSlice(k * UNROLL * U + UNROLL * U, RING * U), used, k * UNROLL + RING)

            def stage_all(used):
                stage(0, slice(0, RING * U), None, None)
                over_groups(a, lambda k, j, first: stage_in(k, j, first, used))

            normalise(0, x, h, ACT.Relu)
            a.wait_ge(sem("step_tables"), 4)
            stage(0, slice(0, RING * U), None, None)
            for b in range(LB):
                a.activation(key_wide[:, b * BANK:(b + 1) * BANK].rearrange("p (t r e) -> p t r e", t=BT, e=HEADS),
                             key[:, :].rearrange("p (r t) -> p t r", r=RANGES)[:, BT * b:BT * (b + 1)].unsqueeze(3).to_broadcast([P, BT, RANGES, HEADS]),
                             ACT.Copy).then_inc(sem("key_wide"), 1)

            def stage_and_turn(k, j, first):
                stage_in(k, j, first, sem("s0_summed"))
                if first and j < LB:
                    a.wait_ge(sem("key_turned"), j + 1)
                    a.activation(key_line[:, j * BANK:(j + 1) * BANK], ps[:, B7:B7 + BANK], ACT.Copy).then_inc(sem("key_line"), 1)
            over_groups(a, stage_and_turn)
            bank_act(bufB, sem("gin_mm1"), sem("gin_z1"), ACT.Relu, bias=col['L0_gnn_b1'])
            bank_act(bufC, sem("gin_mm2"), sem("gin_z2"), ACT.Identity, bias=col['L0_gnn_b2'])
            bn_apply(bufC, bufB, sem("bn0"), sem("gin_bn"))

            normalise(1, x, h, ACT.Relu)
            for w in range(NW):
                a.wait_ge(sem("qkv_mm"), NW + w + 1)
                a.activation(*qkv_move(NW + w), ACT.Copy).then_inc(sem("k_out"), 1)

            def turn(g, sl):
                a.wait_ge(sem("a_turned"), g + 1)
                a.activation(onehotT[:, sl, :], ps[:, sl * BANK:(sl + 1) * BANK], ACT.Copy).then_inc(sem("a_onehotT"), 1)

            stage(0, slice(0, RING * U), None, None)
            turn(0, 0)

            def attend(k, j, first):
                stage_in(k, j, first, sem("a_prod"))
                turn(k * UNROLL + j + 1, (j + 1) % 2)
            over_groups(a, attend)
            a.wait_ge(sem("deg_ready"), 1)
            a.activation(dinv[:, :], dinv[:, :], ACT.Sqrt).then_inc(sem("deg_sqrt"), 1)

            for b in range(LB):
                c = slice(b * BANK, (b + 1) * BANK)
                a.wait_ge(sem("l_less"), b + 1)
                a.activation(line_a[:, c], line_a[:, c], ACT.Exp).then_inc(sem("l_exp"), 1)

            def back_by_slot(dst, b, at, done):
                a.activation(dst.rearrange("p (r t e) -> p t r e", r=RANGES, e=HEADS)[:, BT * b:BT * (b + 1)],
                             ps[:, at:at + BANK].rearrange("p (t r e) -> p t r e", t=BT, e=HEADS), ACT.Copy).then_inc(done, 1)

            for b in range(LB):
                a.wait_ge(sem("m_turned"), b + 1)
                back_by_slot(by_slot, b, b * BANK, sem("m_by_slot"))
            a.wait_ge(sem("l_scan"), 5)
            for b in range(LB):
                a.wait_ge(sem("p_turned"), b + 1)
                back_by_slot(score[:, :], b, b * BANK, sem("p_by_slot"))
            hold(a, sem("m_stored"), 16, "a")
            def turned_denominators(b):
                if b < LB:
                    a.wait_ge(sem("den_turned"), b + 1)
                    back_by_slot(by_slot, b, B7, sem("den_by_slot"))

            def count_to_one(k, j, first):
                if first:
                    turned_denominators(j)
                    return
                if j % 2 == 0:
                    return
                g = k * UNROLL + j
                hold(a, sem("c_summed"), g + 1 - RING, "a")
                for u in range(U):
                    i = a.activation(onehot[:, j % RING, u * P:(u + 1) * P], iota_node[:, :], ACT.Abs, bias=dloc[:, bass.DynSlice(g * U + u, 1)], scale=-1.0)
                i.then_inc(sem("c_distance"), 1)
                hold(a, sem("c_distance"), odd_groups(k, j), "a")
                a.activation(onehot[:, j % RING, :], onehot[:, j % RING, :], ACT.Relu, bias=ones[:, 0:1], scale=-1.0).then_inc(sem("c_onehot_odd"), 1)

            def factors():
                a.wait_ge(sem("f_args"), 1)
                a.activation(f_edge[:, :], f_edge[:, :], ACT.Exp).then_inc(sem("f_exp"), 1)
                a.activation(f_loop[:, :], f_loop[:, :], ACT.Exp).then_inc(sem("f_exp"), 1)
            over_groups(a, count_to_one, factors)

            def bank_out(dst, ready, done):
                for b, (c0, n) in enumerate(BANKS):
                    a.wait_ge(ready, b + 1)
                    a.activation(dst[:, c0:c0 + n], ps[:, c0:c0 + n], ACT.Copy).then_inc(done, 1)
            bank_out(bufB, sem("oT_mm"), sem("oT_out"))
            normalise(2, w3(bufA), w3(bufA), ACT.Identity)
            for b, (c0, n) in enumerate(BANKS):
                for c in range(HC):
                    i = b * HC + c
                    dst = bufC[:, c0:c0 + n] if c == HC - 1 else qkv[:, c * NPAD + c0:c * NPAD + c0 + n]
                    a.wait_ge(sem("ffn1_mm"), i + 1)
                    a.activation(dst, ps[:, product_bank(i):product_bank(i) + n], ACT.Gelu, bias=bf1[c]).then_inc(sem("ffn1_out"), 1)
            normalise(3, w3(bufB), w3(bufB), ACT.Identity)

            normalise(4, x, h, ACT.Relu)

            stage_all(sem("s2_summed"))

            normalise(5, x, h, ACT.Relu)
            stage(0, slice(0, RING * U), None, None)

            def relu_edges(k, j, first):
                stage_in(k, j, first, sem("e_added"))
                a.wait_ge(sem("e_added"), k * UNROLL + j + 1)
                a.activation(ring[j % RING], ring[j % RING], ACT.Relu).then_inc(sem("e_relu"), 1)
            over_groups(a, relu_edges)
            bank_act(bufB, sem("gine_mm"), sem("gine_z"), ACT.Relu, bias=col['L3_gnn_b1'])
            bn_apply(bufB, bufC, sem("bn3"), sem("gine_bn"))

        @block.tensor
        def _(pe):
            LOADED = 5
            regs = [pe.alloc_register(f"columns{i}") for i in range(LOADED * U)]

            def columns(k, j):
                if j % LOADED == 0:
                    pe.load(regs, step_columns[0:1, bass.DynSlice(k * UNROLL + j, LOADED), :].rearrange("a g u -> a (g u)"))
                return [pe.snap(r, min_val=0, max_val=NPAD - P) for r in regs[j % LOADED * U:(j % LOADED + 1) * U]]

            def transpose(dst, src, **kw):
                return pe.matmul(dst, src, ident[0:src.shape[0], 0:src.shape[0]], start=True, stop=True, is_transpose=True, **kw)

            def turn_rows(src3, ready, value, done):
                for b, (c0, n) in enumerate(BANKS):
                    pe.wait_ge(ready, value(b))
                    for w in tiles_of(b):
                        i = transpose(ps[:, w * P:(w + 1) * P], src3[:, w, :])
                    i.then_inc(done, 1)

            def turn_and_multiply(src3, ready, turned, out_, base, product):
                def turn_bank_of(b):
                    ready(b)
                    if b >= 2:
                        pe.wait_ge(out_, base + b - 1)
                    for w in tiles_of(b):
                        at = b % 2 * BANK + w % 4 * P
                        i = transpose(ps[:, at:at + P], src3[:, w, :])
                    i.then_inc(turned, 1)
                turn_bank_of(0)
                for b in range(NB):
                    if b + 1 < NB:
                        turn_bank_of(b + 1)
                    pe.wait_ge(out_, base + b + 1)
                    product(b)

            def all_normed(first):
                return lambda b: pe.wait_ge(sem("normed"), first + tiles_of(b)[-1] + 1)

            def each_window(product):
                def of_bank(b):
                    for w in tiles_of(b):
                        product(w)
                return of_bank

            def clear_sums():
                for b in range(NB):
                    pe.matmul(ps[:, b * BANK:(b + 1) * BANK], zeros[:, 0:P], zeros[:, :], start=True, stop=False, skip_group_check=True)

            def bank_mm(lhsT, rhs, ready, done):
                for b, (c0, n) in enumerate(BANKS):
                    pe.wait_ge(ready, b + 1)
                    pe.matmul(ps[:, c0:c0 + n], lhsT, rhs[:, c0:c0 + n], start=True, stop=True).then_inc(done, 1)

            pe.wait_ge(sem("consts"), 10)
            pe.wait_ge(sem("falls_ready"), 1)
            pe.matmul(ps[0:1, 0:1], ones[:, 0:1], falls_sum, start=True, stop=True).then_inc(sem("falls_added"), 1)
            pe.wait_ge(sem("before_ready"), 1)
            for c, k in enumerate(CHUNKS[:NCH]):
                i = pe.matmul(ps[0:NW - 1, 0:1], before[0:k, c, :], ones[0:k, 0:1], start=c == 0, stop=c == NCH - 1)
            i.then_inc(sem("counts_ready"), 1)
            pe.wait_ge(sem("reached_ready"), 1)
            pe.matmul(ps[:, 2 * BANK:2 * BANK + NS], ones[0:NW - 1, :], fromW[0:NW - 1, :], start=True, stop=True).then_inc(sem("window_ready"), 1)
            pe.wait_ge(sem("select_ready"), 1)
            for i_, tab in enumerate((dstT, srcT)):
                for c, k in enumerate(CHUNKS):
                    i = pe.matmul(ps[:, (3 + i_) * BANK:(3 + i_) * BANK + NS], tab[0:k, c, :], sel[0:k, c, :], start=c == 0, stop=c == NC5 - 1)
                i.then_inc(sem("selected"), 1)
            pe.matmul(ps[:, 5 * BANK:5 * BANK + NS], last_keys[0:1, :], sel[0:1, NCH, :], start=True, stop=True).then_inc(sem("selected"), 1)
            pe.wait_ge(sem("weights_in"), 16 * (12 + len(ROWS) + len(COLS) + HC))
            for i_ in range(3):
                i = pe.matmul(ps[:, i_ * BANK:i_ * BANK + 3 * D], ones[0:1, :], rows_in[0:1, i_ * 3 * D:(i_ + 1) * 3 * D], start=True, stop=True)
            i.then_inc(sem("rows_spread"), 1)

            def sum_groups(phase, onehot_done, summed, by_feature, msg, ready, counts=False, inserted=None):
                def body(k, j, first):
                    g = k * UNROLL + j
                    onehot_done(k, j, first)
                    ready(k, j)
                    at = columns(k, j)
                    for u in range(U):
                        o = onehot[:, j % RING, u * P:(u + 1) * P]
                        m = msg(j, u)
                        i = pe.matmul(acc[:, bass.DynSlice(at[u], P)], m if by_feature else o, o if by_feature else m,
                                      start=False, stop=False, skip_group_check=True)
                        if counts:
                            i = pe.matmul(ps[:, bass.DynSlice(at[u] // P + CNT, 1)], o, ones[:, 0:1], start=False, stop=False, skip_group_check=True)
                    i.then_inc(summed, 1)
                    if first and inserted:
                        inserted(j)
                over_groups(pe, body)

            def turn_bank(src, b, at, done):
                for t_ in range(BT):
                    c = b * BANK + t_ * P
                    i = pe.matmul(ps[:, at + t_ * P:at + (t_ + 1) * P], src[:, c:c + P], ident[:, :], start=True, stop=True)
                i.then_inc(done, 1)

            def turn_keys(j):
                if j < LB:
                    pe.wait_ge(sem("key_wide"), j + 1)
                    if j:
                        pe.wait_ge(sem("key_line"), j)
                    turn_bank(key_wide, j, B7, sem("key_turned"))

            def turn_denominators(j):
                if j < LB:
                    if j == 0:
                        pe.wait_ge(sem("l_scan"), 6)
                    else:
                        pe.wait_ge(sem("den_by_slot"), j)
                    turn_bank(line_b, j, B7, sem("den_turned"))

            def by_vector(name):
                return lambda k, j, first: pe.wait_ge(sem(name), k * UNROLL + j + 1)

            def gathered(phase):
                return lambda k, j: pe.wait_ge(sem(f"gathered{j % RING}"), all_gathered(phase, k, j))

            pe.wait_ge(sem("rows_ready"), 3)
            pe.wait_ge(sem("step_tables"), 4)
            turn_rows(h, sem("normed"), lambda b: tiles_of(b)[-1] + 1, sem("hT_mm"))
            pe.wait_ge(sem("hT_out"), NB)
            clear_sums()
            sum_groups(0, by_vector("s0_onehot"), sem("s0_summed"), True, lambda j, u: gath[:, j % RING * U + u, 0:D], gathered(0),
                       counts=True, inserted=turn_keys)
            bank_mm(Wt[:, W_GIN1, :], bufA, sem("gin_sum"), sem("gin_mm1"))
            bank_mm(Wt[:, W_GIN2, :], bufB, sem("gin_z1"), sem("gin_mm2"))
            turn_rows(w3(bufA), sem("gin_y"), lambda b: b + 1, sem("gin_yT"))

            def project(i_):
                w = i_ % NW
                if 5 <= i_ < NW + 5:
                    pe.wait_ge(sem("qv_out"), i_ - 4)
                elif i_ >= NW + 5:
                    pe.wait_ge(sem("k_out"), i_ - NW - 4)
                c0 = product_bank(i_)
                for n_, s_ in enumerate((W_Q, W_V) if i_ < NW else (W_K,)):
                    i = pe.matmul(ps[:, c0 + n_ * D:c0 + (n_ + 1) * D], hT[:, w * P:(w + 1) * P], Wt[:, s_, :], start=True, stop=True)
                i.then_inc(sem("qkv_mm"), 1)
            pe.wait_ge(sem("wq_scaled"), 1)
            turn_and_multiply(h, all_normed(NW), sem("hT_mm"), sem("hT_out"), NB, each_window(project))
            for i_ in range(NW, 2 * NW):
                project(i_)

            def turn(g, sl, j):
                pe.wait_ge(sem("a_onehot"), g + 1)
                for u in range(U):
                    i = transpose(ps[:, sl * BANK + u * P:sl * BANK + (u + 1) * P], onehot[:, j, u * P:(u + 1) * P])
                i.then_inc(sem("a_turned"), 1)

            pe.wait_ge(sem("ends_known"), 1)
            for i_ in range(3):
                pe.matmul(ps[0:1, B7 + i_ * P:B7 + (i_ + 1) * P], line_ends[:, i_:i_ + 1], ident[:, :], start=True, stop=True)
            pe.wait_ge(sem("upto_ready"), 1)
            pe.matmul(ps[:, B7 + 384:B7 + 384 + NW], upto, count[:, :], start=True, stop=True)
            pe.matmul(ps[:, B7 + 416:B7 + 416 + NW], ones[:, :], count[:, :], start=True, stop=True).then_inc(sem("counted"), 1)
            pe.wait_ge(sem("k_out"), NW)
            turn(0, 0, 0)

            def attend(k, j, first):
                g = k * UNROLL + j
                sl = j % 2
                at = columns(k, j)
                pe.wait_ge(sem("a_onehotT"), g + 1)
                if not (first and j < 2):
                    pe.wait_ge(sem("a_prod"), g - 1)
                k_at = (2 + sl) * BANK
                for u in range(U):
                    i = pe.matmul(ps[:, k_at + u * D:k_at + (u + 1) * D], onehotT[:, sl, u * P:(u + 1) * P],
                                  qkv[:, bass.DynSlice(at[u] * 3 + 2 * D, D)], start=True, stop=True)
                i.then_inc(sem("a_k"), 1)
                turn(g + 1, (j + 1) % 2, (j + 1) % RING)
            over_groups(pe, attend)

            pe.wait_ge(sem("a_onehotT"), NG + 1)
            for b in range(LB):
                pe.wait_ge(sem("l_copied"), b + 1)
                turn_bank(line_a, b, b * BANK, sem("l_turned"))

            def carry_over(nth, scan, column):
                pe.wait_ge(sem("l_scan"), scan)
                pe.matmul(ps[0:1, B7:B7 + P], column, ident[:, :], start=True, stop=True).then_inc(sem("row_mm"), 1)
                pe.wait_ge(sem("row_v"), 3 * (nth + 1))
                pe.matmul(ps[:, B7 + P:B7 + P + 1], row_carry[:, 0:P], ones[0:1, 0:1], start=True, stop=True).then_inc(sem("carry_mm"), 1)
            carry_over(0, 1, line_a[:, LINE - 1:LINE])
            carry_over(1, 3, line_b[:, 0:1])
            for b in range(LB):
                pe.wait_ge(sem("l_less"), b + 1)
                turn_bank(line_b, b, b * BANK, sem("m_turned"))
            carry_over(2, 5, score[:, LINE - 1:LINE])
            for b in range(LB):
                pe.wait_ge(sem("l_exp"), b + 1)
                pe.wait_ge(sem("m_by_slot"), b + 1)
                turn_bank(line_a, b, b * BANK, sem("p_turned"))

            pe.wait_ge(sem("p_by_slot"), LB)
            clear_sums()
            def by_both(k, j, first):
                if first:
                    pe.wait_ge(sem("c_onehot"), j + 1)
                elif j % 2 == 0:
                    pe.wait_ge(sem("c_onehot"), UNROLL + odd_groups(k, j))
                else:
                    pe.wait_ge(sem("c_onehot_odd"), odd_groups(k, j))
            sum_groups(1, by_both, sem("c_summed"), False, lambda j, u: values[j][:, u, :],
                       lambda k, j: pe.wait_ge(sem("c_weighted"), k * UNROLL + j + 1), inserted=turn_denominators)

            turn_rows(w3(bufA), sem("o_all"), lambda b: b + 1, sem("oT_mm"))

            def window_mm(src, slot, ready, done):
                for b in range(NB):
                    pe.wait_ge(ready, b + 1)
                    for w in tiles_of(b):
                        i = pe.matmul(ps[:, w * P:(w + 1) * P], src[:, w * P:(w + 1) * P], Wt[:, slot, :], start=True, stop=True)
                    i.then_inc(done, 1)
            window_mm(bufB, W_O, sem("oT_out"), sem("attn_mm"))
            def widen(b):
                c0, n = BANKS[b]
                for c in range(HC):
                    i = b * HC + c
                    if i >= 5:
                        pe.wait_ge(sem("ffn1_out"), i - 4)
                    pe.matmul(ps[:, product_bank(i):product_bank(i) + n], Wt[:, W_F1 + c, :], bufB[:, c0:c0 + n], start=True, stop=True).then_inc(sem("ffn1_mm"), 1)
            turn_and_multiply(w3(bufA), lambda b: pe.wait_ge(sem("x1"), b + 1), sem("x1T_mm"), sem("x1T_out"), 0, widen)
            pe.wait_ge(sem("ffn1_out"), NB * HC)
            for b in range(NB):
                for w in tiles_of(b):
                    for c in range(HC):
                        src = bufC[:, w * P:(w + 1) * P] if c == HC - 1 else qkv[:, c * NPAD + w * P:c * NPAD + (w + 1) * P]
                        i = pe.matmul(ps[:, w * P:(w + 1) * P], src, Wt[:, W_F2 + c, :], start=c == 0, stop=c == HC - 1)
                i.then_inc(sem("ffn_mm"), 1)

            def convolve(i_):
                w = i_ % NW
                if 5 <= i_ < NW + 5:
                    pe.wait_ge(sem("g2_out"), i_ - 4)
                elif i_ >= NW + 5:
                    pe.wait_ge(sem("lin_out"), i_ - NW - 4)
                pe.matmul(ps[:, product_bank(i_):product_bank(i_) + D], hT[:, w * P:(w + 1) * P], Wt[:, W_GCN if i_ < NW else W_LIN, :],
                          start=True, stop=True).then_inc(sem("gcn_mm") if i_ < NW else sem("lin_mm"), 1)
            turn_and_multiply(h, all_normed(4 * NW), sem("hT_mm"), sem("hT_out"), 2 * NB, each_window(convolve))
            for i_ in range(NW, 2 * NW):
                convolve(i_)
            pe.wait_ge(sem("g2_out"), NW)
            pe.wait_ge(sem("lin_out"), NW)
            clear_sums()
            sum_groups(2, by_vector("s2_onehot"), sem("s2_summed"), False, lambda j, u: gath[:, j % RING * U + u, 0:D], gathered(2))

            turn_rows(h, sem("normed"), lambda b: 5 * NW + tiles_of(b)[-1] + 1, sem("hT_mm"))
            pe.wait_ge(sem("hT_out"), 4 * NB)
            clear_sums()
            sum_groups(3, by_vector("e_onehot"), sem("e_summed"), True, lambda j, u: gath[:, j % RING * U + u, D:2 * D],
                       lambda k, j: pe.wait_ge(sem("e_relu"), k * UNROLL + j + 1))
            bank_mm(Wt[:, W_E1, :], bufA, sem("gine_sum"), sem("gine_mm"))
            window_mm(bufC, W_E2, sem("gine_bn"), sem("out_mm"))


_INS = ['x', 'src', 'dst', 'edge_attr_128', 'L0_gnn_W1', 'L0_gnn_b1', 'L0_gnn_W2', 'L0_gnn_b2', 'L0_gnn_gamma',
        'L0_gnn_beta', 'L1_gnn_Wq', 'L1_gnn_Wk', 'L1_gnn_Wv', 'L1_gnn_Wo', 'L1_gnn_bo', 'L1_gnn_Wf1', 'L1_gnn_bf1',
        'L1_gnn_Wf2', 'L1_gnn_bf2', 'L1_gnn_g1', 'L1_gnn_b1', 'L1_gnn_g2', 'L1_gnn_b2', 'L2_gnn_W_gcn',
        'L2_gnn_b_gcn', 'L2_gnn_W_lin', 'L2_gnn_b_lin', 'L3_gnn_W1', 'L3_gnn_b1', 'L3_gnn_gamma', 'L3_gnn_beta',
        'L3_gnn_W2', 'L3_gnn_b2']


def kernel(**inputs):
    import numpy as _np
    import concourse.bacc as _bacc
    from concourse.bass_utils import run_bass_kernel_spmd as _run

    nc = _bacc.Bacc("TRN2", target_bir_lowering=False, num_devices=1)
    arrays, t = {}, {}
    for name in _INS:
        a = _np.ascontiguousarray(inputs[name])
        arrays[f"in_{name}"] = a
        t[name] = nc.dram_tensor(f"in_{name}", a.shape, mybir.dt.from_np(a.dtype), kind="ExternalInput").ap()
    out = nc.dram_tensor("out", (N_NODES, D), F32, kind="ExternalOutput").ap()
    gnn_kernel(nc, t, out)
    r = _run(nc, [arrays], core_ids=[0])
    return r.results[0]["out"]
```
